# Optimizing a Trainium2 kernel written in Bass

```python
import numpy as np
import jax
import jax.numpy as jnp

def _softmax(x, axis=-1):
    return jax.nn.softmax(x, axis=axis)

def _gelu(x):
    return jax.nn.gelu(x, approximate=True)

def _silu(x):
    return jax.nn.silu(x)

def _sigmoid(x):
    return jax.nn.sigmoid(x)

def _layernorm(x, axis=-1, eps=1e-05):
    m = jnp.mean(x, axis=axis, keepdims=True)
    v = jnp.var(x, axis=axis, keepdims=True)
    return (x - m) / jnp.sqrt(v + eps)

def _scatter_add(tgt, idx, src, axis=0):
    return tgt.at[idx].add(src)

def _segment_sum(src, seg, n):
    return jax.ops.segment_sum(src, seg, n)
kernel_name = 'mk_sandwich_d1_jaxref_r8_36f747'

def setup_inputs(seed: int=0):
    np.random.seed(seed)
    _w = jnp.asarray

    def _L0_attn_setup():
        import math
        import jax, jax.numpy as jnp
        import numpy as np

        def _expmap0(u):
            u0 = u[..., :1]
            us = u[..., 1:]
            mink = -u0 * u0 + jnp.sum(us * us, axis=-1, keepdims=True)
            nomin = jnp.sqrt(jnp.maximum(mink, 1e-08))
            r = jnp.sinh(nomin) * u / nomin
            space = r[..., 1:]
            time = jnp.sqrt(1.0 + jnp.sum(space * space, axis=-1, keepdims=True))
            return jnp.concatenate([time, space], axis=-1)
        key = jax.random.key(seed)
        B, T, E, H = (2, 128, 128, 16)
        ks = jax.random.split(key, 8)
        s = 0.02
        return {'x': jax.random.normal(ks[0], (B, T, E), jnp.float32), 'Wqkv': jax.random.normal(ks[1], (3 * E, E), jnp.float32) * s, 'bqkv': jnp.zeros((3 * E,), jnp.float32), 'Wout': jax.random.normal(ks[2], (E, E), jnp.float32) * s, 'bout': jnp.zeros((E,), jnp.float32), 'Wimp': jax.random.normal(ks[3], (1, E), jnp.float32) * s, 'bimp': jnp.zeros((1,), jnp.float32), 'Walpha': jax.random.normal(ks[4], (H, E), jnp.float32) * s, 'balpha': jnp.zeros((H,), jnp.float32), 'spike_threshold': jnp.asarray(0.5, jnp.float32), 'log_k': jnp.full((H,), 0.54, jnp.float32), 'qk_scale': jnp.asarray(0.1, jnp.float32)}
    _L0_attn_in = _L0_attn_setup()

    def _L0_ffn_setup():
        import jax, jax.numpy as jnp
        import numpy as np
        LN_EPS = 1e-12
        key = jax.random.key(seed)
        ks = jax.random.split(key, 8)
        B, S, H, I, E = (4, 256, 128, 512, 8)
        sH = 1.0 / np.sqrt(H)
        sI = 1.0 / np.sqrt(I)
        return {'hidden_states': jax.random.normal(ks[0], (B, S, H), dtype=jnp.float32), 'Wr': jax.random.uniform(ks[1], (E, H), jnp.float32, -sH, sH), 'W1': jax.random.uniform(ks[2], (E, H, I), jnp.float32, -sH, sH), 'b1': jax.random.uniform(ks[3], (E, I), jnp.float32, -sH, sH), 'Wo': jax.random.uniform(ks[4], (I, H), jnp.float32, -sI, sI), 'bo': jax.random.uniform(ks[5], (H,), jnp.float32, -sI, sI), 'gamma': jnp.ones((H,), jnp.float32), 'beta': jnp.zeros((H,), jnp.float32)}
    _L0_ffn_in = _L0_ffn_setup()
    _d = {'L0_attn_x': _L0_attn_in['x'], 'L0_attn_Wqkv': _L0_attn_in['Wqkv'], 'L0_attn_bqkv': _L0_attn_in['bqkv'], 'L0_attn_Wout': _L0_attn_in['Wout'], 'L0_attn_bout': _L0_attn_in['bout'], 'L0_attn_Wimp': _L0_attn_in['Wimp'], 'L0_attn_bimp': _L0_attn_in['bimp'], 'L0_attn_Walpha': _L0_attn_in['Walpha'], 'L0_attn_balpha': _L0_attn_in['balpha'], 'L0_attn_spike_threshold': _L0_attn_in['spike_threshold'], 'L0_attn_log_k': _L0_attn_in['log_k'], 'L0_attn_qk_scale': _L0_attn_in['qk_scale'], 'L0_ffn_Wr': _L0_ffn_in['Wr'], 'L0_ffn_W1': _L0_ffn_in['W1'], 'L0_ffn_b1': _L0_ffn_in['b1'], 'L0_ffn_Wo': _L0_ffn_in['Wo'], 'L0_ffn_bo': _L0_ffn_in['bo'], 'L0_ffn_gamma': _L0_ffn_in['gamma'], 'L0_ffn_beta': _L0_ffn_in['beta']}
    _x0 = _d['L0_attn_x']
    _d['L0_attn_x'] = jax.random.normal(jax.random.fold_in(jax.random.key(seed), 1), (16, 256, 128), dtype=_x0.dtype)
    del _x0
    return _d

def reference(L0_attn_x, L0_attn_Wqkv, L0_attn_bqkv, L0_attn_Wout, L0_attn_bout, L0_attn_Wimp, L0_attn_bimp, L0_attn_Walpha, L0_attn_balpha, L0_attn_spike_threshold, L0_attn_log_k, L0_attn_qk_scale, L0_ffn_Wr, L0_ffn_W1, L0_ffn_b1, L0_ffn_Wo, L0_ffn_bo, L0_ffn_gamma, L0_ffn_beta):

    def _L0_attn_ref(x, Wqkv, bqkv, Wout, bout, Wimp, bimp, Walpha, balpha, spike_threshold, log_k, qk_scale):
        import math
        import jax, jax.numpy as jnp
        import numpy as np

        def _expmap0(u):
            u0 = u[..., :1]
            us = u[..., 1:]
            mink = -u0 * u0 + jnp.sum(us * us, axis=-1, keepdims=True)
            nomin = jnp.sqrt(jnp.maximum(mink, 1e-08))
            r = jnp.sinh(nomin) * u / nomin
            space = r[..., 1:]
            time = jnp.sqrt(1.0 + jnp.sum(space * space, axis=-1, keepdims=True))
            return jnp.concatenate([time, space], axis=-1)
        B, T, C = x.shape
        H = log_k.shape[0]
        D = C // H
        importance = jax.nn.sigmoid(x @ Wimp.T + bimp)
        spikes = (importance > spike_threshold).astype(x.dtype)
        spike_mask = spikes.reshape(B, 1, T, 1)
        alpha = jax.nn.sigmoid(x @ Walpha.T + balpha)
        alpha = jnp.transpose(alpha, (0, 2, 1))[..., None]
        qkv = (x @ Wqkv.T + bqkv).reshape(B, T, 3, H, D)
        q = jnp.transpose(qkv[:, :, 0], (0, 2, 1, 3))
        k = jnp.transpose(qkv[:, :, 1], (0, 2, 1, 3))
        v = jnp.transpose(qkv[:, :, 2], (0, 2, 1, 3))
        scores_euclid = jnp.einsum('bhtd,bhsd->bhts', q, k) / math.sqrt(D)
        safe_scale = jax.nn.sigmoid(qk_scale) * 1.5
        qn = q / jnp.maximum(jnp.linalg.norm(q, axis=-1, keepdims=True), 1e-12) * safe_scale
        kn = k / jnp.maximum(jnp.linalg.norm(k, axis=-1, keepdims=True), 1e-12) * safe_scale
        q_hyp = _expmap0(qn)
        k_hyp = _expmap0(kn)
        inner = -jnp.einsum('bhti,bhsi->bhts', q_hyp[..., :1], k_hyp[..., :1]) + jnp.einsum('bhtd,bhsd->bhts', q_hyp[..., 1:], k_hyp[..., 1:])
        curv_k = (jax.nn.softplus(log_k) + 1e-06).reshape(1, H, 1, 1)
        mdot = jnp.maximum(-inner, 1.0 + 1e-06)
        dist = jnp.arccosh(mdot)
        scores_hyper = -(dist * dist) / curv_k
        scores = (1.0 - alpha) * scores_euclid + alpha * scores_hyper
        causal = jnp.tril(jnp.ones((T, T), bool))
        scores = jnp.where(causal[None, None], scores, -jnp.inf)
        attn = jax.nn.softmax(scores, axis=-1) * spike_mask
        y = jnp.einsum('bhts,bhsd->bhtd', attn, v)
        y = jnp.transpose(y, (0, 2, 1, 3)).reshape(B, T, C)
        return y @ Wout.T + bout

    def _L0_ffn_ref(hidden_states, Wr, W1, b1, Wo, bo, gamma, beta):
        import jax, jax.numpy as jnp
        import numpy as np
        LN_EPS = 1e-12
        B, S, H = hidden_states.shape
        E = Wr.shape[0]
        x = hidden_states.reshape(-1, H)
        router_logits = x @ Wr.T
        expert_idx = jnp.argmax(jax.nn.softmax(router_logits, axis=-1), axis=-1)
        inter = jnp.zeros((x.shape[0], W1.shape[2]), dtype=x.dtype)
        for e in range(E):
            mask = (expert_idx == e)[:, None].astype(x.dtype)
            inter = inter + mask * jax.nn.gelu(x @ W1[e] + b1[e], approximate=False)
        y = inter @ Wo + bo + x
        mu = jnp.mean(y, axis=-1, keepdims=True)
        var = jnp.mean(jnp.square(y - mu), axis=-1, keepdims=True)
        out = (y - mu) * jax.lax.rsqrt(var + LN_EPS) * gamma + beta
        return out.reshape(B, S, H)
    x = L0_attn_x
    x = x + _layernorm(_L0_attn_ref(_layernorm(x, axis=-1), L0_attn_Wqkv, L0_attn_bqkv, L0_attn_Wout, L0_attn_bout, L0_attn_Wimp, L0_attn_bimp, L0_attn_Walpha, L0_attn_balpha, L0_attn_spike_threshold, L0_attn_log_k, L0_attn_qk_scale), axis=-1)
    x = x + _layernorm(_L0_ffn_ref(_layernorm(x, axis=-1), L0_ffn_Wr, L0_ffn_W1, L0_ffn_b1, L0_ffn_Wo, L0_ffn_bo, L0_ffn_gamma, L0_ffn_beta), axis=-1)
    return x

_drawn_inputs = setup_inputs


def setup_inputs(seed=0):
    import zlib

    import numpy as np

    out = dict(_drawn_inputs(seed))
    spreads = {'L0_attn_bqkv': (0.0, 0.1),
     'L0_attn_bout': (0.0, 0.1),
     'L0_attn_balpha': (0.0, 0.8),
     'L0_attn_log_k': (0.5400000214576721, 0.6),
     'L0_ffn_gamma': (1.0, 0.2),
     'L0_ffn_beta': (0.0, 0.1)}
    factors = {'L0_attn_Walpha': 8.0, 'L0_ffn_b1': 7.806, 'L0_ffn_bo': 4.909}
    for name, (base, spread) in spreads.items():
        noise = np.random.default_rng([zlib.crc32(name.encode()), seed]).standard_normal(out[name].shape)
        drawn = base * np.exp(spread * noise) if base else spread * noise
        out[name] = jnp.asarray(drawn.astype(out[name].dtype))
    for name, factor in factors.items():
        out[name] = (out[name] * factor).astype(out[name].dtype)
    return out
```

```python
from contextlib import ExitStack
from math import factorial

import concourse.bass as bass
from concourse import mybir

ALU = mybir.AluOpType
ACT = mybir.ActivationFunctionType
F32 = mybir.dt.float32
F16 = mybir.dt.float16
BF16 = mybir.dt.bfloat16
AX = mybir.AxisListType.X
ds = bass.ds

P = 128
LN_EPS = 1e-5
FFN_EPS = 1e-12
M_MIN = 1.00000095367431640625
HS = 16.0
MASKED = -1e30


def sandwich(nc, x, w_all, b_all, wout, bout, thr, log_k, qk_scale, wr, w1, b1, wo, bo, gamma, beta, out):
    N, C = x.shape
    H = log_k.shape[1]
    D = C // H
    NE, _, FI = w1.shape
    NP_ = w_all.shape[1]
    NT = N // P
    TB = 2
    NB = NT // TB
    FC = FI // P
    QI, KI, VI, II, AI = 0, C, 2 * C, 3 * C, 3 * C + 1
    G4 = 4
    NG = NT // G4
    CH = 1024
    CHUNKS = [(0, (0, 1), (0, 1, 2, 3)), (0, (2, 3), (0, 1, 2, 3)), (1, (0, 1), (0, 1)),
              (1, (2, 3), (0, 1)), (1, (0, 1), (2, 3)), (1, (2, 3), (2, 3))]
    NC_ = len(CHUNKS)
    HALVES = 2 * NC_

    def heads_of(c):
        tt, rows, quads = CHUNKS[c]
        width = P * (tt + 1)
        got = []
        for bank, r in enumerate(rows):
            for n, g in enumerate(quads):
                got.append((4 * g + r, bank * 512 + n * width, width))
        return got

    ctx = ExitStack()
    with ctx:
        def sb(name, shape, dt=F32):
            return ctx.enter_context(nc.sbuf_tensor(name, shape, dt))

        def ps(name, shape, dt=F32):
            return ctx.enter_context(nc.psum_tensor(name, shape, dt))

        def sem(name):
            return ctx.enter_context(nc.semaphore(name))

        xin = sb("xin", [P, NT, C])
        yatt = xin
        big = sb("big", [P, NT * NP_])
        proj = big[:, :].rearrange("p (t n) -> p t n", n=NP_)
        oma = sb("oma", [P, NT, H])
        acf = sb("acf", [P, NT, H])
        spk = sb("spk", [P, NT])
        gfac = sb("gfac", [P, NT, 2, H])
        tmt = sb("tmt", [P, NT, 2, H])
        za = sb("za", [P, 2, NC_, CH])
        zb = sb("zb", [P, NC_, CH])
        pt = sb("pt", [P, 3, 512])
        stk = sb("stk", [P, TB, 4, H, 4, D], F16)
        vec = sb("vec", [P, TB, 4, H, D])
        opd = sb("opd", [P, 2, 4, 4, TB * P], F16)
        vone = sb("vone", [P, 2, TB, H, D + 1])
        acb = sb("acb", [P, 2, TB * H])
        mxs = sb("mxs", [P, 2, TB * H])
        rin = sb("rin", [P, TB * H])
        wall = sb("wall", [P, NP_])
        ball = sb("ball", [P, NP_])
        ident = sb("ident", [P, P])
        ident16 = sb("ident16", [P, P], F16)
        identb = sb("identb", [P, P], BF16)
        maskb = sb("maskb", [P, P], BF16)
        cst = sb("cst", [P, 2])
        lk = sb("lk", [P, H])
        curv = sb("curv", [P, 4, H])
        sc1 = sb("sc1", [P, 4])
        st6 = sb("st6", [P, NT, 6])
        mu = sb("mu", [P, NT])
        var = sb("var", [P, NT])
        tmp = sb("tmp", [P, 2, NT])
        nmr = sb("nmr", [P, NT])
        oh = sb("oh", [P, 2, G4, NE])
        ohb = sb("ohb", [P, 2, G4, NE], BF16)

        zaf = za[:, :, :, :].rearrange("p a c n -> p (a c n)")
        zbf = zb[:, :, :].rearrange("p c n -> p (c n)")
        nvec = NT * 2 * H
        sq = zaf[:, 0:nvec * D].rearrange("p (v d) -> p v d", d=D)
        s7 = zbf[:, 0:nvec]
        nrm = zbf[:, nvec:2 * nvec]
        mk = zbf[:, 2 * nvec:3 * nvec]
        xn = zaf[:, nvec * D:nvec * D + 2 * G4 * C].rearrange("p (u t n) -> p u t n", u=2, t=G4)
        xnt = zbf[:, 3 * nvec:3 * nvec + 2 * G4 * C].rearrange("p (u n) -> p u n", u=2)
        acc = zbf[:, 5 * nvec:6 * nvec]
        sig = zaf[:, nvec * D + 2 * G4 * C:nvec * D + 2 * G4 * C + NT * (H + 1)].rearrange("p (t n) -> p t n", n=H + 1)

        w1s = big[:, 0:NE * FI].rearrange("p (e f) -> p e f", e=NE)
        o = NE * FI
        wos = big[:, o:o + FC * C].rearrange("p (k n) -> p k n", k=FC)
        o += FC * C
        wouts = big[:, o:o + C]
        o += C
        wrs = big[:, o:o + NE]
        o += NE
        b1s = big[0:NE, o:o + FI]
        o += FI
        bouts, bos, gams, bets = (big[:, o + n * C:o + (n + 1) * C] for n in range(4))
        o += 4 * C
        xte = big[:, o:o + 2 * G4 * P].rearrange("p (u n) -> p u n", u=2)
        o += 2 * G4 * P
        gel = big[:, o:o + FC * G4 * P].rearrange("p (k n) -> p k n", k=FC)
        o += FC * G4 * P
        oht = big[0:NE, o:o + 2 * G4 * P].rearrange("e (u n) -> e u n", u=2)
        o += 2 * G4 * P
        assert o <= NT * NP_
        GC = G4 * C
        x1 = zaf[:, 0:NT * C].rearrange("p (t n) -> p t n", n=C)
        br = zaf[:, NT * C:2 * NT * C].rearrange("p (t n) -> p t n", n=C)
        hln = zaf[:, 2 * NT * C:3 * NT * C].rearrange("p (t n) -> p t n", n=C)
        ycp = zbf[:, 0:2 * GC].rearrange("p (u n) -> p u n", u=2)
        ytr = zbf[:, 2 * GC:4 * GC].rearrange("p (u n) -> p u n", u=2)
        hs = ycp
        hts = ytr
        lg = zbf[:, 4 * GC:4 * GC + G4 * NE].rearrange("p (t e) -> p t e", e=NE)
        lgm = zbf[:, 4 * GC + 64:4 * GC + 64 + G4]
        eqr = zbf[:, 4 * GC + 128:4 * GC + 128 + G4 * NE].rearrange("p (t e) -> p t e", e=NE)
        eqm = zbf[:, 4 * GC + 192:4 * GC + 192 + G4]
        rank = zbf[:, 4 * GC + 256:4 * GC + 256 + NE]

        score = [ps(f"score{n}", [P, CH]) for n in range(2)]
        tra = [ps(f"tra{n}", [P, 512]) for n in range(2)]
        bld = ps("bld", [P, 8 * P], F16)
        yps = ps("yps", [P, 512])
        yv = yps[:, 0:TB * H * (D + 1)].rearrange("p (v d) -> p v d", d=D + 1)
        bldf = bld[:, :].bitcast(F32)

        x_in = sem("x_in")
        wa_in = sem("wa_in")
        cn_in = sem("cn_in")
        const_ok = sem("const_ok")
        stat_ok = sem("stat_ok")
        root_ok = sem("root_ok")
        rstd_ok = sem("rstd_ok")
        xn_ok = sem("xn_ok")
        xnt_ps = sem("xnt_ps")
        xnt_ok = sem("xnt_ok")
        proj_ps = sem("proj_ps")
        proj_ok = sem("proj_ok")
        dve_a = sem("dve_a")
        act_a = sem("act_a")
        act_p = sem("act_p")
        fac_ok = sem("fac_ok")
        tok_step = sem("tok_step")
        tok_ok = sem("tok_ok")
        v_ok = sem("v_ok")
        fill_ok = sem("fill_ok")
        opd_ok = sem("opd_ok")
        m_ps = sem("m_ps")
        w_ok = sem("w_ok")
        s1_ok = sem("s1_ok")
        s_ok = sem("s_ok")
        z_ok = sem("z_ok")
        l_ok = sem("l_ok")
        x_ok = sem("x_ok")
        e_ps = sem("e_ps")
        sc_ok = sem("sc_ok")
        sub_ok = sem("sub_ok")
        t_ps = sem("t_ps")
        exp_ok = sem("exp_ok")
        pv_ok = sem("pv_ok")
        y_ok = sem("y_ok")
        yn_step = sem("yn_step")
        wc_in = sem("wc_in")
        xc_in = sem("xc_in")
        c_tr = sem("c_tr")
        c_ev = sem("c_ev")
        c_pj = sem("c_pj")
        ao_ok = sem("ao_ok")
        dve_c = sem("dve_c")
        act_c = sem("act_c")
        h_ok = sem("h_ok")
        h_tr = sem("h_tr")
        h_ev = sem("h_ev")
        lg_ps = sem("lg_ps")
        oh_ok = sem("oh_ok")
        oh_tr = sem("oh_tr")
        oht_ok = sem("oht_ok")
        mk_ps = sem("mk_ps")
        xe_ok = sem("xe_ok")
        xe_used = sem("xe_used")
        pre_ps = sem("pre_ps")
        gel_ok = sem("gel_ok")
        dn_ps = sem("dn_ps")
        yf_ok = sem("yf_ok")
        fin_ok = sem("fin_ok")
        out_ok = sem("out_ok")
        c_cp = sem("c_cp")
        hs_ok = sem("hs_ok")
        hln_ok = sem("hln_ok")
        tm_ps = sem("tm_ps")
        stat_c = sem("stat_c")
        root_c = sem("root_c")
        rstd_c = sem("rstd_c")
        nrm_ok = sem("nrm_ok")
        bn_ok = sem("bn_ok")
        dve_b = sem("dve_b")
        x1_ok = sem("x1_ok")
        oh_step = sem("oh_step")
        yr_ok = sem("yr_ok")
        gb_ok = sem("gb_ok")

        block = ctx.enter_context(nc.Block())

        seen = sem("seen")
        CONSTS = 9
        EUC, HYP = 0, 1

        @block.sync
        def _(sp):
            xv = x.rearrange("(t p) n -> p t n", p=P)
            sp.dma_start(xin[:, :, :], xv).then_inc(x_in, 16)
            sp.dma_start(wall[:, :], w_all).then_inc(wa_in, 16)
            sp.dma_start(ball[:, :], b_all.broadcast_to([P, NP_])).then_inc(wa_in, 16)
            sp.dma_start(lk[:, :], log_k.broadcast_to([P, H])).then_inc(cn_in, 16)
            sp.dma_start(sc1[:, 0:1], thr.broadcast_to([P, 1])).then_inc(cn_in, 16)
            sp.dma_start(sc1[:, 1:2], qk_scale.broadcast_to([P, 1])).then_inc(cn_in, 16)
            sp.wait_ge(v_ok, 2 * NB)
            sp.dma_start(wouts, wout).then_inc(wc_in, 16)
            sp.dma_start(bouts, bout.broadcast_to([P, C])).then_inc(wc_in, 16)
            sp.dma_start(wrs, wr).then_inc(wc_in, 16)
            sp.dma_start(w1s, w1.rearrange("e p f -> p e f")).then_inc(wc_in, 16)
            sp.dma_start(wos, wo.rearrange("(k p) n -> p k n", p=P)).then_inc(wc_in, 16)
            sp.dma_start(b1s, b1).then_inc(wc_in, 16)
            sp.dma_start(bos, bo.broadcast_to([P, C])).then_inc(wc_in, 16)
            sp.dma_start(gams, gamma.broadcast_to([P, C])).then_inc(wc_in, 16)
            sp.dma_start(bets, beta.broadcast_to([P, C])).then_inc(wc_in, 16)
            sp.wait_ge(t_ps, NB * HALVES)
            sp.dma_start(x1, xv).then_inc(xc_in, 16)
            ov = out.rearrange("(t p) n -> p t n", p=P)
            with sp.Fori(0, NG) as n:
                sp.wait_ge(fin_ok, n + 1)
                sp.dma_start(ov[:, ds(n * G4, G4), :], x1[:, ds(n * G4, G4), :]).then_inc(out_ok, 16)
            sp.wait_ge(out_ok, 16 * NG)

        def reuse(eng, signal, count):
            if not (isinstance(count, int) and count == 0):
                eng.wait_ge(signal, count)

        def groups(eng, group):
            group(0, 0)
            group(1, 1)
            with eng.Fori(1, NG // 2) as i:
                group(i * 2, 0)
                group(i * 2 + 1, 1)

        def expert_groups(eng, group):
            group(0, 0)
            group(1, 1)
            with eng.Fori(1, NG // 2 - 1) as i:
                group(i * 2, 0)
                group(i * 2 + 1, 1)
            group(NG - 2, 0)
            group(NG - 1, 1, last=True)

        def items(prev, work):
            if prev and work:
                return [("floor", 0), ("floor", 1), ("mix", 0), ("floor", 2), ("floor", 3), ("mix", 1), ("floor", 4),
                        ("floor", 5), ("mix", 2), ("mix", 3), ("mix", 4), ("mix", 5)]
            return [("floor" if work else "mix", c) for c in range(NC_)]

        def steps(eng, step):
            step(0, 0, has_prev=False, has_two=False)
            step(1, 1, has_two=False)
            with eng.Fori(0, (NB - 4) // 2) as i:
                step(i * 2 + 2, 0)
                step(i * 2 + 3, 1)
            step(NB - 2, 0)
            step(NB - 1, 1, build=False)
            step(NB, 0, work=False, build=False)

        @block.gpsimd
        def _(pool):
            nc.gpsimd.memset(ident[:, :], 0.0).then_inc(const_ok, 1)
            nc.gpsimd.memset(identb[:, :], 0.0).then_inc(const_ok, 1)
            nc.gpsimd.memset(vone[:, :, :, :, :], 1.0).then_inc(const_ok, 1)
            nc.gpsimd.memset(cst[:, 0:1], (M_MIN - 1) / 2).then_inc(const_ok, 1)
            nc.gpsimd.memset(cst[:, 1:2], (M_MIN + 1) / 2).then_inc(const_ok, 1)
            pool.wait_ge(const_ok, 5)
            nc.gpsimd.affine_select(out=ident[:, :], in_=ident[:, :], compare_op=ALU.not_equal, fill=1.0, base=0,
                                    pattern=[[-1, P]], channel_multiplier=1).then_inc(const_ok, 1)
            nc.gpsimd.affine_select(out=maskb[:, :], in_=identb[:, :], compare_op=ALU.is_ge, fill=MASKED, base=0,
                                    pattern=[[-1, P]], channel_multiplier=1).then_inc(const_ok, 1)
            pool.wait_ge(const_ok, 7)
            nc.gpsimd.tensor_copy(ident16[:, :], ident[:, :]).then_inc(const_ok, 1)
            nc.gpsimd.tensor_copy(identb[:, :], ident[:, :]).then_inc(const_ok, 1)
            pool.wait_ge(fac_ok, 1)

            TS = 13

            def tokens(b):
                k0 = b * TS
                t0 = b * 4
                qv = proj[:, ds(b * TB, TB), QI:QI + C].rearrange("p t (h d) -> p t h d", d=D)
                kv = proj[:, ds(b * TB, TB), KI:KI + C].rearrange("p t (h d) -> p t h d", d=D)

                def per_head(a):
                    return a.unsqueeze(3).broadcast_to([P, TB, H, D])

                nc.gpsimd.tensor_tensor(vec[:, :, 0, :, :], qv, per_head(oma[:, ds(b * TB, TB), :]),
                                        ALU.mult).then_inc(tok_step, 1)
                nc.gpsimd.tensor_copy(vec[:, :, 2, :, :], kv).then_inc(tok_step, 1)
                nc.gpsimd.tensor_tensor(vec[:, :, 1, :, :], qv, per_head(gfac[:, ds(b * TB, TB), 0, :]),
                                        ALU.mult).then_inc(tok_step, 1)
                nc.gpsimd.tensor_tensor(vec[:, :, 3, :, :], kv, per_head(gfac[:, ds(b * TB, TB), 1, :]),
                                        ALU.mult).then_inc(tok_step, 1)
                pool.wait_ge(tok_step, k0 + 4)
                pool.sem_inc(seen)
                for qk in range(2):
                    nc.gpsimd.tensor_copy(vec[:, :, 1 + 2 * qk, :, 0], tmt[:, ds(b * TB, TB), qk, :])\
                        .then_inc(tok_step, 1)
                pool.wait_ge(tok_step, k0 + 6)
                pool.sem_inc(seen)
                slots = {0: (slice(0, 2), slice(2, 4)), 1: (slice(0, 4, 2), slice(1, 4, 2))}
                views = []
                for t in range(TB):
                    for side in range(2):
                        src = vec[:, t, 2 * side:2 * side + 2, :, :].rearrange("p a h d -> p (a h) d")
                        src = src.unsqueeze(2).broadcast_to([P, 2 * H, 2, D])
                        dst = stk[:, t, 2 * side:2 * side + 2, :, :, :].rearrange("p a h s d -> p (a h) s d")
                        views.append((dst[:, :, slots[side][0], :], dst[:, :, slots[side][1], :], src))
                if not (isinstance(t0, int) and t0 == 0):
                    pool.wait_ge(fill_ok, t0)
                    pool.sem_inc(seen)
                for high, low, src in views:
                    nc.gpsimd.tensor_scalar(high, src, 1.0, 0.0, ALU.mult, ALU.add).then_inc(tok_step, 1)
                pool.wait_ge(tok_step, k0 + 10)
                for high, low, src in views[:-1]:
                    nc.gpsimd.tensor_tensor(low, src, high, ALU.subtract).then_inc(tok_step, 1)
                high, low, src = views[-1]
                nc.gpsimd.tensor_tensor(low, src, high, ALU.subtract).then_inc(tok_ok, 1)
                pool.wait_ge(tok_step, k0 + 13)
                pool.wait_ge(tok_ok, b + 1)

            def factors(b, par, first):
                if not first:
                    pool.wait_ge(x_ok, (b - 1) * NC_)
                nc.gpsimd.tensor_copy(acb[:, par, :].rearrange("p (t h) -> p t h", h=H),
                                      acf[:, ds(b * TB, TB), :]).then_inc(v_ok, 1)

            def values(b, par, first):
                if not first:
                    pool.wait_ge(pv_ok, (b - 1) * HALVES)
                for t in range(TB):
                    last = nc.gpsimd.tensor_copy(
                        vone[:, par, t, :, 0:D],
                        proj[:, ds(b * TB + t, 1), VI:VI + C].rearrange("p a (h d) -> p (a h) d", d=D))
                last.then_inc(v_ok, 1)

            def subtract(b, par, c):
                tt = CHUNKS[c][0]
                pool.wait_ge(sc_ok, b * NC_ + c + 1)
                pool.sem_inc(seen)
                for h, col, width in heads_of(c):
                    v = za[:, par, c, col:col + width]
                    last = nc.gpsimd.tensor_scalar(v, v, -1.0, mxs[:, par, tt * H + h:tt * H + h + 1],
                                                   ALU.mult, ALU.add)
                last.then_inc(sub_ok, 1)

            def step(s, par, has_prev=True, has_two=True, work=True, build=True):
                if work:
                    factors(s, par, not has_prev)
                if build:
                    tokens(s + 1)
                for c in range(NC_):
                    if has_prev:
                        subtract(s - 1, 1 - par, c)
                    if work and c == 3:
                        values(s, par, not has_prev)

            tokens(0)
            steps(pool, step)

            def group1(n, u):
                pool.wait_ge(y_ok, NB)
                reuse(pool, c_tr, n)
                nc.gpsimd.tensor_copy(ycp[:, u, :].rearrange("p (t n) -> p t n", n=C),
                                      yatt[:, ds(n * G4, G4), :]).then_inc(c_cp, 1)

            groups(pool, group1)
            def group2(n, u):
                pool.wait_ge(hs_ok, n + 1)
                nc.gpsimd.tensor_copy(hln[:, ds(n * G4, G4), :],
                                      hs[:, u, :].rearrange("p (t n) -> p t n", n=C)).then_inc(hln_ok, 1)


            groups(pool, group2)
        @block.tensor
        def _(pe):
            pe.wait_ge(const_ok, CONSTS)
            pe.wait_ge(wa_in, 32)
            def group3(n, u):
                pe.wait_ge(xn_ok, n + 1)
                reuse(pe, xnt_ok, n)
                for k in range(G4):
                    last = nc.tensor.transpose(tra[u][:, k * P:(k + 1) * P], xn[:, u, k, :], ident[:, :])
                last.then_inc(xnt_ps, 1)
                pe.wait_ge(xnt_ok, n + 1)
                for k in range(G4):
                    reuse(pe, proj_ok, n * G4)
                    nc.tensor.matmul(score[k // 2][:, (k % 2) * 512:(k % 2) * 512 + NP_],
                                     xnt[:, u, k * P:(k + 1) * P], wall[:, :],
                                     start=True, stop=True).then_inc(proj_ps, 1)


            groups(pe, group3)
            def fill(b, kind, side, idx):
                pe.wait_ge(tok_ok, b + 1)
                pe.wait_ge(opd_ok, idx)
                for g in range(4):
                    for t in range(TB):
                        src = stk[:, t, 2 * side + kind, 4 * g:4 * g + 4, :, :].rearrange("p h s d -> p (h s d)")
                        last = nc.tensor.transpose(bld[:, (g * TB + t) * P:(g * TB + t + 1) * P], src, ident16[:, :])
                last.then_inc(fill_ok, 1)

            def products(bank2, par, kind, c, mask):
                tt, rows, quads = CHUNKS[c]
                width = P * (tt + 1)
                for bank, r in enumerate(rows):
                    for n, g in enumerate(quads):
                        col = bank * 512 + n * width
                        last = nc.tensor.matmul(
                            bank2[:, col:col + width],
                            opd[32 * r:32 * r + 32, par, kind, g, tt * P:(tt + 1) * P],
                            opd[32 * r:32 * r + 32, par, 2 + kind, g, 0:width],
                            start=not mask or n == 0, stop=not mask)
                if mask:
                    for bank in range(2):
                        seen_by = bank2[:, bank * 512:(bank + 1) * 512].rearrange("p (n w) -> p n w", w=width)
                        last = nc.tensor.matmul(seen_by[:, :, tt * P:(tt + 1) * P], identb[:, :],
                                                maskb[:, :].unsqueeze(1).broadcast_to([P, len(quads), P]),
                                                start=False, stop=True)
                return last

            def produce(s, par, work, prev, pos, free=None):
                users = items(prev, work)
                kind, c = users[pos]
                if pos >= 2:
                    free = (s, users[pos - 2])
                if free is not None:
                    at, (used, n) = free
                    if used == "floor":
                        pe.wait_ge(w_ok, at * NC_ + n + 1)
                    else:
                        pe.wait_ge(sc_ok, (at - 1) * NC_ + n + 1)
                if kind == "floor":
                    if c == 0:
                        pe.wait_ge(opd_ok, s * 4 + 2)
                    products(score[pos % 2], par, HYP, c, False).then_inc(m_ps, 1)
                else:
                    if c == 0:
                        pe.wait_ge(opd_ok, s * 4)
                    products(score[pos % 2], 1 - par, EUC, c, True).then_inc(e_ps, 1)

            def turn(b, par, c):
                pe.wait_ge(sub_ok, b * NC_ + c + 1)
                for j in range(2):
                    k = 2 * c + j
                    pe.wait_ge(exp_ok, b * HALVES + (k - 1 if k >= 2 else 0))
                    for n in range(4):
                        last = nc.tensor.transpose(tra[j][:, n * P:(n + 1) * P],
                                                   za[:, par, c, j * 512 + n * P:j * 512 + (n + 1) * P], ident[:, :])
                    last.then_inc(t_ps, 1)

            def attend(b, par, c):
                tt, rows, quads = CHUNKS[c]
                if c == 0:
                    pe.wait_ge(y_ok, b)
                    pe.wait_ge(v_ok, 2 * b + 2)
                for j in range(2):
                    k = 2 * c + j
                    pe.wait_ge(exp_ok, b * HALVES + k + 1)
                    n = 0
                    for g in quads:
                        h = 4 * g + rows[j]
                        for t in range(tt + 1):
                            last = nc.tensor.matmul(yv[:, tt * H + h, :], pt[:, k % 3, n * P:(n + 1) * P],
                                                    vone[:, par, t, h, :], start=(t == 0), stop=(t == tt))
                            n += 1
                    last.then_inc(pv_ok, 1)

            def step(s, par, has_prev=True, has_two=True, work=True, build=True):
                b, bpar, a = s - 1, 1 - par, s - 2
                users = items(has_prev, work)

                def prod(pos):
                    produce(s, par, work, has_prev, pos)

                if has_prev and work:
                    prod(2)
                    prod(3)
                    fill(s, EUC, 0, 4 * s + 2)
                    if has_two:
                        attend(a, par, 4)
                    prod(4)
                    prod(5)
                    fill(s, EUC, 1, 4 * s + 3)
                    if has_two:
                        turn(a, par, 5)
                    for pos in range(6, 10):
                        prod(pos)
                    if has_two:
                        attend(a, par, 5)
                    turn(b, bpar, 0)
                    prod(10)
                    if build:
                        fill(s + 1, HYP, 0, 4 * s + 4)
                    turn(b, bpar, 1)
                    attend(b, bpar, 0)
                    prod(11)
                    if build:
                        fill(s + 1, HYP, 1, 4 * s + 5)
                elif work:
                    for pos in range(2, NC_):
                        prod(pos)
                    for side in range(2):
                        fill(s, EUC, side, 4 * s + 2 + side)
                    for side in range(2):
                        fill(s + 1, HYP, side, 4 * s + 4 + side)
                else:
                    attend(a, par, 4)
                    turn(a, par, 5)
                    attend(a, par, 5)
                    prod(2)
                    turn(b, bpar, 0)
                    prod(3)
                    turn(b, bpar, 1)
                    attend(b, bpar, 0)
                    prod(4)
                    prod(5)
                if has_prev:
                    turn(b, bpar, 2)
                    attend(b, bpar, 1)
                if work:
                    produce(s + 1, 1 - par, build, True, 0, free=(s, users[-2]))
                if has_prev:
                    turn(b, bpar, 3)
                    attend(b, bpar, 2)
                    turn(b, bpar, 4)
                if work:
                    produce(s + 1, 1 - par, build, True, 1, free=(s, users[-1]))
                if has_prev:
                    attend(b, bpar, 3)

            pe.wait_ge(proj_ok, NT)
            fill(0, HYP, 0, 0)
            fill(0, HYP, 1, 1)
            produce(0, 0, True, False, 0)
            produce(0, 0, True, False, 1)
            steps(pe, step)
            attend(NB - 1, 1, 4)
            turn(NB - 1, 1, 5)
            attend(NB - 1, 1, 5)

            pe.wait_ge(sc_ok, NB * NC_)
            pe.wait_ge(wc_in, 16 * 9)
            def group4(n, u):
                pe.wait_ge(c_cp, n + 1)
                reuse(pe, c_ev, n)
                for k in range(G4):
                    last = nc.tensor.transpose(tra[u][:, k * P:(k + 1) * P], ycp[:, u, k * P:(k + 1) * P], ident[:, :])
                last.then_inc(c_tr, 1)
                pe.wait_ge(c_ev, n + 1)
                reuse(pe, ao_ok, n)
                for k in range(G4):
                    last = nc.tensor.matmul(score[u][:, k * P:(k + 1) * P], ytr[:, u, k * P:(k + 1) * P], wouts,
                                            start=True, stop=True)
                last.then_inc(c_pj, 1)


            groups(pe, group4)
            pre_bank = [score[0][:, 0:512], score[0][:, 512:1024], score[1][:, 0:512], score[1][:, 512:1024]]

            def route(n, u):
                pe.wait_ge(hs_ok, n + 1)
                reuse(pe, oht_ok, n)
                for k in range(G4):
                    last = nc.tensor.transpose(bldf[:, k * P:(k + 1) * P], hs[:, u, k * P:(k + 1) * P], ident[:, :])
                last.then_inc(h_tr, 1)
                pe.wait_ge(h_ev, n + 1)
                for k in range(G4):
                    last = nc.tensor.matmul(bldf[:, k * NE:(k + 1) * NE], hts[:, u, k * P:(k + 1) * P], wrs,
                                            start=True, stop=True)
                last.then_inc(lg_ps, 1)
                pe.wait_ge(oh_ok, n + 1)
                for k in range(G4):
                    last = nc.tensor.transpose(bldf[0:NE, k * P:(k + 1) * P], oh[:, u, k, :], ident[:, :])
                last.then_inc(oh_tr, 1)

            def spread(n, u, e):
                if e < 2:
                    reuse(pe, xe_ok, n * NE)
                else:
                    pe.wait_ge(xe_ok, n * NE + e - 1)
                for k in range(G4):
                    last = nc.tensor.matmul(tra[e % 2][:, k * P:(k + 1) * P],
                                            ohb[:, u, k, e:e + 1].broadcast_to([P, P]), identb[:, :],
                                            start=True, stop=True)
                last.then_inc(mk_ps, 1)

            def up(n, u):
                pe.wait_ge(oht_ok, n + 1)
                spread(n, u, 0)
                spread(n, u, 1)
                for f in range(FC):
                    reuse(pe, gel_ok, n * FC)
                    nc.tensor.matmul(pre_bank[f], b1s[:, f * P:(f + 1) * P], oht[:, u, :], start=True, stop=False)
                for e in range(NE):
                    pe.wait_ge(xe_ok, n * NE + e + 1)
                    for f in range(FC):
                        last = nc.tensor.matmul(pre_bank[f], w1s[:, e, f * P:(f + 1) * P], xte[:, e % 2, :],
                                                start=False, stop=(e == NE - 1))
                        if e == NE - 1:
                            last.then_inc(pre_ps, 1)
                    if e < NE - 1:
                        last.then_inc(xe_used, 1)
                    if e + 2 < NE:
                        spread(n, u, e + 2)

            def down(n):
                pe.wait_ge(gel_ok, (n + 1) * FC)
                reuse(pe, yf_ok, n)
                for k in range(G4):
                    for f in range(FC):
                        last = nc.tensor.matmul(yps[:, k * P:(k + 1) * P], gel[:, f, k * P:(k + 1) * P], wos[:, f, :],
                                                start=(f == 0), stop=(f == FC - 1))
                last.then_inc(dn_ps, 1)

            def expert_group(n, u, last=False):
                up(n, u)
                if not last:
                    route(n + 1, 1 - u)
                down(n)

            route(0, 0)
            expert_groups(pe, expert_group)

        @block.scalar
        def _(act):
            act.wait_ge(dve_a, 1)
            nc.scalar.activation(curv[:, 1, :], curv[:, 0, :], ACT.Exp).then_inc(act_a, 1)
            nc.scalar.activation(sc1[:, 2:3], sc1[:, 1:2], ACT.Exp, scale=-1.0).then_inc(act_a, 1)
            act.wait_ge(act_a, 1)
            nc.scalar.activation(curv[:, 2, :], curv[:, 1, :], ACT.Ln, bias=1.0).then_inc(act_a, 1)
            act.wait_ge(stat_ok, 1)
            nc.scalar.activation(nmr[:, :], var[:, :], ACT.Sqrt).then_inc(root_ok, 1)
            def group5(n, u):
                act.wait_ge(rstd_ok, 1)
                reuse(act, xnt_ps, n)
                for k in range(G4):
                    last = nc.scalar.activation(
                        xn[:, u, k, :], xin[:, ds(n * G4 + k, 1), :].rearrange("p a n -> p (a n)"), ACT.Identity,
                        scale=var[:, ds(n * G4 + k, 1)], bias=nmr[:, ds(n * G4 + k, 1)])
                last.then_inc(xn_ok, 1)

            groups(act, group5)
            with act.Fori(0, NG) as n:
                act.wait_ge(proj_ok, (n + 1) * G4)
                nc.scalar.activation(
                    sq[:, ds(n * (G4 * 2 * H), G4 * 2 * H), :].rearrange("p (t v) d -> p t (v d)", t=G4),
                    proj[:, ds(n * G4, G4), 0:2 * C], ACT.Square).then_inc(act_p, 1)
            act.wait_ge(dve_a, 8)
            nc.scalar.activation(nrm, nrm, ACT.Sqrt).then_inc(root_ok, 1)
            act.wait_ge(tm_ps, 1)
            nc.scalar.activation(acc, acc, ACT.Sqrt, bias=1.0).then_inc(root_ok, 1)
            nc.scalar.activation(sig, proj[:, :, II:II + H + 1], ACT.Exp, scale=-1.0).then_inc(root_ok, 1)

            def evac(par, kind, side, idx):
                act.wait_ge(fill_ok, idx + 1)
                nc.scalar.activation(opd[:, par, 2 * side + kind, :, :].rearrange("p g n -> p (g n)"), bld[:, :],
                                     ACT.Copy).then_inc(opd_ok, 1)

            def log(s, par, c):
                act.wait_ge(z_ok, s * NC_ + c + 1)
                nc.scalar.activation(za[:, par, c, :], za[:, par, c, :], ACT.Ln).then_inc(l_ok, 1)

            def exps(b, c):
                for j in range(2):
                    k = 2 * c + j
                    act.wait_ge(t_ps, b * HALVES + k + 1)
                    act.wait_ge(pv_ok, b * HALVES + (k - 2 if k >= 3 else 0))
                    nc.scalar.activation(pt[:, k % 3, :], tra[j][:, :], ACT.Exp, scale=-1.0).then_inc(exp_ok, 1)

            def step(s, par, has_prev=True, has_two=True, work=True, build=True):
                if work:
                    for c in range(NC_):
                        if has_two and c in (0, 5):
                            act.wait_ge(t_ps, (s - 2) * HALVES + (10 if c == 0 else 12))
                        act.wait_ge(w_ok, s * NC_ + c + 1)
                        nc.scalar.activation(za[:, par, c, :], zb[:, c, :], ACT.Sqrt, bias=cst[:, 0:1],
                                             scale=0.5 / (HS * HS)).then_inc(s1_ok, 1)
                        act.wait_ge(s1_ok, s * NC_ + c + 1)
                        nc.scalar.activation(zb[:, c, :], zb[:, c, :], ACT.Sqrt, bias=cst[:, 1:2],
                                             scale=0.5 / (HS * HS)).then_inc(s_ok, 1)
                        if has_prev and c in (1, 3):
                            evac(par, EUC, c // 2, 4 * s + 2 + c // 2)
                    if not has_prev:
                        for side in range(2):
                            evac(par, EUC, side, 4 * s + 2 + side)
                    nc.scalar.preload_act_table_set("natural_log_exp_and_others")
                if has_two:
                    exps(s - 2, 5)
                for c in range(NC_):
                    if work:
                        log(s, par, c)
                    if build and c in (1, 3):
                        evac(1 - par, HYP, c // 2, 4 * s + 4 + c // 2)
                    if has_prev and c < 5:
                        exps(s - 1, c)

            evac(0, HYP, 0, 0)
            evac(0, HYP, 1, 1)
            steps(act, step)
            exps(NB - 1, 5)

            def group6(n, u):
                act.wait_ge(c_tr, n + 1)
                reuse(act, c_pj, n)
                nc.scalar.activation(ytr[:, u, :], tra[u][:, :], ACT.Copy).then_inc(c_ev, 1)


            groups(act, group6)
            def scaled(dst, src, t):
                return nc.scalar.activation(dst, src.rearrange("p a n -> p (a n)"), ACT.Identity,
                                            scale=var[:, ds(t, 1)], bias=nmr[:, ds(t, 1)])

            def root(stage):
                act.wait_ge(stat_c, stage + 1)
                nc.scalar.activation(nmr[:, :], var[:, :], ACT.Sqrt).then_inc(root_c, 1)
                act.wait_ge(rstd_c, stage + 1)

            def in_place(stage):
                with act.Fori(0, NG) as n:
                    for k in range(G4):
                        t = n * G4 + k
                        last = scaled(br[:, ds(t, 1), :].rearrange("p a n -> p (a n)"), br[:, ds(t, 1), :], t)
                    last.then_inc(nrm_ok, 1)

            root(0)
            in_place(0)
            root(1)

            def feed(n, u):
                for k in range(G4):
                    t = n * G4 + k
                    last = scaled(hs[:, u, k * P:(k + 1) * P], x1[:, ds(t, 1), :], t)
                last.then_inc(hs_ok, 1)

            def route(n, u):
                act.wait_ge(oh_tr, n + 1)
                nc.scalar.activation(oht[:, u, :], bldf[0:NE, :], ACT.Copy).then_inc(oht_ok, 1)

            def gelu(n):
                reuse(act, dn_ps, n)
                for f in range(FC):
                    act.wait_ge(pre_ps, n * FC + f + 1)
                    nc.scalar.activation(gel[:, f, :], [score[0][:, 0:512], score[0][:, 512:1024], score[1][:, 0:512],
                                                        score[1][:, 512:1024]][f], ACT.Gelu).then_inc(gel_ok, 1)

            def expert_group(n, u, last=False, feeds=True):
                if feeds:
                    act.wait_ge(h_tr, n + 1)
                    act.wait_ge(hln_ok, n + 1)
                    feed(n + 2, u)
                gelu(n)
                if not last:
                    route(n + 1, 1 - u)

            feed(0, 0)
            feed(1, 1)
            route(0, 0)
            expert_group(0, 0)
            expert_group(1, 1)
            with act.Fori(1, NG // 2 - 1) as i:
                expert_group(i * 2, 0)
                expert_group(i * 2 + 1, 1)
            expert_group(NG - 2, 0, feeds=False)
            expert_group(NG - 1, 1, last=True, feeds=False)
            root(2)
            in_place(2)
            root(3)
            in_place(3)

        @block.vector
        def _(dve):
            V = nc.vector
            count_a = [0]

            def link(ins):
                count_a[0] += 1
                ins.then_inc(dve_a, 1)
                dve.wait_ge(dve_a, count_a[0])

            count_c = [0]

            def link_c(ins):
                count_c[0] += 1
                ins.then_inc(dve_c, 1)
                dve.wait_ge(dve_c, count_c[0])

            def moments(eps, chain):
                chain(V.tensor_tensor(mu[:, :], st6[:, :, 1], st6[:, :, 4], ALU.add))
                chain(V.tensor_tensor(tmp[:, 0, :], st6[:, :, 1], st6[:, :, 4], ALU.subtract))
                chain(V.tensor_tensor(tmp[:, 1, :], st6[:, :, 2], st6[:, :, 5], ALU.add))
                chain(V.tensor_scalar(mu[:, :], mu[:, :], 0.5, None, ALU.mult))
                chain(V.scalar_tensor_tensor(tmp[:, 0, :], tmp[:, 0, :], 0.25, tmp[:, 0, :], ALU.mult, ALU.mult))
                chain(V.scalar_tensor_tensor(tmp[:, 0, :], tmp[:, 1, :], 1.0 / C, tmp[:, 0, :], ALU.mult, ALU.add))
                return V.tensor_scalar(var[:, :], tmp[:, 0, :], eps, None, ALU.add)

            def inverses(chain):
                chain(V.reciprocal(var[:, :], nmr[:, :]))
                return V.scalar_tensor_tensor(nmr[:, :], mu[:, :], -1.0, var[:, :], ALU.mult, ALU.mult)

            dve.wait_ge(cn_in, 48)
            link(V.scalar_tensor_tensor(curv[:, 0, :], lk[:, :], -1.0, lk[:, :], ALU.mult, ALU.min))
            dve.wait_ge(act_a, 3)
            link(V.tensor_scalar(curv[:, 3, :], curv[:, 1, :], 1.0, -1.0, ALU.add, ALU.add))
            link(V.tensor_scalar(curv[:, 3, :], curv[:, 3, :], 1e-30, None, ALU.add))
            link(V.reciprocal(curv[:, 3, :], curv[:, 3, :]))
            link(V.scalar_tensor_tensor(curv[:, 2, :], curv[:, 2, :], 1e-30, curv[:, 3, :], ALU.add, ALU.mult))
            link(V.tensor_tensor(curv[:, 2, :], curv[:, 2, :], curv[:, 1, :], ALU.mult))
            link(V.scalar_tensor_tensor(curv[:, 2, :], lk[:, :], 0.0, curv[:, 2, :], ALU.max, ALU.add))
            n_before = count_a[0]
            assert n_before == 7
            dve.wait_ge(x_in, 16)
            with dve.Fori(0, NG) as n:
                for k in range(G4):
                    last = V.bn_stats(st6[:, ds(n * G4 + k, 1), :], xin[:, ds(n * G4 + k, 1), :])
                last.then_inc(bn_ok, 1)
            dve.wait_ge(bn_ok, NG)

            def link_b(ins):
                count_b[0] += 1
                ins.then_inc(dve_b, 1)
                dve.wait_ge(dve_b, count_b[0])

            count_b = [0]
            link_b(V.tensor_scalar(curv[:, 2, :], curv[:, 2, :], 1e-6, None, ALU.add))
            link_b(V.reciprocal(curv[:, 2, :], curv[:, 2, :]))
            link_b(V.tensor_scalar(curv[:, 2, :], curv[:, 2, :], -4.0, None, ALU.mult))
            link_b(V.tensor_scalar(sc1[:, 2:3], sc1[:, 2:3], 1.0, None, ALU.add))
            link_b(V.reciprocal(sc1[:, 2:3], sc1[:, 2:3]))
            link_b(V.tensor_scalar(sc1[:, 2:3], sc1[:, 2:3], 1.5, None, ALU.mult))
            moments(LN_EPS, link_b).then_inc(stat_ok, 1)
            dve.wait_ge(root_ok, 1)
            inverses(link_b).then_inc(rstd_ok, 1)
            dve.wait_ge(wa_in, 32)
            def group7(n, u):
                dve.wait_ge(xnt_ps, n + 1)
                reuse(dve, proj_ps, n * G4)
                V.tensor_copy(xnt[:, u, :], tra[u][:, :]).then_inc(xnt_ok, 1)
                for k in range(G4):
                    dve.wait_ge(proj_ps, n * G4 + k + 1)
                    V.tensor_tensor(proj[:, ds(n * G4 + k, 1), :].rearrange("p a n -> p (a n)"),
                                    score[k // 2][:, (k % 2) * 512:(k % 2) * 512 + NP_], ball[:, :],
                                    ALU.add).then_inc(proj_ok, 1)

            groups(dve, group7)
            dve.wait_ge(act_p, NG)
            dve.wait_ge(proj_ok, NT)
            link_b(V.tensor_reduce(s7, sq[:, :, 1:D], AX, ALU.add))
            link_b(V.tensor_tensor(mk, s7, sq[:, :, 0], ALU.subtract))
            V.tensor_tensor(nrm, s7, sq[:, :, 0], ALU.add).then_inc(dve_a, 1)
            dve.wait_ge(root_ok, 2)
            link_b(V.tensor_scalar(nrm, nrm, 1e-12, None, ALU.max))
            link_b(V.reciprocal(nrm, nrm))
            link_b(V.tensor_scalar(nrm, nrm, sc1[:, 2:3], None, ALU.mult))
            link_b(V.tensor_tensor(mk, mk, nrm, ALU.mult))
            link_b(V.tensor_tensor(mk, mk, nrm, ALU.mult))
            link_b(V.tensor_scalar(mk, mk, 1e-8, None, ALU.max))
            link_b(V.tensor_scalar(acc, mk, 1.0 / factorial(15), None, ALU.mult))
            for k in range(6, 0, -1):
                link_b(V.scalar_tensor_tensor(acc, acc, 1.0 / factorial(2 * k + 1), mk, ALU.add, ALU.mult))
            link_b(V.scalar_tensor_tensor(nrm, acc, 1.0, nrm, ALU.add, ALU.mult))
            link_b(V.tensor_tensor(acc, nrm, nrm, ALU.mult))
            link_b(V.tensor_tensor(acc, acc, s7, ALU.mult))
            nv = nrm.rearrange("p (t q h) -> p t q h", q=2, h=H)
            for qk, sign in ((0, -HS), (1, HS)):
                link_b(V.tensor_scalar(gfac[:, :, qk, :], nv[:, :, qk, :], sign, None, ALU.mult))
            V.tensor_copy(rin[:, 0:1], sc1[:, 2:3]).then_inc(tm_ps, 1)
            dve.wait_ge(root_ok, 4)
            link_b(V.tensor_scalar(tmt[:, :, :, :].rearrange("p t q h -> p (t q h)"), acc, HS, None, ALU.mult))
            link_b(V.tensor_scalar(sig, sig, 1.0, None, ALU.add))
            link_b(V.reciprocal(sig, sig))
            link_b(V.tensor_scalar(spk[:, :], sig[:, :, 0], sc1[:, 0:1], None, ALU.is_gt))
            link_b(V.tensor_scalar(oma[:, :, :], sig[:, :, 1:], -float(D) ** -0.5, float(D) ** -0.5,
                                   ALU.mult, ALU.add))
            V.tensor_tensor(acf[:, :, :], sig[:, :, 1:], curv[:, 2:3, :].broadcast_to([P, NT, H]),
                            ALU.mult).then_inc(fac_ok, 1)
            dve.wait_ge(fac_ok, 1)

            def floor(s, c, bank2, has_prev):
                dve.wait_ge(m_ps, s * NC_ + c + 1)
                if has_prev:
                    dve.wait_ge(z_ok, (s - 1) * NC_ + c + 1)
                V.tensor_scalar(zb[:, c, :], bank2[:, :], -M_MIN * HS * HS, 0.0, ALU.add,
                                ALU.max).then_inc(w_ok, 1)

            def normalise(b):
                dve.wait_ge(pv_ok, (b + 1) * HALVES)
                V.reciprocal(rin[:, :], yv[:, :, D]).then_inc(yn_step, 1)
                dve.wait_ge(yn_step, b * 2 + 1)
                rv = rin[:, :].rearrange("p (t h) -> p t h", h=H)
                V.tensor_tensor(rv, rv, spk[:, ds(b * TB, TB)].unsqueeze(2).broadcast_to([P, TB, H]),
                                ALU.mult).then_inc(yn_step, 1)
                dve.wait_ge(yn_step, b * 2 + 2)
                V.tensor_tensor(yatt[:, ds(b * TB, TB), :].rearrange("p t (h d) -> p (t h) d", d=D), yv[:, :, 0:D],
                                rin[:, :].unsqueeze(2).broadcast_to([P, TB * H, D]), ALU.mult).then_inc(y_ok, 1)

            def mix(b, par, c, bank2):
                tt = CHUNKS[c][0]
                dve.wait_ge(l_ok, b * NC_ + c + 1)
                dve.wait_ge(v_ok, 2 * b + 1)
                for h, col, width in heads_of(c):
                    v = za[:, par, c, col:col + width]
                    last = V.scalar_tensor_tensor(v, v, acb[:, par, tt * H + h:tt * H + h + 1], v, ALU.mult, ALU.mult)
                last.then_inc(x_ok, 1)
                dve.wait_ge(x_ok, b * NC_ + c + 1)
                dve.wait_ge(e_ps, b * NC_ + c + 1)
                dve.sem_inc(seen)
                for h, col, width in heads_of(c):
                    v = za[:, par, c, col:col + width]
                    last = V.tensor_tensor_reduce(out=v, in0=bank2[:, col:col + width], in1=v, scale=1.0,
                                                  scalar=-3.0e38, op0=ALU.add, op1=ALU.max,
                                                  accum_out=mxs[:, par, tt * H + h:tt * H + h + 1])
                last.then_inc(sc_ok, 1)

            def add_roots(s, par, c):
                dve.wait_ge(s_ok, s * NC_ + c + 1)
                V.tensor_tensor(za[:, par, c, :], za[:, par, c, :], zb[:, c, :], ALU.add).then_inc(z_ok, 1)

            def step(s, par, has_prev=True, has_two=True, work=True, build=True):
                sums = {8: (0,), 9: (1, 2), 10: (3, 4), 11: (5,)} if has_prev and work else {}
                for pos, (kind, c) in enumerate(items(has_prev, work)):
                    for n in sums.get(pos, ()):
                        add_roots(s, par, n)
                    if kind == "floor":
                        floor(s, c, score[pos % 2], has_prev)
                    else:
                        mix(s - 1, 1 - par, c, score[pos % 2])
                    if has_two and (pos == 9 or (not work and pos == 0)):
                        normalise(s - 2)
                if work and not sums:
                    for n in range(NC_):
                        add_roots(s, par, n)

            steps(dve, step)
            normalise(NB - 1)

            dve.wait_ge(wc_in, 16 * 9)
            def group8(n, u):
                dve.wait_ge(c_pj, n + 1)
                V.tensor_tensor(br[:, ds(n * G4, G4), :], score[u][:, 0:512].rearrange("p (t n) -> p t n", n=C),
                                bouts.unsqueeze(1).broadcast_to([P, G4, C]), ALU.add).then_inc(ao_ok, 1)
                dve.wait_ge(ao_ok, n + 1)
                for k in range(G4):
                    last = V.bn_stats(st6[:, ds(n * G4 + k, 1), :], br[:, ds(n * G4 + k, 1), :])
                last.then_inc(bn_ok, 1)

            groups(dve, group8)
            dve.wait_ge(bn_ok, 2 * NG)
            moments(LN_EPS, link_c).then_inc(stat_c, 1)
            dve.wait_ge(root_c, 1)
            inverses(link_c).then_inc(rstd_c, 1)
            dve.wait_ge(xc_in, 16)
            with dve.Fori(0, NG) as n:
                dve.wait_ge(nrm_ok, n + 1)
                V.tensor_tensor(x1[:, ds(n * G4, G4), :], x1[:, ds(n * G4, G4), :], br[:, ds(n * G4, G4), :],
                                ALU.add).then_inc(x1_ok, 1)
                dve.wait_ge(x1_ok, n + 1)
                for k in range(G4):
                    last = V.bn_stats(st6[:, ds(n * G4 + k, 1), :], x1[:, ds(n * G4 + k, 1), :])
                last.then_inc(bn_ok, 1)
            dve.wait_ge(bn_ok, 3 * NG)
            moments(LN_EPS, link_c).then_inc(stat_c, 1)
            for e in range(NE):
                last = V.memset(rank[:, e:e + 1], float(NE - e))
            link_c(last)
            dve.wait_ge(root_c, 2)
            inverses(link_c).then_inc(rstd_c, 1)

            OS = 6

            def route(n, u):
                dve.wait_ge(h_tr, n + 1)
                V.tensor_copy(hts[:, u, :], bldf[:, :]).then_inc(h_ev, 1)
                dve.wait_ge(lg_ps, n + 1)
                V.tensor_copy(lg, bldf[:, 0:G4 * NE].rearrange("p (t e) -> p t e", e=NE)).then_inc(oh_step, 1)
                dve.wait_ge(oh_step, n * OS + 1)
                V.tensor_reduce(lgm, lg, AX, ALU.max).then_inc(oh_step, 1)
                dve.wait_ge(oh_step, n * OS + 2)
                V.tensor_tensor(lg, lg, lgm.unsqueeze(2).broadcast_to([P, G4, NE]), ALU.is_equal).then_inc(oh_step, 1)
                dve.wait_ge(oh_step, n * OS + 3)
                V.tensor_tensor(eqr, lg, rank.unsqueeze(1).broadcast_to([P, G4, NE]), ALU.mult).then_inc(oh_step, 1)
                dve.wait_ge(oh_step, n * OS + 4)
                V.tensor_reduce(eqm, eqr, AX, ALU.max).then_inc(oh_step, 1)
                dve.wait_ge(oh_step, n * OS + 5)
                V.tensor_tensor(ohb[:, u, :, :], eqr, eqm.unsqueeze(2).broadcast_to([P, G4, NE]),
                                ALU.is_equal).then_inc(oh_step, 1)
                V.tensor_tensor(oh[:, u, :, :], eqr, eqm.unsqueeze(2).broadcast_to([P, G4, NE]),
                                ALU.is_equal).then_inc(oh_ok, 1)

            def select(n, u):
                for e in range(NE):
                    dve.wait_ge(mk_ps, n * NE + e + 1)
                    if e < 2:
                        reuse(dve, pre_ps, n * FC)
                    else:
                        dve.wait_ge(xe_used, n * (NE - 1) + e - 1)
                    V.tensor_tensor(xte[:, e % 2, :], hts[:, u, :], tra[e % 2][:, :], ALU.mult).then_inc(xe_ok, 1)

            def finish(n):
                dve.wait_ge(dn_ps, n + 1)
                g = br[:, ds(n * G4, G4), :]
                V.tensor_tensor(g, yps[:, :].rearrange("p (t n) -> p t n", n=C),
                                bos.unsqueeze(1).broadcast_to([P, G4, C]), ALU.add).then_inc(yf_ok, 1)
                dve.wait_ge(yf_ok, n + 1)
                dve.wait_ge(hln_ok, n + 1)
                V.tensor_tensor(g, g, hln[:, ds(n * G4, G4), :], ALU.add).then_inc(yr_ok, 1)
                dve.wait_ge(yr_ok, n + 1)
                for k in range(G4):
                    last = V.bn_stats(st6[:, ds(n * G4 + k, 1), :], br[:, ds(n * G4 + k, 1), :])
                last.then_inc(bn_ok, 1)

            def expert_group(n, u, last=False):
                select(n, u)
                if not last:
                    route(n + 1, 1 - u)
                finish(n)

            route(0, 0)
            expert_groups(dve, expert_group)

            dve.wait_ge(bn_ok, 4 * NG)
            moments(FFN_EPS, link_c).then_inc(stat_c, 1)
            dve.wait_ge(root_c, 3)
            inverses(link_c).then_inc(rstd_c, 1)
            with dve.Fori(0, NG) as n:
                g = br[:, ds(n * G4, G4), :]
                dve.wait_ge(nrm_ok, n + NG + 1)
                V.tensor_tensor(g, g, gams.unsqueeze(1).broadcast_to([P, G4, C]), ALU.mult).then_inc(gb_ok, 1)
                dve.wait_ge(gb_ok, n * 2 + 1)
                V.tensor_tensor(g, g, bets.unsqueeze(1).broadcast_to([P, G4, C]), ALU.add).then_inc(gb_ok, 1)
                dve.wait_ge(gb_ok, n * 2 + 2)
                for k in range(G4):
                    last = V.bn_stats(st6[:, ds(n * G4 + k, 1), :], br[:, ds(n * G4 + k, 1), :])
                last.then_inc(bn_ok, 1)
            dve.wait_ge(bn_ok, 5 * NG)
            moments(LN_EPS, link_c).then_inc(stat_c, 1)
            dve.wait_ge(root_c, 4)
            inverses(link_c).then_inc(rstd_c, 1)
            with dve.Fori(0, NG) as n:
                dve.wait_ge(nrm_ok, n + 2 * NG + 1)
                V.tensor_tensor(x1[:, ds(n * G4, G4), :], x1[:, ds(n * G4, G4), :], br[:, ds(n * G4, G4), :],
                                ALU.add).then_inc(fin_ok, 1)


def kernel(**inputs):
    import numpy as np
    import concourse.bacc as bacc
    from concourse import mybir as _mybir
    from concourse.bass_utils import run_bass_kernel_spmd

    a = {k.replace("L0_", ""): np.asarray(v) for k, v in inputs.items()}
    shape = a["attn_x"].shape
    c = shape[-1]
    data = {
        "x": a["attn_x"].reshape(-1, c),
        "w_all": np.concatenate([a["attn_Wqkv"], a["attn_Wimp"], a["attn_Walpha"]], 0).T,
        "b_all": np.concatenate([a["attn_bqkv"], a["attn_bimp"], a["attn_balpha"]], 0).reshape(1, -1),
        "wout": a["attn_Wout"].T,
        "bout": a["attn_bout"].reshape(1, -1),
        "thr": a["attn_spike_threshold"].reshape(1, 1),
        "log_k": a["attn_log_k"].reshape(1, -1),
        "qk_scale": a["attn_qk_scale"].reshape(1, 1),
        "wr": a["ffn_Wr"].T,
        "w1": a["ffn_W1"],
        "b1": a["ffn_b1"],
        "wo": a["ffn_Wo"],
        "bo": a["ffn_bo"].reshape(1, -1),
        "gamma": a["ffn_gamma"].reshape(1, -1),
        "beta": a["ffn_beta"].reshape(1, -1),
    }
    nc = bacc.Bacc("TRN2", target_bir_lowering=False, num_devices=1)
    arrays, args = {}, []
    for name, v in data.items():
        v = np.ascontiguousarray(v)
        arrays["in_" + name] = v
        args.append(nc.dram_tensor("in_" + name, v.shape, _mybir.dt.from_np(v.dtype), kind="ExternalInput").ap())
    out = nc.dram_tensor("out_x", data["x"].shape, _mybir.dt.float32, kind="ExternalOutput").ap()
    sandwich(nc, *args, out)
    r = run_bass_kernel_spmd(nc, [arrays], core_ids=[0])
    return r.results[0]["out_x"].reshape(shape)
```

```python
from contextlib import ExitStack
from math import factorial

import concourse.bass as bass
from concourse import mybir

ALU = mybir.AluOpType
ACT = mybir.ActivationFunctionType
F32 = mybir.dt.float32
F16 = mybir.dt.float16
BF16 = mybir.dt.bfloat16
AX = mybir.AxisListType.X
ds = bass.ds

P = 128
LN_EPS = 1e-5
FFN_EPS = 1e-12
M_MIN = 1.00000095367431640625
HS = 16.0
WS = 64.0
MASKED = -1e30


def sandwich(nc, x, w_all, b_all, wout, bout, thr, log_k, qk_scale, wr, w1, b1, wo, bo, gamma, beta, out):
    N, C = x.shape
    H = log_k.shape[1]
    D = C // H
    NE, _, FI = w1.shape
    NP_ = w_all.shape[1]
    NT = N // P
    TB = 2
    NB = NT // TB
    FC = FI // P
    QI, KI, VI, II, AI = 0, C, 2 * C, 3 * C, 3 * C + 1
    G4 = 4
    NG = NT // G4
    CH = 1024
    CHUNKS = [(0, (0, 1), (0, 1, 2, 3)), (0, (2, 3), (0, 1, 2, 3)), (1, (0, 1), (0, 1)),
              (1, (2, 3), (0, 1)), (1, (0, 1), (2, 3)), (1, (2, 3), (2, 3))]
    NC_ = len(CHUNKS)
    HALVES = 2 * NC_
    ZV = 5
    ZP = NC_ - ZV
    YW = H // 2 * (D + 1)

    def heads_of(c):
        tt, rows, quads = CHUNKS[c]
        width = P * (tt + 1)
        got = []
        for bank, r in enumerate(rows):
            for n, g in enumerate(quads):
                got.append((4 * g + r, bank * 512 + n * width, width))
        return got

    ctx = ExitStack()
    with ctx:
        def sb(name, shape, dt=F32):
            return ctx.enter_context(nc.sbuf_tensor(name, shape, dt))

        def ps(name, shape, dt=F32):
            return ctx.enter_context(nc.psum_tensor(name, shape, dt))

        def sem(name):
            return ctx.enter_context(nc.semaphore(name))

        xin = sb("xin", [P, NT, C])
        yatt = xin
        big = sb("big", [P, NT * NP_])
        proj = big[:, :].rearrange("p (t n) -> p t n", n=NP_)
        oma = proj[:, :, AI:AI + H]
        acf = sb("acf", [P, NT, H])
        spk = sb("spk", [P, NT])
        gfac = sb("gfac", [P, NT, 2, H])
        tmt = sb("tmt", [P, NT, 2, H])
        za = sb("za", [P, 2, NC_, CH])
        zb = sb("zb", [P, NC_, CH])
        pt = sb("pt", [P, 4, 512])
        stk = sb("stk", [P, TB, 4, H, 4, D], F16)
        vec = sb("vec", [P, TB, 4, H, D])
        opd = sb("opd", [P, 2, 4, 4, TB * P], F16)
        vone = sb("vone", [P, 2, TB, H, YW])
        vflat = vone[:, :, :, :, :].rearrange("p u t h w -> p u t (h w)")
        ysb = sb("ysb", [YW, 2 * TB * P])
        acb = sb("acb", [P, 2, TB * H])
        mxs = sb("mxs", [P, 2, TB * H])
        rin = sb("rin", [P, TB * H])
        ident = sb("ident", [P, P])
        ident16 = sb("ident16", [P, P], F16)
        identb = sb("identb", [P, P], BF16)
        maskb = sb("maskb", [P, P], BF16)
        sc1 = sb("sc1", [P, 4])
        st6 = sb("st6", [P, NT, 6])
        mu = sb("mu", [P, NT])
        var = sb("var", [P, NT])
        tmp = sb("tmp", [P, 2, NT])
        nmr = sb("nmr", [P, NT])

        zaf = za[:, :, :, :].rearrange("p a c n -> p (a c n)")
        zbf = zb[:, :, :].rearrange("p c n -> p (c n)")
        nvec = NT * 2 * H
        sq = zaf[:, 0:nvec * D].rearrange("p (v d) -> p v d", d=D)
        s7 = zbf[:, 0:nvec]
        nrm = zbf[:, nvec:2 * nvec]
        mk = zbf[:, 2 * nvec:3 * nvec]
        xn = zaf[:, nvec * D:nvec * D + 2 * G4 * C].rearrange("p (u t n) -> p u t n", u=2, t=G4)
        xnt = zbf[:, 3 * nvec:3 * nvec + 2 * G4 * C].rearrange("p (u n) -> p u n", u=2)
        acc = zbf[:, 5 * nvec:6 * nvec]
        sig = zaf[:, nvec * D + 2 * G4 * C:nvec * D + 2 * G4 * C + NT * (H + 1)].rearrange("p (t n) -> p t n", n=H + 1)

        o = nvec * D + 2 * G4 * C + NT * (H + 1)
        wall = zaf[:, o:o + NP_]
        ball = zaf[:, o + NP_:o + 2 * NP_]
        o += 2 * NP_
        lk = zaf[:, o:o + H]
        curv = zaf[:, o + H:o + 5 * H].rearrange("p (k h) -> p k h", h=H)

        w1s = big[:, 0:NE * FI].rearrange("p (e f) -> p e f", e=NE)
        o = NE * FI
        wos = big[:, o:o + FC * C].rearrange("p (k n) -> p k n", k=FC)
        o += FC * C
        wouts = big[:, o:o + C]
        o += C
        wrs = big[:, o:o + NE]
        o += NE
        LO = 32
        b1s = big[0:LO + NE, o:o + FI]
        o += FI
        bouts, bos, gams, bets = (big[:, o + n * C:o + (n + 1) * C] for n in range(4))
        o += 4 * C
        GT = G4 * P
        xte = big[:, o:o + 2 * GT].bitcast(F16).rearrange("p (u s n) -> p u s n", u=2, s=2)
        o += 2 * GT
        gel = big[:, o:o + FC * GT].rearrange("p (k n) -> p k n", k=FC)
        o += FC * GT
        oht = big[0:LO + NE, o:o + GT].bitcast(F16).rearrange("e (u n) -> e u n", u=2)
        o += GT
        w1h = big[:, o:o + NE * FI // 2].bitcast(F16).rearrange("p (e f) -> p e f", e=NE)
        o += NE * FI // 2
        b16 = big[0:LO + NE, o:o + FI // 2].bitcast(F16)
        o += FI // 2
        ht16 = big[:, o:o + 2 * GT].bitcast(F16).rearrange("p (u s n) -> p u s n", u=2, s=2)
        o += 2 * GT
        gst = big[:, o:o + G4 * 6].rearrange("p (t n) -> p t n", n=6)
        o += G4 * 6
        gmu, gvar, gnmr, gt0, gt1 = (big[:, o + n * G4:o + (n + 1) * G4] for n in range(5))
        o += 5 * G4
        assert o <= NT * NP_
        GC = G4 * C
        x1 = zaf[:, 0:NT * C].rearrange("p (t n) -> p t n", n=C)
        br = zaf[:, NT * C:2 * NT * C].rearrange("p (t n) -> p t n", n=C)
        hln = zaf[:, 2 * NT * C:3 * NT * C].rearrange("p (t n) -> p t n", n=C)
        ycp = zbf[:, 0:2 * GC].rearrange("p (u n) -> p u n", u=2)
        ytr = zbf[:, 2 * GC:4 * GC].rearrange("p (u n) -> p u n", u=2)
        hs = ycp
        hts = ytr
        lg = zbf[:, 4 * GC:4 * GC + G4 * NE].rearrange("p (t e) -> p t e", e=NE)
        lgm = zbf[:, 4 * GC + 64:4 * GC + 64 + G4]
        eqr = zbf[:, 4 * GC + 128:4 * GC + 128 + G4 * NE].rearrange("p (t e) -> p t e", e=NE)
        eqm = zbf[:, 4 * GC + 192:4 * GC + 192 + G4]
        OW = LO + NE
        oh = zbf[:, 5 * GC:5 * GC + 2 * G4 * OW].rearrange("p (u t e) -> p u t e", u=2, t=G4)
        o = 5 * GC + 2 * G4 * OW
        ohb = zbf[:, o:o + G4 * NE].bitcast(BF16).rearrange("p (u t e) -> p u t e", u=2, t=G4)
        o += G4 * NE
        w1l = zbf[:, o:o + NE * FI // 2].bitcast(F16).rearrange("p (e f) -> p e f", e=NE)
        assert o + NE * FI // 2 <= NC_ * CH
        rank = zbf[:, 4 * GC + 256:4 * GC + 256 + NE]

        score = [ps(f"score{n}", [P, CH]) for n in range(2)]
        tra = [ps(f"tra{n}", [P, 512]) for n in range(2)]
        bld = ps("bld", [P, 8 * P], F16)
        yps = ps("yps", [P, 512])
        bldf = bld[:, :].bitcast(F32)
        yv = bldf[:, 0:TB * H * (D + 1)].rearrange("p (v d) -> p v d", d=D + 1)

        x_in = sem("x_in")
        wa_in = sem("wa_in")
        cn_in = sem("cn_in")
        const_ok = sem("const_ok")
        stat_ok = sem("stat_ok")
        root_ok = sem("root_ok")
        rstd_ok = sem("rstd_ok")
        xn_ok = sem("xn_ok")
        xnt_ps = sem("xnt_ps")
        xnt_ok = sem("xnt_ok")
        proj_ps = sem("proj_ps")
        proj_ok = sem("proj_ok")
        dve_a = sem("dve_a")
        act_a = sem("act_a")
        act_p = sem("act_p")
        fac_ok = sem("fac_ok")
        tok_step = sem("tok_step")
        tok_ok = sem("tok_ok")
        v_ok = sem("v_ok")
        fill_ok = sem("fill_ok")
        opd_ok = sem("opd_ok")
        m_ps = sem("m_ps")
        w_ok = sem("w_ok")
        s1_ok = sem("s1_ok")
        s_ok = sem("s_ok")
        z_ok = sem("z_ok")
        zp_ok = sem("zp_ok")
        l_ok = sem("l_ok")
        x_ok = sem("x_ok")
        e_ps = sem("e_ps")
        sc_ok = sem("sc_ok")
        sub_ok = sem("sub_ok")
        t_ps = sem("t_ps")
        exp_ok = sem("exp_ok")
        pv_ok = sem("pv_ok")
        yev_ok = sem("yev_ok")
        ytr_ps = sem("ytr_ps")
        y_ok = sem("y_ok")
        yn_step = sem("yn_step")
        wc_in = sem("wc_in")
        xc_in = sem("xc_in")
        c_tr = sem("c_tr")
        c_ev = sem("c_ev")
        c_pj = sem("c_pj")
        ao_ok = sem("ao_ok")
        dve_c = sem("dve_c")
        act_c = sem("act_c")
        h_ok = sem("h_ok")
        h_tr = sem("h_tr")
        h_ev = sem("h_ev")
        lg_ps = sem("lg_ps")
        oh_ok = sem("oh_ok")
        oh_tr = sem("oh_tr")
        oht_ok = sem("oht_ok")
        mk_ps = sem("mk_ps")
        xe_ok = sem("xe_ok")
        xe_used = sem("xe_used")
        pre_ps = sem("pre_ps")
        gel_ok = sem("gel_ok")
        dn_ps = sem("dn_ps")
        yf_ok = sem("yf_ok")
        fin_ok = sem("fin_ok")
        out_ok = sem("out_ok")
        c_cp = sem("c_cp")
        hs_ok = sem("hs_ok")
        hln_ok = sem("hln_ok")
        tm_ps = sem("tm_ps")
        stat_c = sem("stat_c")
        root_c = sem("root_c")
        rstd_c = sem("rstd_c")
        nrm_ok = sem("nrm_ok")
        bn_ok = sem("bn_ok")
        dve_b = sem("dve_b")
        x1_ok = sem("x1_ok")
        oh_step = sem("oh_step")
        yr_ok = sem("yr_ok")
        w16_step = sem("w16_step")
        w16_ok = sem("w16_ok")
        h16_ok = sem("h16_ok")
        oh_zero = sem("oh_zero")
        ln_step = sem("ln_step")
        stat_g = sem("stat_g")
        root_g = sem("root_g")
        rstd_g = sem("rstd_g")
        nrm_g = sem("nrm_g")

        block = ctx.enter_context(nc.Block())

        seen = sem("seen")
        CONSTS = 8
        EUC, HYP = 0, 1

        @block.sync
        def _(sp):
            xv = x.rearrange("(t p) n -> p t n", p=P)
            sp.dma_start(xin[:, :, :], xv).then_inc(x_in, 16)
            sp.dma_start(wall[:, :], w_all).then_inc(wa_in, 16)
            sp.dma_start(ball[:, :], b_all.broadcast_to([P, NP_])).then_inc(wa_in, 16)
            sp.dma_start(lk[:, :], log_k.broadcast_to([P, H])).then_inc(cn_in, 16)
            sp.dma_start(sc1[:, 0:1], thr.broadcast_to([P, 1])).then_inc(cn_in, 16)
            sp.dma_start(sc1[:, 1:2], qk_scale.broadcast_to([P, 1])).then_inc(cn_in, 16)
            sp.wait_ge(v_ok, 2 * NB)
            sp.dma_start(wouts, wout).then_inc(wc_in, 16)
            sp.dma_start(bouts, bout.broadcast_to([P, C])).then_inc(wc_in, 16)
            sp.dma_start(wrs, wr).then_inc(wc_in, 16)
            sp.dma_start(w1s, w1.rearrange("e p f -> p e f")).then_inc(wc_in, 16)
            sp.dma_start(wos, wo.rearrange("(k p) n -> p k n", p=P)).then_inc(wc_in, 16)
            sp.dma_start(b1s[0:NE, :], b1).then_inc(wc_in, 16)
            sp.dma_start(b1s[LO:LO + NE, :], b1).then_inc(wc_in, 16)
            sp.dma_start(bos, bo.broadcast_to([P, C])).then_inc(wc_in, 16)
            sp.dma_start(gams, gamma.broadcast_to([P, C])).then_inc(wc_in, 16)
            sp.dma_start(bets, beta.broadcast_to([P, C])).then_inc(wc_in, 16)
            sp.wait_ge(t_ps, NB * HALVES)
            sp.dma_start(x1, xv).then_inc(xc_in, 16)
            ov = out.rearrange("(t p) n -> p t n", p=P)
            with sp.Fori(0, NG) as n:
                sp.wait_ge(fin_ok, n + 1)
                sp.dma_start(ov[:, ds(n * G4, G4), :], x1[:, ds(n * G4, G4), :]).then_inc(out_ok, 16)
            sp.wait_ge(out_ok, 16 * NG)

        def reuse(eng, signal, count):
            if not (isinstance(count, int) and count <= 0):
                eng.wait_ge(signal, count)

        def groups(eng, group):
            group(0, 0)
            group(1, 1)
            with eng.Fori(1, NG // 2) as i:
                group(i * 2, 0)
                group(i * 2 + 1, 1)

        def expert_groups(eng, group):
            group(0, 0)
            group(1, 1)
            with eng.Fori(1, NG // 2 - 1) as i:
                group(i * 2, 0)
                group(i * 2 + 1, 1)
            group(NG - 2, 0)
            group(NG - 1, 1, last=True)

        def items(prev, work):
            if prev and work:
                return [("floor", 0), ("floor", 1), ("mix", 0), ("floor", 2), ("floor", 3), ("mix", 1), ("floor", 4),
                        ("floor", 5), ("mix", 2), ("mix", 3), ("mix", 4), ("mix", 5)]
            return [("floor" if work else "mix", c) for c in range(NC_)]

        def steps(eng, step):
            step(0, 0, has_prev=False, has_two=False)
            step(1, 1, has_two=False)
            step(2, 0)
            with eng.Fori(0, (NB - 4) // 2) as i:
                step(i * 2 + 3, 1)
                step(i * 2 + 4, 0)
            step(NB - 1, 1, build=False)
            step(NB, 0, work=False, build=False)

        @block.gpsimd
        def _(pool):
            nc.gpsimd.memset(ident[:, :], 0.0).then_inc(const_ok, 1)
            nc.gpsimd.memset(identb[:, :], 0.0).then_inc(const_ok, 1)
            nc.gpsimd.memset(vone[:, :, :, :, :], 0.0).then_inc(const_ok, 1)
            pool.wait_ge(const_ok, 3)
            nc.gpsimd.affine_select(out=ident[:, :], in_=ident[:, :], compare_op=ALU.not_equal, fill=1.0, base=0,
                                    pattern=[[-1, P]], channel_multiplier=1).then_inc(const_ok, 1)
            nc.gpsimd.affine_select(out=maskb[:, :], in_=identb[:, :], compare_op=ALU.is_ge, fill=MASKED, base=0,
                                    pattern=[[-1, P]], channel_multiplier=1).then_inc(const_ok, 1)
            nc.gpsimd.memset(vone[:, :, :, :, D:D + 1], 1.0).then_inc(const_ok, 1)
            pool.wait_ge(const_ok, 6)
            nc.gpsimd.tensor_copy(ident16[:, :], ident[:, :]).then_inc(const_ok, 1)
            nc.gpsimd.tensor_copy(identb[:, :], ident[:, :]).then_inc(const_ok, 1)
            pool.wait_ge(fac_ok, 1)

            TS = 13

            def tokens(b):
                k0 = b * TS
                t0 = b * 4
                qv = proj[:, ds(b * TB, TB), QI:QI + C].rearrange("p t (h d) -> p t h d", d=D)
                kv = proj[:, ds(b * TB, TB), KI:KI + C].rearrange("p t (h d) -> p t h d", d=D)

                def per_head(a):
                    return a.unsqueeze(3).broadcast_to([P, TB, H, D])

                nc.gpsimd.tensor_tensor(vec[:, :, 0, :, :], qv, per_head(oma[:, ds(b * TB, TB), :]),
                                        ALU.mult).then_inc(tok_step, 1)
                nc.gpsimd.tensor_copy(vec[:, :, 2, :, :], kv).then_inc(tok_step, 1)
                nc.gpsimd.tensor_tensor(vec[:, :, 1, :, :], qv, per_head(gfac[:, ds(b * TB, TB), 0, :]),
                                        ALU.mult).then_inc(tok_step, 1)
                nc.gpsimd.tensor_tensor(vec[:, :, 3, :, :], kv, per_head(gfac[:, ds(b * TB, TB), 1, :]),
                                        ALU.mult).then_inc(tok_step, 1)
                pool.wait_ge(tok_step, k0 + 4)
                pool.sem_inc(seen)
                for qk in range(2):
                    nc.gpsimd.tensor_copy(vec[:, :, 1 + 2 * qk, :, 0], tmt[:, ds(b * TB, TB), qk, :])\
                        .then_inc(tok_step, 1)
                pool.wait_ge(tok_step, k0 + 6)
                pool.sem_inc(seen)
                slots = {0: (slice(0, 2), slice(2, 4)), 1: (slice(0, 4, 2), slice(1, 4, 2))}
                views = []
                for t in range(TB):
                    for side in range(2):
                        src = vec[:, t, 2 * side:2 * side + 2, :, :].rearrange("p a h d -> p (a h) d")
                        src = src.unsqueeze(2).broadcast_to([P, 2 * H, 2, D])
                        dst = stk[:, t, 2 * side:2 * side + 2, :, :, :].rearrange("p a h s d -> p (a h) s d")
                        views.append((dst[:, :, slots[side][0], :], dst[:, :, slots[side][1], :], src))
                if not (isinstance(t0, int) and t0 == 0):
                    pool.wait_ge(fill_ok, t0)
                    pool.sem_inc(seen)
                for high, low, src in views:
                    nc.gpsimd.tensor_scalar(high, src, 1.0, 0.0, ALU.mult, ALU.add).then_inc(tok_step, 1)
                pool.wait_ge(tok_step, k0 + 10)
                for high, low, src in views[:-1]:
                    nc.gpsimd.tensor_tensor(low, src, high, ALU.subtract).then_inc(tok_step, 1)
                high, low, src = views[-1]
                nc.gpsimd.tensor_tensor(low, src, high, ALU.subtract).then_inc(tok_ok, 1)
                pool.wait_ge(tok_step, k0 + 13)
                pool.wait_ge(tok_ok, b + 1)

            def factors(b, par, first):
                if not first:
                    pool.wait_ge(x_ok, (b - 1) * NC_)
                nc.gpsimd.tensor_copy(acb[:, par, :].rearrange("p (t h) -> p t h", h=H),
                                      acf[:, ds(b * TB, TB), :]).then_inc(v_ok, 1)

            def values(b, par, first):
                if not first:
                    pool.wait_ge(pv_ok, (b - 1) * HALVES)
                for t in range(TB):
                    last = nc.gpsimd.tensor_copy(
                        vone[:, par, t, :, 0:D],
                        proj[:, ds(b * TB + t, 1), VI:VI + C].rearrange("p a (h d) -> p (a h) d", d=D))
                last.then_inc(v_ok, 1)

            def subtract(b, par, c):
                tt = CHUNKS[c][0]
                pool.wait_ge(sc_ok, b * NC_ + c + 1)
                pool.sem_inc(seen)
                for h, col, width in heads_of(c):
                    v = za[:, par, c, col:col + width]
                    last = nc.gpsimd.tensor_scalar(v, v, -1.0, mxs[:, par, tt * H + h:tt * H + h + 1],
                                                   ALU.mult, ALU.add)
                last.then_inc(sub_ok, 1)

            def add_roots(s, par, c):
                pool.wait_ge(s_ok, s * NC_ + c + 1)
                nc.gpsimd.tensor_tensor(za[:, par, c, :], za[:, par, c, :], zb[:, c, :], ALU.add).then_inc(zp_ok, 1)

            def step(s, par, has_prev=True, has_two=True, work=True, build=True):
                if work:
                    factors(s, par, not has_prev)
                if build:
                    tokens(s + 1)
                for c in range(NC_):
                    if has_prev:
                        subtract(s - 1, 1 - par, c)
                    if work and c == 2:
                        for n in range(ZV, NC_):
                            add_roots(s, par, n)
                    if work and c == 3:
                        values(s, par, not has_prev)

            tokens(0)
            steps(pool, step)

            def scaled_halves(w, high, low, k0):
                nc.gpsimd.tensor_scalar(w, w, WS, 0.0, ALU.mult, ALU.add).then_inc(w16_step, 1)
                pool.wait_ge(w16_step, k0 + 1)
                nc.gpsimd.tensor_scalar(high, w, 1.0, 0.0, ALU.mult, ALU.add).then_inc(w16_step, 1)
                pool.wait_ge(w16_step, k0 + 2)
                return nc.gpsimd.tensor_tensor(low, w, high, ALU.subtract)

            pool.wait_ge(wc_in, 16 * 10)
            scaled_halves(w1s, w1h, w1l, 0).then_inc(w16_ok, 1)
            nc.gpsimd.memset(b16, 0.0).then_inc(w16_step, 1)
            pool.wait_ge(w16_step, 3)
            b_low = b16[LO:LO + NE, :]
            nc.gpsimd.tensor_scalar(b16[0:NE, :], b1s[0:NE, :], WS, 0.0, ALU.mult, ALU.add).then_inc(w16_ok, 1)
            scaled_halves(b1s[LO:LO + NE, :], b_low, b_low, 3).then_inc(w16_ok, 1)
            pool.wait_ge(w16_ok, 3)

            def group2(n, u):
                pool.wait_ge(hs_ok, n + 1)
                nc.gpsimd.tensor_copy(hln[:, ds(n * G4, G4), :],
                                      hs[:, u, :].rearrange("p (t n) -> p t n", n=C)).then_inc(hln_ok, 1)


            groups(pool, group2)
        @block.tensor
        def _(pe):
            pe.wait_ge(const_ok, CONSTS)
            pe.wait_ge(wa_in, 32)
            def group3(n, u):
                pe.wait_ge(xn_ok, n + 1)
                reuse(pe, xnt_ok, n)
                for k in range(G4):
                    last = nc.tensor.transpose(tra[u][:, k * P:(k + 1) * P], xn[:, u, k, :], ident[:, :])
                last.then_inc(xnt_ps, 1)
                pe.wait_ge(xnt_ok, n + 1)
                for k in range(G4):
                    reuse(pe, proj_ok, n * G4)
                    nc.tensor.matmul(score[k // 2][:, (k % 2) * 512:(k % 2) * 512 + NP_],
                                     xnt[:, u, k * P:(k + 1) * P], wall[:, :],
                                     start=True, stop=True).then_inc(proj_ps, 1)


            groups(pe, group3)
            def fill(b, kind, side, idx):
                pe.wait_ge(tok_ok, b + 1)
                pe.wait_ge(opd_ok, idx)
                for g in range(4):
                    for t in range(TB):
                        src = stk[:, t, 2 * side + kind, 4 * g:4 * g + 4, :, :].rearrange("p h s d -> p (h s d)")
                        last = nc.tensor.transpose(bld[:, (g * TB + t) * P:(g * TB + t + 1) * P], src, ident16[:, :])
                last.then_inc(fill_ok, 1)

            def products(bank2, par, kind, c, mask):
                tt, rows, quads = CHUNKS[c]
                width = P * (tt + 1)
                for bank, r in enumerate(rows):
                    for n, g in enumerate(quads):
                        col = bank * 512 + n * width
                        last = nc.tensor.matmul(
                            bank2[:, col:col + width],
                            opd[32 * r:32 * r + 32, par, kind, g, tt * P:(tt + 1) * P],
                            opd[32 * r:32 * r + 32, par, 2 + kind, g, 0:width],
                            start=not mask or n == 0, stop=not mask)
                if mask:
                    for bank in range(2):
                        seen_by = bank2[:, bank * 512:(bank + 1) * 512].rearrange("p (n w) -> p n w", w=width)
                        last = nc.tensor.matmul(seen_by[:, :, tt * P:(tt + 1) * P], identb[:, :],
                                                maskb[:, :].unsqueeze(1).broadcast_to([P, len(quads), P]),
                                                start=False, stop=True)
                return last

            def produce(s, par, work, prev, pos, free=None):
                users = items(prev, work)
                kind, c = users[pos]
                if pos >= 2:
                    free = (s, users[pos - 2])
                if free is not None:
                    at, (used, n) = free
                    if used == "floor":
                        pe.wait_ge(w_ok, at * NC_ + n + 1)
                    else:
                        pe.wait_ge(sc_ok, (at - 1) * NC_ + n + 1)
                if kind == "floor":
                    if c == 0:
                        pe.wait_ge(opd_ok, s * 4 + 2)
                    products(score[pos % 2], par, HYP, c, False).then_inc(m_ps, 1)
                else:
                    if c == 0:
                        pe.wait_ge(opd_ok, s * 4)
                    products(score[pos % 2], 1 - par, EUC, c, True).then_inc(e_ps, 1)

            def turn(b, par, c):
                pe.wait_ge(sub_ok, b * NC_ + c + 1)
                for j in range(2):
                    k = 2 * c + j
                    reuse(pe, exp_ok, b * HALVES + k - 1)
                    for n in range(4):
                        last = nc.tensor.transpose(tra[j][:, n * P:(n + 1) * P],
                                                   za[:, par, c, j * 512 + n * P:j * 512 + (n + 1) * P], ident[:, :])
                    last.then_inc(t_ps, 1)

            def attend(b, par, c):
                tt, rows, quads = CHUNKS[c]
                if c == 0:
                    reuse(pe, yev_ok, b)
                    pe.wait_ge(v_ok, 2 * b + 2)
                for j in range(2):
                    k = 2 * c + j
                    pe.wait_ge(exp_ok, b * HALVES + k + 1)
                    n = 0
                    for g in quads:
                        h = 4 * g + rows[j]
                        half, place = divmod(h, H // 2)
                        col = (half * TB + tt) * P
                        for t in range(tt + 1):
                            first = h * YW - place * (D + 1)
                            last = nc.tensor.matmul(
                                yps[0:YW, col:col + P], vflat[:, par, t, first:first + YW],
                                pt[:, k % 4, n * P:(n + 1) * P], start=(k == 0 and n == 0),
                                stop=(k == HALVES - 1 and g == quads[-1] and t == tt))
                            n += 1
                    last.then_inc(pv_ok, 1)

            def untangle(b, idx):
                pe.wait_ge(yev_ok, b + 1)
                pe.wait_ge(opd_ok, idx)
                for tt in range(TB):
                    for half in range(2):
                        last = nc.tensor.transpose(bldf[:, (tt * 2 + half) * YW:(tt * 2 + half + 1) * YW],
                                                   ysb[:, (half * TB + tt) * P:(half * TB + tt + 1) * P],
                                                   ident[0:YW, 0:YW])
                last.then_inc(ytr_ps, 1)

            def step(s, par, has_prev=True, has_two=True, work=True, build=True):
                b, bpar, a = s - 1, 1 - par, s - 2
                users = items(has_prev, work)

                def prod(pos):
                    produce(s, par, work, has_prev, pos)

                if has_prev and work:
                    prod(2)
                    prod(3)
                    if has_two:
                        reuse(pe, y_ok, a)
                    fill(s, EUC, 0, 4 * s + 2)
                    if has_two:
                        attend(a, par, 3)
                    prod(4)
                    prod(5)
                    prod(6)
                    fill(s, EUC, 1, 4 * s + 3)
                    if has_two:
                        turn(a, par, 5)
                    prod(7)
                    if has_two:
                        attend(a, par, 4)
                    for pos in range(8, 10):
                        prod(pos)
                    if build:
                        fill(s + 1, HYP, 0, 4 * s + 4)
                    prod(10)
                    turn(b, bpar, 0)
                    if has_two:
                        attend(a, par, 5)
                    prod(11)
                    if build:
                        fill(s + 1, HYP, 1, 4 * s + 5)
                    turn(b, bpar, 1)
                    if has_two:
                        untangle(a, 4 * s + (6 if build else 4))
                    attend(b, bpar, 0)
                elif work:
                    for pos in range(2, NC_):
                        prod(pos)
                    for side in range(2):
                        fill(s, EUC, side, 4 * s + 2 + side)
                    for side in range(2):
                        fill(s + 1, HYP, side, 4 * s + 4 + side)
                else:
                    attend(a, par, 3)
                    attend(a, par, 4)
                    turn(a, par, 5)
                    attend(a, par, 5)
                    prod(2)
                    turn(b, bpar, 0)
                    prod(3)
                    turn(b, bpar, 1)
                    pe.wait_ge(y_ok, a)
                    untangle(a, 4 * s)
                    attend(b, bpar, 0)
                    prod(4)
                    prod(5)
                if has_prev:
                    turn(b, bpar, 2)
                    attend(b, bpar, 1)
                if work:
                    produce(s + 1, 1 - par, build, True, 0, free=(s, users[-2]))
                if has_prev:
                    turn(b, bpar, 3)
                if work:
                    produce(s + 1, 1 - par, build, True, 1, free=(s, users[-1]))
                if has_prev:
                    attend(b, bpar, 2)
                    turn(b, bpar, 4)

            pe.wait_ge(proj_ok, NT)
            fill(0, HYP, 0, 0)
            fill(0, HYP, 1, 1)
            produce(0, 0, True, False, 0)
            produce(0, 0, True, False, 1)
            steps(pe, step)
            attend(NB - 1, 1, 3)
            attend(NB - 1, 1, 4)
            turn(NB - 1, 1, 5)
            attend(NB - 1, 1, 5)
            pe.wait_ge(y_ok, NB - 1)
            untangle(NB - 1, 4 * NB)

            pe.wait_ge(sc_ok, NB * NC_)
            pe.wait_ge(wc_in, 16 * 10)
            def group4(n, u):
                pe.wait_ge(c_cp, n + 1)
                reuse(pe, c_ev, n)
                for k in range(G4):
                    last = nc.tensor.transpose(tra[u][:, k * P:(k + 1) * P], ycp[:, u, k * P:(k + 1) * P], ident[:, :])
                last.then_inc(c_tr, 1)
                pe.wait_ge(c_ev, n + 1)
                reuse(pe, ao_ok, n)
                for k in range(G4):
                    last = nc.tensor.matmul(score[u][:, k * P:(k + 1) * P], ytr[:, u, k * P:(k + 1) * P], wouts,
                                            start=True, stop=True)
                last.then_inc(c_pj, 1)


            groups(pe, group4)
            pre_bank = [score[0][:, 0:512], score[0][:, 512:1024], score[1][:, 0:512], score[1][:, 512:1024]]

            def route(n, u, part):
                if part == 0:
                    pe.wait_ge(hs_ok, n + 1)
                    reuse(pe, oht_ok, n)
                    for k in range(G4):
                        last = nc.tensor.transpose(bldf[:, k * P:(k + 1) * P], hs[:, u, k * P:(k + 1) * P],
                                                   ident[:, :])
                    last.then_inc(h_tr, 1)
                elif part == 1:
                    pe.wait_ge(h_ev, n + 1)
                    for k in range(G4):
                        last = nc.tensor.matmul(bldf[:, k * NE:(k + 1) * NE], hts[:, u, k * P:(k + 1) * P], wrs,
                                                start=True, stop=True)
                    last.then_inc(lg_ps, 1)
                else:
                    pe.wait_ge(oh_ok, n + 1)
                    pe.sem_inc(seen)
                    for k in range(G4):
                        last = nc.tensor.transpose(bldf[0:OW, k * P:(k + 1) * P], oh[:, u, k, :], ident[:, :])
                    last.then_inc(oh_tr, 1)

            def spread(n, u, e):
                if e < 2:
                    reuse(pe, xe_ok, n * NE)
                else:
                    pe.wait_ge(xe_ok, n * NE + e - 1)
                for k in range(G4):
                    last = nc.tensor.matmul(tra[e % 2][:, k * P:(k + 1) * P],
                                            ohb[:, u, k, e:e + 1].broadcast_to([P, P]), identb[:, :],
                                            start=True, stop=True)
                last.then_inc(mk_ps, 1)

            def biases(n, u):
                pe.wait_ge(oht_ok, n + 1)
                for f in range(FC):
                    reuse(pe, gel_ok, n * FC)
                    nc.tensor.matmul(pre_bank[f], b16[:, f * P:(f + 1) * P], oht[:, u, :], start=True, stop=False)

            def up(n, u, last_group):
                for e in range(NE):
                    pe.wait_ge(xe_ok, n * NE + e + 1)
                    for f in range(FC):
                        for w, half in ((w1h, 0), (w1h, 1), (w1l, 0)):
                            last = nc.tensor.matmul(pre_bank[f], w[:, e, f * P:(f + 1) * P], xte[:, e % 2, half, :],
                                                    start=False, stop=(e == NE - 1 and w is w1l))
                        if e == NE - 1:
                            last.then_inc(pre_ps, 1)
                    if e < NE - 1:
                        last.then_inc(xe_used, 1)
                    if e + 2 < NE:
                        spread(n, u, e + 2)
                    if not last_group and e in (1, 3, 5):
                        route(n + 1, 1 - u, e // 2)
                if not last_group:
                    spread(n + 1, 1 - u, 0)
                    spread(n + 1, 1 - u, 1)

            def down(n):
                pe.wait_ge(gel_ok, (n + 1) * FC)
                reuse(pe, yf_ok, n)
                for k in range(G4):
                    for f in range(FC):
                        last = nc.tensor.matmul(yps[:, k * P:(k + 1) * P], gel[:, f, k * P:(k + 1) * P], wos[:, f, :],
                                                start=(f == 0), stop=(f == FC - 1))
                last.then_inc(dn_ps, 1)

            def expert_group(n, u, last=False):
                up(n, u, last)
                down(n)
                if not last:
                    biases(n + 1, 1 - u)

            for part in range(3):
                route(0, 0, part)
            pe.wait_ge(w16_ok, 3)
            spread(0, 0, 0)
            spread(0, 0, 1)
            biases(0, 0)
            expert_groups(pe, expert_group)

        @block.scalar
        def _(act):
            act.wait_ge(dve_a, 1)
            nc.scalar.activation(curv[:, 1, :], curv[:, 0, :], ACT.Exp).then_inc(act_a, 1)
            nc.scalar.activation(sc1[:, 2:3], sc1[:, 1:2], ACT.Exp, scale=-1.0).then_inc(act_a, 1)
            act.wait_ge(act_a, 1)
            nc.scalar.activation(curv[:, 2, :], curv[:, 1, :], ACT.Ln, bias=1.0).then_inc(act_a, 1)
            act.wait_ge(stat_ok, 1)
            nc.scalar.activation(nmr[:, :], var[:, :], ACT.Sqrt).then_inc(root_ok, 1)
            def group5(n, u):
                act.wait_ge(rstd_ok, 1)
                reuse(act, xnt_ps, n)
                for k in range(G4):
                    last = nc.scalar.activation(
                        xn[:, u, k, :], xin[:, ds(n * G4 + k, 1), :].rearrange("p a n -> p (a n)"), ACT.Identity,
                        scale=var[:, ds(n * G4 + k, 1)], bias=nmr[:, ds(n * G4 + k, 1)])
                last.then_inc(xn_ok, 1)

            groups(act, group5)
            with act.Fori(0, NG) as n:
                act.wait_ge(proj_ok, (n + 1) * G4)
                nc.scalar.activation(
                    sq[:, ds(n * (G4 * 2 * H), G4 * 2 * H), :].rearrange("p (t v) d -> p t (v d)", t=G4),
                    proj[:, ds(n * G4, G4), 0:2 * C], ACT.Square).then_inc(act_p, 1)
            act.wait_ge(dve_a, 8)
            nc.scalar.activation(nrm, nrm, ACT.Sqrt).then_inc(root_ok, 1)
            act.wait_ge(tm_ps, 1)
            nc.scalar.activation(acc, acc, ACT.Sqrt, bias=1.0).then_inc(root_ok, 1)
            nc.scalar.activation(sig, proj[:, :, II:II + H + 1], ACT.Exp, scale=-1.0).then_inc(root_ok, 1)

            def evac(par, kind, side, idx):
                act.wait_ge(fill_ok, idx + 1)
                nc.scalar.activation(opd[:, par, 2 * side + kind, :, :].rearrange("p g n -> p (g n)"), bld[:, :],
                                     ACT.Copy).then_inc(opd_ok, 1)

            def log(s, par, c):
                if c < ZV:
                    act.wait_ge(z_ok, s * ZV + c + 1)
                else:
                    act.wait_ge(zp_ok, s * ZP + c - ZV + 1)
                nc.scalar.activation(za[:, par, c, :], za[:, par, c, :], ACT.Ln).then_inc(l_ok, 1)

            def exps(b, c):
                for j in range(2):
                    k = 2 * c + j
                    act.wait_ge(t_ps, b * HALVES + k + 1)
                    reuse(act, pv_ok, b * HALVES + k - 3)
                    nc.scalar.activation(pt[:, k % 4, :], tra[j][:, :], ACT.Exp, scale=-1.0).then_inc(exp_ok, 1)

            def feature_y(b):
                act.wait_ge(pv_ok, (b + 1) * HALVES)
                reuse(act, ytr_ps, b)
                nc.scalar.activation(ysb[:, :], yps[0:YW, :], ACT.Copy).then_inc(yev_ok, 1)

            def step(s, par, has_prev=True, has_two=True, work=True, build=True):
                if work:
                    for c in range(NC_):
                        if has_two and c in (0, 5):
                            act.wait_ge(t_ps, (s - 2) * HALVES + (10 if c == 0 else 12))
                        act.wait_ge(w_ok, s * NC_ + c + 1)
                        nc.scalar.activation(za[:, par, c, :], zb[:, c, :], ACT.Sqrt,
                                             scale=0.5 / (HS * HS)).then_inc(s1_ok, 1)
                        act.wait_ge(s1_ok, s * NC_ + c + 1)
                        nc.scalar.activation(zb[:, c, :], zb[:, c, :], ACT.Sqrt, bias=1.0,
                                             scale=0.5 / (HS * HS)).then_inc(s_ok, 1)
                        if has_prev and c in (1, 3):
                            evac(par, EUC, c // 2, 4 * s + 2 + c // 2)
                    if not has_prev:
                        for side in range(2):
                            evac(par, EUC, side, 4 * s + 2 + side)
                    if has_prev and build:
                        evac(1 - par, HYP, 0, 4 * s + 4)
                    nc.scalar.preload_act_table_set("natural_log_exp_and_others")
                if has_two:
                    exps(s - 2, 5)
                for c in range(NC_):
                    if work:
                        log(s, par, c)
                    if build and not has_prev and c == 0:
                        evac(1 - par, HYP, 0, 4 * s + 4)
                    if build and c == 1:
                        evac(1 - par, HYP, 1, 4 * s + 5)
                    if has_prev and c < 5:
                        exps(s - 1, c)
                    if has_two and c == 0:
                        feature_y(s - 2)

            evac(0, HYP, 0, 0)
            evac(0, HYP, 1, 1)
            steps(act, step)
            exps(NB - 1, 5)
            feature_y(NB - 1)

            def group6(n, u):
                act.wait_ge(c_tr, n + 1)
                reuse(act, c_pj, n)
                nc.scalar.activation(ytr[:, u, :], tra[u][:, :], ACT.Copy).then_inc(c_ev, 1)


            groups(act, group6)
            def scaled(dst, src, t):
                return nc.scalar.activation(dst, src.rearrange("p a n -> p (a n)"), ACT.Identity,
                                            scale=var[:, ds(t, 1)], bias=nmr[:, ds(t, 1)])

            def root(stage):
                act.wait_ge(stat_c, stage + 1)
                nc.scalar.activation(nmr[:, :], var[:, :], ACT.Sqrt).then_inc(root_c, 1)
                act.wait_ge(rstd_c, stage + 1)

            def in_place(stage):
                with act.Fori(0, NG) as n:
                    for k in range(G4):
                        t = n * G4 + k
                        last = scaled(br[:, ds(t, 1), :].rearrange("p a n -> p (a n)"), br[:, ds(t, 1), :], t)
                    last.then_inc(nrm_ok, 1)

            root(0)
            in_place(0)
            root(1)

            def feed(n, u):
                for k in range(G4):
                    t = n * G4 + k
                    last = scaled(hs[:, u, k * P:(k + 1) * P], x1[:, ds(t, 1), :], t)
                last.then_inc(hs_ok, 1)

            def route(n, u):
                act.wait_ge(oh_tr, n + 1)
                nc.scalar.activation(oht[:, u, :], bldf[0:OW, :], ACT.Copy).then_inc(oht_ok, 1)

            def gelu(n):
                reuse(act, dn_ps, n)
                for f in range(FC):
                    act.wait_ge(pre_ps, n * FC + f + 1)
                    nc.scalar.activation(gel[:, f, :], [score[0][:, 0:512], score[0][:, 512:1024], score[1][:, 0:512],
                                                        score[1][:, 512:1024]][f], ACT.Gelu,
                                         scale=1.0 / WS).then_inc(gel_ok, 1)

            def polish(n):
                for half in range(2):
                    act.wait_ge(stat_g, n * 2 + half + 1)
                    nc.scalar.activation(gnmr, gvar, ACT.Sqrt).then_inc(root_g, 1)
                    act.wait_ge(rstd_g, n * 2 + half + 1)
                    act.sem_inc(seen)
                    for k in range(G4):
                        v = br[:, ds(n * G4 + k, 1), :].rearrange("p a n -> p (a n)")
                        last = nc.scalar.activation(v, v, ACT.Identity, scale=gvar[:, k:k + 1], bias=gnmr[:, k:k + 1])
                    last.then_inc(nrm_g, 1)

            def expert_group(n, u, last=False, feeds=True, first=False):
                if feeds:
                    act.wait_ge(h_tr, n + 1)
                    act.wait_ge(hln_ok, n + 1)
                    feed(n + 2, u)
                if not first:
                    polish(n - 1)
                if not last:
                    route(n + 1, 1 - u)
                gelu(n)

            feed(0, 0)
            feed(1, 1)
            route(0, 0)
            expert_group(0, 0, first=True)
            expert_group(1, 1)
            with act.Fori(1, NG // 2 - 1) as i:
                expert_group(i * 2, 0)
                expert_group(i * 2 + 1, 1)
            expert_group(NG - 2, 0, feeds=False)
            expert_group(NG - 1, 1, last=True, feeds=False)
            polish(NG - 1)

        @block.vector
        def _(dve):
            V = nc.vector
            count_a = [0]

            def link(ins):
                count_a[0] += 1
                ins.then_inc(dve_a, 1)
                dve.wait_ge(dve_a, count_a[0])

            count_c = [0]

            def link_c(ins):
                count_c[0] += 1
                ins.then_inc(dve_c, 1)
                dve.wait_ge(dve_c, count_c[0])

            def moments(eps, chain, stats=(st6, mu, var, tmp[:, 0, :], tmp[:, 1, :])):
                st, m, v, t0, t1 = stats
                chain(V.tensor_tensor(m[:, :], st[:, :, 1], st[:, :, 4], ALU.add))
                chain(V.tensor_tensor(t0, st[:, :, 1], st[:, :, 4], ALU.subtract))
                chain(V.tensor_tensor(t1, st[:, :, 2], st[:, :, 5], ALU.add))
                chain(V.tensor_scalar(m[:, :], m[:, :], 0.5, None, ALU.mult))
                chain(V.scalar_tensor_tensor(t0, t0, 0.25, t0, ALU.mult, ALU.mult))
                chain(V.scalar_tensor_tensor(t0, t1, 1.0 / C, t0, ALU.mult, ALU.add))
                return V.tensor_scalar(v[:, :], t0, eps, None, ALU.add)

            def inverses(chain, stats=(mu, var, nmr)):
                m, v, r = stats
                chain(V.reciprocal(v[:, :], r[:, :]))
                return V.scalar_tensor_tensor(r[:, :], m[:, :], -1.0, v[:, :], ALU.mult, ALU.mult)

            dve.wait_ge(cn_in, 48)
            link(V.scalar_tensor_tensor(curv[:, 0, :], lk[:, :], -1.0, lk[:, :], ALU.mult, ALU.min))
            dve.wait_ge(act_a, 3)
            link(V.tensor_scalar(curv[:, 3, :], curv[:, 1, :], 1.0, -1.0, ALU.add, ALU.add))
            link(V.tensor_scalar(curv[:, 3, :], curv[:, 3, :], 1e-30, None, ALU.add))
            link(V.reciprocal(curv[:, 3, :], curv[:, 3, :]))
            link(V.scalar_tensor_tensor(curv[:, 2, :], curv[:, 2, :], 1e-30, curv[:, 3, :], ALU.add, ALU.mult))
            link(V.tensor_tensor(curv[:, 2, :], curv[:, 2, :], curv[:, 1, :], ALU.mult))
            link(V.scalar_tensor_tensor(curv[:, 2, :], lk[:, :], 0.0, curv[:, 2, :], ALU.max, ALU.add))
            n_before = count_a[0]
            assert n_before == 7
            dve.wait_ge(x_in, 16)
            with dve.Fori(0, NG) as n:
                for k in range(G4):
                    last = V.bn_stats(st6[:, ds(n * G4 + k, 1), :], xin[:, ds(n * G4 + k, 1), :])
                last.then_inc(bn_ok, 1)
            dve.wait_ge(bn_ok, NG)

            def link_b(ins):
                count_b[0] += 1
                ins.then_inc(dve_b, 1)
                dve.wait_ge(dve_b, count_b[0])

            count_b = [0]
            link_b(V.tensor_scalar(curv[:, 2, :], curv[:, 2, :], 1e-6, None, ALU.add))
            link_b(V.reciprocal(curv[:, 2, :], curv[:, 2, :]))
            link_b(V.tensor_scalar(curv[:, 2, :], curv[:, 2, :], -4.0, None, ALU.mult))
            link_b(V.tensor_scalar(sc1[:, 2:3], sc1[:, 2:3], 1.0, None, ALU.add))
            link_b(V.reciprocal(sc1[:, 2:3], sc1[:, 2:3]))
            link_b(V.tensor_scalar(sc1[:, 2:3], sc1[:, 2:3], 1.5, None, ALU.mult))
            moments(LN_EPS, link_b).then_inc(stat_ok, 1)
            dve.wait_ge(root_ok, 1)
            inverses(link_b).then_inc(rstd_ok, 1)
            dve.wait_ge(wa_in, 32)
            def group7(n, u):
                dve.wait_ge(xnt_ps, n + 1)
                reuse(dve, proj_ps, n * G4)
                V.tensor_copy(xnt[:, u, :], tra[u][:, :]).then_inc(xnt_ok, 1)
                for k in range(G4):
                    dve.wait_ge(proj_ps, n * G4 + k + 1)
                    V.tensor_tensor(proj[:, ds(n * G4 + k, 1), :].rearrange("p a n -> p (a n)"),
                                    score[k // 2][:, (k % 2) * 512:(k % 2) * 512 + NP_], ball[:, :],
                                    ALU.add).then_inc(proj_ok, 1)

            groups(dve, group7)
            dve.wait_ge(act_p, NG)
            dve.wait_ge(proj_ok, NT)
            link_b(V.tensor_reduce(s7, sq[:, :, 1:D], AX, ALU.add))
            link_b(V.tensor_tensor(mk, s7, sq[:, :, 0], ALU.subtract))
            V.tensor_tensor(nrm, s7, sq[:, :, 0], ALU.add).then_inc(dve_a, 1)
            dve.wait_ge(root_ok, 2)
            link_b(V.tensor_scalar(nrm, nrm, 1e-12, None, ALU.max))
            link_b(V.reciprocal(nrm, nrm))
            link_b(V.tensor_scalar(nrm, nrm, sc1[:, 2:3], None, ALU.mult))
            link_b(V.tensor_tensor(mk, mk, nrm, ALU.mult))
            link_b(V.tensor_tensor(mk, mk, nrm, ALU.mult))
            link_b(V.tensor_scalar(mk, mk, 1e-8, None, ALU.max))
            link_b(V.tensor_scalar(acc, mk, 1.0 / factorial(15), None, ALU.mult))
            for k in range(6, 0, -1):
                link_b(V.scalar_tensor_tensor(acc, acc, 1.0 / factorial(2 * k + 1), mk, ALU.add, ALU.mult))
            link_b(V.scalar_tensor_tensor(nrm, acc, 1.0, nrm, ALU.add, ALU.mult))
            link_b(V.tensor_tensor(acc, nrm, nrm, ALU.mult))
            link_b(V.tensor_tensor(acc, acc, s7, ALU.mult))
            nv = nrm.rearrange("p (t q h) -> p t q h", q=2, h=H)
            for qk, sign in ((0, -HS), (1, HS)):
                link_b(V.tensor_scalar(gfac[:, :, qk, :], nv[:, :, qk, :], sign, None, ALU.mult))
            V.tensor_copy(rin[:, 0:1], sc1[:, 2:3]).then_inc(tm_ps, 1)
            dve.wait_ge(root_ok, 4)
            link_b(V.tensor_scalar(tmt[:, :, :, :].rearrange("p t q h -> p (t q h)"), acc, HS, None, ALU.mult))
            link_b(V.tensor_scalar(sig, sig, 1.0, None, ALU.add))
            link_b(V.reciprocal(sig, sig))
            link_b(V.tensor_scalar(spk[:, :], sig[:, :, 0], sc1[:, 0:1], None, ALU.is_gt))
            link_b(V.tensor_scalar(oma[:, :, :], sig[:, :, 1:], -float(D) ** -0.5, float(D) ** -0.5,
                                   ALU.mult, ALU.add))
            V.tensor_tensor(acf[:, :, :], sig[:, :, 1:], curv[:, 2:3, :].broadcast_to([P, NT, H]),
                            ALU.mult).then_inc(fac_ok, 1)
            dve.wait_ge(fac_ok, 1)

            def floor(s, c, bank2, has_prev):
                dve.wait_ge(m_ps, s * NC_ + c + 1)
                if has_prev:
                    if c < ZV:
                        dve.wait_ge(z_ok, (s - 1) * ZV + c + 1)
                    else:
                        dve.wait_ge(zp_ok, (s - 1) * ZP + c - ZV + 1)
                V.tensor_scalar(zb[:, c, :], bank2[:, :], M_MIN * HS * HS, -HS * HS, ALU.max,
                                ALU.add).then_inc(w_ok, 1)

            def normalise(b):
                dve.wait_ge(ytr_ps, b + 1)
                V.reciprocal(rin[:, :], yv[:, :, D]).then_inc(yn_step, 1)
                dve.wait_ge(yn_step, b * 2 + 1)
                rv = rin[:, :].rearrange("p (t h) -> p t h", h=H)
                V.tensor_tensor(rv, rv, spk[:, ds(b * TB, TB)].unsqueeze(2).broadcast_to([P, TB, H]),
                                ALU.mult).then_inc(yn_step, 1)
                dve.wait_ge(yn_step, b * 2 + 2)
                V.tensor_tensor(yatt[:, ds(b * TB, TB), :].rearrange("p t (h d) -> p (t h) d", d=D), yv[:, :, 0:D],
                                rin[:, :].unsqueeze(2).broadcast_to([P, TB * H, D]), ALU.mult).then_inc(y_ok, 1)

            def mix(b, par, c, bank2):
                tt = CHUNKS[c][0]
                dve.wait_ge(l_ok, b * NC_ + c + 1)
                dve.wait_ge(v_ok, 2 * b + 1)
                for h, col, width in heads_of(c):
                    v = za[:, par, c, col:col + width]
                    last = V.scalar_tensor_tensor(v, v, acb[:, par, tt * H + h:tt * H + h + 1], v, ALU.mult, ALU.mult)
                last.then_inc(x_ok, 1)
                dve.wait_ge(x_ok, b * NC_ + c + 1)
                dve.wait_ge(e_ps, b * NC_ + c + 1)
                dve.sem_inc(seen)
                for h, col, width in heads_of(c):
                    v = za[:, par, c, col:col + width]
                    last = V.tensor_tensor_reduce(out=v, in0=bank2[:, col:col + width], in1=v, scale=1.0,
                                                  scalar=-3.0e38, op0=ALU.add, op1=ALU.max,
                                                  accum_out=mxs[:, par, tt * H + h:tt * H + h + 1])
                last.then_inc(sc_ok, 1)

            def add_roots(s, par, c):
                dve.wait_ge(s_ok, s * NC_ + c + 1)
                V.tensor_tensor(za[:, par, c, :], za[:, par, c, :], zb[:, c, :], ALU.add).then_inc(z_ok, 1)

            def step(s, par, has_prev=True, has_two=True, work=True, build=True):
                sums = {8: (0,), 9: (1,), 10: (2, 3), 11: (4,)} if has_prev and work else {}
                for pos, (kind, c) in enumerate(items(has_prev, work)):
                    for n in sums.get(pos, ()):
                        add_roots(s, par, n)
                    if kind == "floor":
                        floor(s, c, score[pos % 2], has_prev)
                    else:
                        mix(s - 1, 1 - par, c, score[pos % 2])
                    if has_two and (pos == 11 or (not work and pos == 3)):
                        normalise(s - 2)
                if work and not sums:
                    for n in range(ZV):
                        add_roots(s, par, n)

            steps(dve, step)
            normalise(NB - 1)
            V.memset(oh, 0.0).then_inc(oh_zero, 1)
            dve.wait_ge(oh_zero, 1)

            dve.wait_ge(wc_in, 16 * 10)
            def group8(n, u, first=False):
                if not first:
                    reuse(dve, c_tr, n - 1)
                V.tensor_copy(ycp[:, u, :].rearrange("p (t n) -> p t n", n=C),
                              yatt[:, ds(n * G4, G4), :]).then_inc(c_cp, 1)
                if not first:
                    project(n - 1, 1 - u)

            def project(n, u):
                dve.wait_ge(c_pj, n + 1)
                V.tensor_tensor(br[:, ds(n * G4, G4), :], score[u][:, 0:512].rearrange("p (t n) -> p t n", n=C),
                                bouts.unsqueeze(1).broadcast_to([P, G4, C]), ALU.add).then_inc(ao_ok, 1)
                dve.wait_ge(ao_ok, n + 1)
                for k in range(G4):
                    last = V.bn_stats(st6[:, ds(n * G4 + k, 1), :], br[:, ds(n * G4 + k, 1), :])
                last.then_inc(bn_ok, 1)

            dve.wait_ge(y_ok, NB)
            group8(0, 0, first=True)
            group8(1, 1)
            with dve.Fori(1, NG // 2) as i:
                group8(i * 2, 0)
                group8(i * 2 + 1, 1)
            project(NG - 1, 1)
            dve.wait_ge(bn_ok, 2 * NG)
            moments(LN_EPS, link_c).then_inc(stat_c, 1)
            dve.wait_ge(root_c, 1)
            inverses(link_c).then_inc(rstd_c, 1)
            dve.wait_ge(xc_in, 16)
            with dve.Fori(0, NG) as n:
                dve.wait_ge(nrm_ok, n + 1)
                V.tensor_tensor(x1[:, ds(n * G4, G4), :], x1[:, ds(n * G4, G4), :], br[:, ds(n * G4, G4), :],
                                ALU.add).then_inc(x1_ok, 1)
                dve.wait_ge(x1_ok, n + 1)
                for k in range(G4):
                    last = V.bn_stats(st6[:, ds(n * G4 + k, 1), :], x1[:, ds(n * G4 + k, 1), :])
                last.then_inc(bn_ok, 1)
            dve.wait_ge(bn_ok, 3 * NG)
            moments(LN_EPS, link_c).then_inc(stat_c, 1)
            for e in range(NE):
                last = V.memset(rank[:, e:e + 1], float(NE - e))
            link_c(last)
            dve.wait_ge(root_c, 2)
            inverses(link_c).then_inc(rstd_c, 1)

            OS = 6

            def route(n, u, part):
                if part == 0:
                    dve.wait_ge(h_tr, n + 1)
                    V.tensor_copy(hts[:, u, :], bldf[:, :]).then_inc(h_ev, 1)
                    dve.wait_ge(h_ev, n + 1)
                    V.tensor_copy(ht16[:, u, 0, :], hts[:, u, :]).then_inc(h16_ok, 1)
                    dve.wait_ge(h16_ok, n * 2 + 1)
                    V.tensor_tensor(ht16[:, u, 1, :], hts[:, u, :], ht16[:, u, 0, :], ALU.subtract).then_inc(h16_ok, 1)
                    return
                dve.wait_ge(lg_ps, n + 1)
                V.tensor_copy(lg, bldf[:, 0:G4 * NE].rearrange("p (t e) -> p t e", e=NE)).then_inc(oh_step, 1)
                dve.wait_ge(oh_step, n * OS + 1)
                V.tensor_reduce(lgm, lg, AX, ALU.max).then_inc(oh_step, 1)
                dve.wait_ge(oh_step, n * OS + 2)
                V.tensor_tensor(lg, lg, lgm.unsqueeze(2).broadcast_to([P, G4, NE]), ALU.is_equal).then_inc(oh_step, 1)
                dve.wait_ge(oh_step, n * OS + 3)
                V.tensor_tensor(eqr, lg, rank.unsqueeze(1).broadcast_to([P, G4, NE]), ALU.mult).then_inc(oh_step, 1)
                dve.wait_ge(oh_step, n * OS + 4)
                V.tensor_reduce(eqm, eqr, AX, ALU.max).then_inc(oh_step, 1)
                dve.wait_ge(oh_step, n * OS + 5)
                V.tensor_tensor(ohb[:, u, :, :], eqr, eqm.unsqueeze(2).broadcast_to([P, G4, NE]),
                                ALU.is_equal).then_inc(oh_step, 1)
                for first in (0, LO):
                    last = V.tensor_tensor(oh[:, u, :, first:first + NE], eqr,
                                           eqm.unsqueeze(2).broadcast_to([P, G4, NE]), ALU.is_equal)
                last.then_inc(oh_ok, 1)

            def select(n, u, experts):
                dve.wait_ge(h16_ok, (n + 1) * 2)
                for e in experts:
                    dve.wait_ge(mk_ps, n * NE + e + 1)
                    if e < 2:
                        reuse(dve, pre_ps, n * FC)
                    else:
                        dve.wait_ge(xe_used, n * (NE - 1) + e - 1)
                    V.tensor_tensor(xte[:, e % 2, :, :], ht16[:, u, :, :],
                                    tra[e % 2][:, :].unsqueeze(1).broadcast_to([P, 2, GT]),
                                    ALU.mult).then_inc(xe_ok, 1)

            def finish(n):
                dve.wait_ge(dn_ps, n + 1)
                g = br[:, ds(n * G4, G4), :]
                V.tensor_tensor(g, yps[:, :].rearrange("p (t n) -> p t n", n=C),
                                bos.unsqueeze(1).broadcast_to([P, G4, C]), ALU.add).then_inc(yf_ok, 1)
                dve.wait_ge(yf_ok, n + 1)
                dve.wait_ge(hln_ok, n + 1)
                V.tensor_tensor(g, g, hln[:, ds(n * G4, G4), :], ALU.add).then_inc(yr_ok, 1)
                dve.wait_ge(yr_ok, n + 1)
                stats(n)

            def stats(n):
                dve.sem_inc(seen)
                for k in range(G4):
                    last = V.bn_stats(gst[:, k:k + 1, :], br[:, ds(n * G4 + k, 1), :])
                last.then_inc(bn_ok, 1)

            LS = 16

            def linked(base):
                count = [base]

                def chain(ins):
                    count[0] = count[0] + 1
                    ins.then_inc(ln_step, 1)
                    dve.wait_ge(ln_step, count[0])
                return chain

            gstats = (gst, gmu, gvar, gt0, gt1)
            ginv = (gmu, gvar, gnmr)

            def polish(n, part):
                g = br[:, ds(n * G4, G4), :]
                base = n * LS
                if part == 0:
                    dve.wait_ge(bn_ok, 3 * NG + n * 2 + 1)
                    moments(FFN_EPS, linked(base), gstats).then_inc(stat_g, 1)
                elif part == 1:
                    dve.wait_ge(root_g, n * 2 + 1)
                    inverses(linked(base + 6), ginv).then_inc(rstd_g, 1)
                elif part == 2:
                    chain = linked(base + 7)
                    dve.wait_ge(nrm_g, n * 2 + 1)
                    chain(V.tensor_tensor(g, g, gams.unsqueeze(1).broadcast_to([P, G4, C]), ALU.mult))
                    chain(V.tensor_tensor(g, g, bets.unsqueeze(1).broadcast_to([P, G4, C]), ALU.add))
                    stats(n)
                    dve.wait_ge(bn_ok, 3 * NG + n * 2 + 2)
                    moments(LN_EPS, chain, gstats).then_inc(stat_g, 1)
                elif part == 3:
                    dve.wait_ge(root_g, n * 2 + 2)
                    inverses(linked(base + 15), ginv).then_inc(rstd_g, 1)
                else:
                    dve.wait_ge(nrm_g, n * 2 + 2)
                    V.tensor_tensor(x1[:, ds(n * G4, G4), :], x1[:, ds(n * G4, G4), :], g, ALU.add).then_inc(fin_ok, 1)

            def expert_group(n, u, last=False, first=False):
                for part, e in enumerate(range(2, 7)):
                    select(n, u, (e,))
                    if not first:
                        polish(n - 1, part)
                    if not last and part in (1, 3):
                        route(n + 1, 1 - u, part // 2)
                select(n, u, (7,))
                if not last:
                    select(n + 1, 1 - u, (0, 1))
                finish(n)

            route(0, 0, 0)
            route(0, 0, 1)
            select(0, 0, (0, 1))
            expert_group(0, 0, first=True)
            expert_group(1, 1)
            with dve.Fori(1, NG // 2 - 1) as i:
                expert_group(i * 2, 0)
                expert_group(i * 2 + 1, 1)
            expert_group(NG - 2, 0)
            expert_group(NG - 1, 1, last=True)
            for part in range(5):
                polish(NG - 1, part)


def kernel(**inputs):
    import numpy as np
    import concourse.bacc as bacc
    from concourse import mybir as _mybir
    from concourse.bass_utils import run_bass_kernel_spmd

    a = {k.replace("L0_", ""): np.asarray(v) for k, v in inputs.items()}
    shape = a["attn_x"].shape
    c = shape[-1]
    data = {
        "x": a["attn_x"].reshape(-1, c),
        "w_all": np.concatenate([a["attn_Wqkv"], a["attn_Wimp"], a["attn_Walpha"]], 0).T,
        "b_all": np.concatenate([a["attn_bqkv"], a["attn_bimp"], a["attn_balpha"]], 0).reshape(1, -1),
        "wout": a["attn_Wout"].T,
        "bout": a["attn_bout"].reshape(1, -1),
        "thr": a["attn_spike_threshold"].reshape(1, 1),
        "log_k": a["attn_log_k"].reshape(1, -1),
        "qk_scale": a["attn_qk_scale"].reshape(1, 1),
        "wr": a["ffn_Wr"].T,
        "w1": a["ffn_W1"],
        "b1": a["ffn_b1"],
        "wo": a["ffn_Wo"],
        "bo": a["ffn_bo"].reshape(1, -1),
        "gamma": a["ffn_gamma"].reshape(1, -1),
        "beta": a["ffn_beta"].reshape(1, -1),
    }
    nc = bacc.Bacc("TRN2", target_bir_lowering=False, num_devices=1)
    arrays, args = {}, []
    for name, v in data.items():
        v = np.ascontiguousarray(v)
        arrays["in_" + name] = v
        args.append(nc.dram_tensor("in_" + name, v.shape, _mybir.dt.from_np(v.dtype), kind="ExternalInput").ap())
    out = nc.dram_tensor("out_x", data["x"].shape, _mybir.dt.float32, kind="ExternalOutput").ap()
    sandwich(nc, *args, out)
    r = run_bass_kernel_spmd(nc, [arrays], core_ids=[0])
    return r.results[0]["out_x"].reshape(shape)
```

```python
from contextlib import ExitStack
from math import factorial

import concourse.bass as bass
from concourse import mybir

ALU = mybir.AluOpType
ACT = mybir.ActivationFunctionType
F32 = mybir.dt.float32
F16 = mybir.dt.float16
BF16 = mybir.dt.bfloat16
AX = mybir.AxisListType.X
ds = bass.ds

P = 128
LN_EPS = 1e-5
FFN_EPS = 1e-12
M_MIN = 1.00000095367431640625
HS = 16.0
WS = 64.0
MASKED = -1e30


def sandwich(nc, x, w_all, b_all, wout, bout, thr, log_k, qk_scale, wr, w1, b1, wo, bo, gamma, beta, out):
    N, C = x.shape
    H = log_k.shape[1]
    D = C // H
    NE, _, FI = w1.shape
    NP_ = w_all.shape[1]
    NT = N // P
    TB = 2
    NB = NT // TB
    FC = FI // P
    QI, KI, VI, II, AI = 0, C, 2 * C, 3 * C, 3 * C + 1
    G4 = 4
    NG = NT // G4
    X_PARTS = (slice(0, 2 * G4), slice(2 * G4, NT))
    CH = 1024
    CHUNKS = [(0, (0, 1), (0, 1, 2, 3)), (0, (2, 3), (0, 1, 2, 3)), (1, (0, 1), (0, 1)),
              (1, (2, 3), (0, 1)), (1, (0, 1), (2, 3)), (1, (2, 3), (2, 3))]
    NC_ = len(CHUNKS)
    HALVES = 2 * NC_
    ZV = 4
    ZP = NC_ - ZV
    YW = H // 2 * (D + 1)

    def heads_of(c):
        tt, rows, quads = CHUNKS[c]
        width = P * (tt + 1)
        got = []
        for bank, r in enumerate(rows):
            for n, g in enumerate(quads):
                got.append((4 * g + r, bank * 512 + n * width, width))
        return got

    ctx = ExitStack()
    with ctx:
        def sb(name, shape, dt=F32):
            return ctx.enter_context(nc.sbuf_tensor(name, shape, dt))

        def ps(name, shape, dt=F32):
            return ctx.enter_context(nc.psum_tensor(name, shape, dt))

        def sem(name):
            return ctx.enter_context(nc.semaphore(name))

        xin = sb("xin", [P, NT, C])
        yatt = xin
        big = sb("big", [P, NT * NP_])
        proj = big[:, :].rearrange("p (t n) -> p t n", n=NP_)
        oma = proj[:, :, AI:AI + H]
        acf = sb("acf", [P, NT, H])
        spk = sb("spk", [P, NT])
        gfac = sb("gfac", [P, NT, 2, H])
        tmt = sb("tmt", [P, NT, 2, H])
        za = sb("za", [P, 2, NC_, CH])
        zb = sb("zb", [P, NC_, CH])
        pt = sb("pt", [P, 4, 512])
        stk = sb("stk", [P, TB, 4, H, 4, D], F16)
        vec = sb("vec", [P, TB, 4, H, D])
        opd = sb("opd", [P, 2, 4, 4, TB * P], F16)
        vone = sb("vone", [P, 2, TB, H, YW])
        vflat = vone[:, :, :, :, :].rearrange("p u t h w -> p u t (h w)")
        ysb = sb("ysb", [YW, 2 * TB * P])
        acb = sb("acb", [P, 2, TB * H])
        mxs = sb("mxs", [P, 2, TB * H])
        rin = sb("rin", [P, TB * H])
        ident = sb("ident", [P, P])
        ident16 = sb("ident16", [P, P], F16)
        identb = sb("identb", [P, P], BF16)
        maskb = sb("maskb", [P, P], BF16)
        sc1 = sb("sc1", [P, 4])
        st6 = sb("st6", [P, NT, 6])
        mu = sb("mu", [P, NT])
        var = sb("var", [P, NT])
        tmp = sb("tmp", [P, 2, NT])
        nmr = sb("nmr", [P, NT])

        zaf = za[:, :, :, :].rearrange("p a c n -> p (a c n)")
        zbf = zb[:, :, :].rearrange("p c n -> p (c n)")
        nvec = NT * 2 * H
        sq = zaf[:, 0:nvec * D].rearrange("p (v d) -> p v d", d=D)
        s7 = zbf[:, 0:nvec]
        nrm = zbf[:, nvec:2 * nvec]
        mk = zbf[:, 2 * nvec:3 * nvec]
        xn = zaf[:, nvec * D:nvec * D + 2 * G4 * C].rearrange("p (u t n) -> p u t n", u=2, t=G4)
        xnt = zbf[:, 3 * nvec:3 * nvec + 2 * G4 * C].rearrange("p (u n) -> p u n", u=2)
        acc = zbf[:, 5 * nvec:6 * nvec]
        sig = zaf[:, nvec * D + 2 * G4 * C:nvec * D + 2 * G4 * C + NT * (H + 1)].rearrange("p (t n) -> p t n", n=H + 1)

        o = nvec * D + 2 * G4 * C + NT * (H + 1)
        wall = zaf[:, o:o + NP_]
        ball = zaf[:, o + NP_:o + 2 * NP_]
        o += 2 * NP_
        lk = zaf[:, o:o + H]
        curv = zaf[:, o + H:o + 5 * H].rearrange("p (k h) -> p k h", h=H)

        PARTS = [(slice(a, b), slice(a * 2 * H, b * 2 * H)) for a, b in ((0, G4), (G4, NT))]

        w1s = big[:, 0:NE * FI].rearrange("p (e f) -> p e f", e=NE)
        o = NE * FI
        wos = big[:, o:o + FC * C].rearrange("p (k n) -> p k n", k=FC)
        o += FC * C
        wouts = big[:, o:o + C]
        o += C
        wrs = big[:, o:o + NE]
        o += NE
        LO = 32
        b1s = big[0:LO + NE, o:o + FI]
        o += FI
        bouts, bos, gams, bets = (big[:, o + n * C:o + (n + 1) * C] for n in range(4))
        o += 4 * C
        GT = G4 * P
        xte = big[:, o:o + 2 * GT].bitcast(F16).rearrange("p (u s n) -> p u s n", u=2, s=2)
        o += 2 * GT
        gel = big[:, o:o + FC * GT].rearrange("p (k n) -> p k n", k=FC)
        o += FC * GT
        oht = big[0:LO + NE, o:o + GT].bitcast(F16).rearrange("e (u n) -> e u n", u=2)
        o += GT
        w1h = big[:, o:o + NE * FI // 2].bitcast(F16).rearrange("p (e f) -> p e f", e=NE)
        o += NE * FI // 2
        b16 = big[0:LO + NE, o:o + FI // 2].bitcast(F16)
        o += FI // 2
        ht16 = big[:, o:o + 2 * GT].bitcast(F16).rearrange("p (u s n) -> p u s n", u=2, s=2)
        o += 2 * GT
        gst = big[:, o:o + G4 * 6].rearrange("p (t n) -> p t n", n=6)
        o += G4 * 6
        pst = big[:, o:o + G4 * 6].rearrange("p (t n) -> p t n", n=6)
        o += G4 * 6
        gmu, gvar, gnmr, gt0, gt1, pmu, pvar, pnmr, pt0, pt1 = (big[:, o + n * G4:o + (n + 1) * G4] for n in range(10))
        o += 10 * G4
        assert o <= NT * NP_
        GC = G4 * C
        x1 = zaf[:, 0:NT * C].rearrange("p (t n) -> p t n", n=C)
        br = xin
        hln = zaf[:, 2 * NT * C:3 * NT * C].rearrange("p (t n) -> p t n", n=C)
        ytr = zbf[:, 2 * GC:4 * GC].rearrange("p (u n) -> p u n", u=2)
        hs = zbf[:, 0:2 * GC].rearrange("p (u n) -> p u n", u=2)
        hts = ytr
        lg = zbf[:, 4 * GC:4 * GC + G4 * NE].rearrange("p (t e) -> p t e", e=NE)
        lgm = zbf[:, 4 * GC + 64:4 * GC + 64 + G4]
        eqr = zbf[:, 4 * GC + 128:4 * GC + 128 + G4 * NE].rearrange("p (t e) -> p t e", e=NE)
        eqm = zbf[:, 4 * GC + 192:4 * GC + 192 + G4]
        OW = LO + NE
        oh = zbf[:, 5 * GC:5 * GC + 2 * G4 * OW].rearrange("p (u t e) -> p u t e", u=2, t=G4)
        o = 5 * GC + 2 * G4 * OW
        ohb = zbf[:, o:o + G4 * NE].bitcast(BF16).rearrange("p (u t e) -> p u t e", u=2, t=G4)
        o += G4 * NE
        w1l = zbf[:, o:o + NE * FI // 2].bitcast(F16).rearrange("p (e f) -> p e f", e=NE)
        assert o + NE * FI // 2 <= NC_ * CH
        rank = zbf[:, 4 * GC + 256:4 * GC + 256 + NE]

        score = [ps(f"score{n}", [P, CH]) for n in range(2)]
        tra = [ps(f"tra{n}", [P, 512]) for n in range(2)]
        bld = ps("bld", [P, 8 * P], F16)
        yps = ps("yps", [P, 512])
        bldf = bld[:, :].bitcast(F32)
        yv = bldf[:, 0:TB * H * (D + 1)].rearrange("p (v d) -> p v d", d=D + 1)

        x_in = [sem("x_in0"), sem("x_in1")]
        wa_in = sem("wa_in")
        cn_in = sem("cn_in")
        const_ok = sem("const_ok")
        stat_ok = sem("stat_ok")
        root_ok = sem("root_ok")
        rstd_ok = sem("rstd_ok")
        xn_ok = sem("xn_ok")
        xnt_ps = sem("xnt_ps")
        xnt_ok = sem("xnt_ok")
        proj_ps = sem("proj_ps")
        proj_ok = sem("proj_ok")
        dve_a = sem("dve_a")
        act_a = sem("act_a")
        act_p = sem("act_p")
        len_step = sem("len_step")
        fac_ok = sem("fac_ok")
        tok_step = sem("tok_step")
        tok_ok = sem("tok_ok")
        v_ok = sem("v_ok")
        fill_ok = sem("fill_ok")
        opd_ok = sem("opd_ok")
        m_ps = sem("m_ps")
        w_ok = sem("w_ok")
        s1_ok = sem("s1_ok")
        s_ok = sem("s_ok")
        z_ok = sem("z_ok")
        zp_ok = sem("zp_ok")
        l_ok = sem("l_ok")
        x_ok = sem("x_ok")
        e_ps = sem("e_ps")
        sc_ok = sem("sc_ok")
        sub_ok = sem("sub_ok")
        t_ps = sem("t_ps")
        exp_ok = sem("exp_ok")
        pv_ok = sem("pv_ok")
        yev_ok = sem("yev_ok")
        ytr_ps = sem("ytr_ps")
        y_ok = sem("y_ok")
        yn_step = sem("yn_step")
        wc_in = sem("wc_in")
        xc_in = sem("xc_in")
        c_tr = sem("c_tr")
        c_ev = sem("c_ev")
        c_pj = sem("c_pj")
        ao_ok = sem("ao_ok")
        dve_c = sem("dve_c")
        h_tr = sem("h_tr")
        h_ev = sem("h_ev")
        lg_ps = sem("lg_ps")
        oh_ok = sem("oh_ok")
        oh_tr = sem("oh_tr")
        oht_ok = sem("oht_ok")
        mk_ps = sem("mk_ps")
        xe_ok = sem("xe_ok")
        xe_used = sem("xe_used")
        pre_ps = sem("pre_ps")
        gel_ok = sem("gel_ok")
        dn_ps = sem("dn_ps")
        yf_ok = sem("yf_ok")
        fin_ok = sem("fin_ok")
        out_ok = sem("out_ok")
        hs_ok = sem("hs_ok")
        hln_ok = sem("hln_ok")
        tm_ps = sem("tm_ps")
        stat_c = sem("stat_c")
        root_c = sem("root_c")
        rstd_c = sem("rstd_c")
        bn_ok = sem("bn_ok")
        dve_b = sem("dve_b")
        x1_ok = sem("x1_ok")
        oh_step = sem("oh_step")
        yr_ok = sem("yr_ok")
        w16_step = sem("w16_step")
        w16_ok = sem("w16_ok")
        h16_ok = sem("h16_ok")
        oh_zero = sem("oh_zero")
        ln_step = sem("ln_step")
        stat_g = sem("stat_g")
        root_g = sem("root_g")
        rstd_g = sem("rstd_g")
        nrm_g = sem("nrm_g")
        nrm_p = sem("nrm_p")
        stat_p = sem("stat_p")
        root_p = sem("root_p")
        rstd_p = sem("rstd_p")
        pre_step = sem("pre_step")

        block = ctx.enter_context(nc.Block())

        seen = sem("seen")
        CONSTS = 8
        EUC, HYP = 0, 1

        @block.sync
        def _(sp):
            xv = x.rearrange("(t p) n -> p t n", p=P)
            sp.dma_start(lk[:, :], log_k.broadcast_to([P, H])).then_inc(cn_in, 16)
            sp.dma_start(sc1[:, 0:1], thr.broadcast_to([P, 1])).then_inc(cn_in, 16)
            sp.dma_start(sc1[:, 1:2], qk_scale.broadcast_to([P, 1])).then_inc(cn_in, 16)
            sp.dma_start(xin[:, X_PARTS[0], :], xv[:, X_PARTS[0], :]).then_inc(x_in[0], 16)
            sp.dma_start(wall[:, :], w_all).then_inc(wa_in, 16)
            sp.dma_start(ball[:, :], b_all.broadcast_to([P, NP_])).then_inc(wa_in, 16)
            sp.dma_start(xin[:, X_PARTS[1], :], xv[:, X_PARTS[1], :]).then_inc(x_in[1], 16)
            sp.wait_ge(v_ok, 2 * NB)
            sp.dma_start(wouts, wout).then_inc(wc_in, 16)
            sp.dma_start(bouts, bout.broadcast_to([P, C])).then_inc(wc_in, 16)
            sp.dma_start(wrs, wr).then_inc(wc_in, 16)
            sp.dma_start(w1s, w1.rearrange("e p f -> p e f")).then_inc(wc_in, 16)
            sp.dma_start(wos, wo.rearrange("(k p) n -> p k n", p=P)).then_inc(wc_in, 16)
            sp.dma_start(b1s[0:NE, :], b1).then_inc(wc_in, 16)
            sp.dma_start(b1s[LO:LO + NE, :], b1).then_inc(wc_in, 16)
            sp.dma_start(bos, bo.broadcast_to([P, C])).then_inc(wc_in, 16)
            sp.dma_start(gams, gamma.broadcast_to([P, C])).then_inc(wc_in, 16)
            sp.dma_start(bets, beta.broadcast_to([P, C])).then_inc(wc_in, 16)
            sp.wait_ge(t_ps, (NB - 1) * HALVES)
            sp.dma_start(x1, xv).then_inc(xc_in, 16)
            ov = out.rearrange("(t p) n -> p t n", p=P)
            with sp.Fori(0, NG) as n:
                sp.wait_ge(fin_ok, n + 1)
                sp.dma_start(ov[:, ds(n * G4, G4), :], x1[:, ds(n * G4, G4), :]).then_inc(out_ok, 16)
            sp.wait_ge(out_ok, 16 * NG)

        def reuse(eng, signal, count):
            if not (isinstance(count, int) and count <= 0):
                eng.wait_ge(signal, count)

        def groups(eng, group):
            group(0, 0)
            group(1, 1)
            with eng.Fori(1, NG // 2) as i:
                group(i * 2, 0)
                group(i * 2 + 1, 1)

        def expert_groups(eng, group):
            group(0, 0)
            group(1, 1)
            with eng.Fori(1, NG // 2 - 1) as i:
                group(i * 2, 0)
                group(i * 2 + 1, 1)
            group(NG - 2, 0)
            group(NG - 1, 1, last=True)

        def items(prev, work):
            if prev and work:
                return [("floor", 0), ("floor", 1), ("mix", 0), ("floor", 2), ("floor", 3), ("mix", 1), ("floor", 4),
                        ("floor", 5), ("mix", 2), ("mix", 3), ("mix", 4), ("mix", 5)]
            return [("floor" if work else "mix", c) for c in range(NC_)]

        def steps(eng, step):
            step(0, 0, has_prev=False, has_two=False)
            step(1, 1, has_two=False)
            step(2, 0)
            with eng.Fori(0, (NB - 4) // 2) as i:
                step(i * 2 + 3, 1)
                step(i * 2 + 4, 0)
            step(NB - 1, 1, build=False)
            step(NB, 0, work=False, build=False)

        @block.gpsimd
        def _(pool):
            nc.gpsimd.memset(ident[:, :], 0.0).then_inc(const_ok, 1)
            nc.gpsimd.memset(identb[:, :], 0.0).then_inc(const_ok, 1)
            nc.gpsimd.memset(vone[:, :, :, :, :], 0.0).then_inc(const_ok, 1)
            pool.wait_ge(const_ok, 3)
            nc.gpsimd.affine_select(out=ident[:, :], in_=ident[:, :], compare_op=ALU.not_equal, fill=1.0, base=0,
                                    pattern=[[-1, P]], channel_multiplier=1).then_inc(const_ok, 1)
            nc.gpsimd.affine_select(out=maskb[:, :], in_=identb[:, :], compare_op=ALU.is_ge, fill=MASKED, base=0,
                                    pattern=[[-1, P]], channel_multiplier=1).then_inc(const_ok, 1)
            nc.gpsimd.memset(vone[:, :, :, :, D:D + 1], 1.0).then_inc(const_ok, 1)
            pool.wait_ge(const_ok, 6)
            nc.gpsimd.tensor_copy(ident16[:, :], ident[:, :]).then_inc(const_ok, 1)
            nc.gpsimd.tensor_copy(identb[:, :], ident[:, :]).then_inc(const_ok, 1)
            pool.wait_ge(fac_ok, 1)

            TS = 13

            def tokens(b):
                k0 = b * TS
                t0 = b * 4
                qv = proj[:, ds(b * TB, TB), QI:QI + C].rearrange("p t (h d) -> p t h d", d=D)
                kv = proj[:, ds(b * TB, TB), KI:KI + C].rearrange("p t (h d) -> p t h d", d=D)

                def per_head(a):
                    return a.unsqueeze(3).broadcast_to([P, TB, H, D])

                nc.gpsimd.tensor_tensor(vec[:, :, 0, :, :], qv, per_head(oma[:, ds(b * TB, TB), :]),
                                        ALU.mult).then_inc(tok_step, 1)
                nc.gpsimd.tensor_copy(vec[:, :, 2, :, :], kv).then_inc(tok_step, 1)
                nc.gpsimd.tensor_tensor(vec[:, :, 1, :, :], qv, per_head(gfac[:, ds(b * TB, TB), 0, :]),
                                        ALU.mult).then_inc(tok_step, 1)
                nc.gpsimd.tensor_tensor(vec[:, :, 3, :, :], kv, per_head(gfac[:, ds(b * TB, TB), 1, :]),
                                        ALU.mult).then_inc(tok_step, 1)
                pool.wait_ge(tok_step, k0 + 4)
                pool.sem_inc(seen)
                for qk in range(2):
                    nc.gpsimd.tensor_copy(vec[:, :, 1 + 2 * qk, :, 0], tmt[:, ds(b * TB, TB), qk, :])\
                        .then_inc(tok_step, 1)
                pool.wait_ge(tok_step, k0 + 6)
                pool.sem_inc(seen)
                slots = {0: (slice(0, 2), slice(2, 4)), 1: (slice(0, 4, 2), slice(1, 4, 2))}
                views = []
                for t in range(TB):
                    for side in range(2):
                        src = vec[:, t, 2 * side:2 * side + 2, :, :].rearrange("p a h d -> p (a h) d")
                        src = src.unsqueeze(2).broadcast_to([P, 2 * H, 2, D])
                        dst = stk[:, t, 2 * side:2 * side + 2, :, :, :].rearrange("p a h s d -> p (a h) s d")
                        views.append((dst[:, :, slots[side][0], :], dst[:, :, slots[side][1], :], src))
                if not (isinstance(t0, int) and t0 == 0):
                    pool.wait_ge(fill_ok, t0)
                    pool.sem_inc(seen)
                for high, low, src in views:
                    nc.gpsimd.tensor_scalar(high, src, 1.0, 0.0, ALU.mult, ALU.add).then_inc(tok_step, 1)
                pool.wait_ge(tok_step, k0 + 10)
                for high, low, src in views[:-1]:
                    nc.gpsimd.tensor_tensor(low, src, high, ALU.subtract).then_inc(tok_step, 1)
                high, low, src = views[-1]
                nc.gpsimd.tensor_tensor(low, src, high, ALU.subtract).then_inc(tok_ok, 1)
                pool.wait_ge(tok_step, k0 + 13)
                pool.wait_ge(tok_ok, b + 1)

            def factors(b, par, first):
                if not first:
                    pool.wait_ge(x_ok, (b - 1) * NC_)
                nc.gpsimd.tensor_copy(acb[:, par, :].rearrange("p (t h) -> p t h", h=H),
                                      acf[:, ds(b * TB, TB), :]).then_inc(v_ok, 1)

            def values(b, par, first):
                if not first:
                    pool.wait_ge(pv_ok, (b - 1) * HALVES)
                for t in range(TB):
                    last = nc.gpsimd.tensor_copy(
                        vone[:, par, t, :, 0:D],
                        proj[:, ds(b * TB + t, 1), VI:VI + C].rearrange("p a (h d) -> p (a h) d", d=D))
                last.then_inc(v_ok, 1)

            def subtract(b, par, c):
                tt = CHUNKS[c][0]
                pool.wait_ge(sc_ok, b * NC_ + c + 1)
                pool.sem_inc(seen)
                for h, col, width in heads_of(c):
                    v = za[:, par, c, col:col + width]
                    last = nc.gpsimd.tensor_scalar(v, v, -1.0, mxs[:, par, tt * H + h:tt * H + h + 1],
                                                   ALU.mult, ALU.add)
                last.then_inc(sub_ok, 1)

            def add_roots(s, par, c):
                pool.wait_ge(s_ok, s * NC_ + c + 1)
                nc.gpsimd.tensor_tensor(za[:, par, c, :], za[:, par, c, :], zb[:, c, :], ALU.add).then_inc(zp_ok, 1)

            def step(s, par, has_prev=True, has_two=True, work=True, build=True):
                if has_prev and not has_two:
                    pool.wait_ge(fac_ok, 2)
                if work:
                    factors(s, par, not has_prev)
                if build and has_prev:
                    tokens(s + 1)
                for c in range(NC_):
                    if has_prev:
                        subtract(s - 1, 1 - par, c)
                    if work and c in (2, 3):
                        add_roots(s, par, ZV + c - 2)
                    if work and c == 3:
                        values(s, par, not has_prev)

            tokens(0)
            tokens(1)
            steps(pool, step)

            def scaled_halves(w, high, low, k0):
                nc.gpsimd.tensor_scalar(w, w, WS, 0.0, ALU.mult, ALU.add).then_inc(w16_step, 1)
                pool.wait_ge(w16_step, k0 + 1)
                nc.gpsimd.tensor_scalar(high, w, 1.0, 0.0, ALU.mult, ALU.add).then_inc(w16_step, 1)
                pool.wait_ge(w16_step, k0 + 2)
                return nc.gpsimd.tensor_tensor(low, w, high, ALU.subtract)

            pool.wait_ge(wc_in, 16 * 10)
            scaled_halves(w1s, w1h, w1l, 0).then_inc(w16_ok, 1)
            nc.gpsimd.memset(b16, 0.0).then_inc(w16_step, 1)
            pool.wait_ge(w16_step, 3)
            b_low = b16[LO:LO + NE, :]
            nc.gpsimd.tensor_scalar(b16[0:NE, :], b1s[0:NE, :], WS, 0.0, ALU.mult, ALU.add).then_inc(w16_ok, 1)
            scaled_halves(b1s[LO:LO + NE, :], b_low, b_low, 3).then_inc(w16_ok, 1)
            pool.wait_ge(w16_ok, 3)

            def copy_input(n, u):
                pool.wait_ge(hs_ok, n + 1)
                nc.gpsimd.tensor_copy(hln[:, ds(n * G4, G4), :],
                                      hs[:, u, :].rearrange("p (t n) -> p t n", n=C)).then_inc(hln_ok, 1)

            groups(pool, copy_input)

        @block.tensor
        def _(pe):
            pe.wait_ge(const_ok, CONSTS)
            pe.wait_ge(wa_in, 32)
            def turn_x(n, u):
                pe.wait_ge(xn_ok, n + 1)
                reuse(pe, xnt_ok, n - 1)
                for k in range(G4):
                    last = nc.tensor.transpose(tra[u][:, k * P:(k + 1) * P], xn[:, u, k, :], ident[:, :])
                last.then_inc(xnt_ps, 1)

            def project_x(n, u):
                pe.wait_ge(xnt_ok, n + 1)
                for k in range(G4):
                    reuse(pe, proj_ok, (n - 1) * G4 + k + 1)
                    nc.tensor.matmul(score[k // 2][:, (k % 2) * 512:(k % 2) * 512 + NP_],
                                     xnt[:, u, k * P:(k + 1) * P], wall[:, :],
                                     start=True, stop=True).then_inc(proj_ps, 1)

            def group_a(n, u, last=False):
                if not last:
                    turn_x(n + 1, 1 - u)
                project_x(n, u)

            turn_x(0, 0)
            expert_groups(pe, group_a)

            def fill(b, kind, side, idx):
                pe.wait_ge(tok_ok, b + 1)
                pe.wait_ge(opd_ok, idx)
                for g in range(4):
                    for t in range(TB):
                        src = stk[:, t, 2 * side + kind, 4 * g:4 * g + 4, :, :].rearrange("p h s d -> p (h s d)")
                        last = nc.tensor.transpose(bld[:, (g * TB + t) * P:(g * TB + t + 1) * P], src, ident16[:, :])
                last.then_inc(fill_ok, 1)

            def products(bank2, par, kind, c, mask):
                tt, rows, quads = CHUNKS[c]
                width = P * (tt + 1)
                for bank, r in enumerate(rows):
                    for n, g in enumerate(quads):
                        col = bank * 512 + n * width
                        last = nc.tensor.matmul(
                            bank2[:, col:col + width],
                            opd[32 * r:32 * r + 32, par, kind, g, tt * P:(tt + 1) * P],
                            opd[32 * r:32 * r + 32, par, 2 + kind, g, 0:width],
                            start=not mask or n == 0, stop=not mask)
                if mask:
                    for bank in range(2):
                        seen_by = bank2[:, bank * 512:(bank + 1) * 512].rearrange("p (n w) -> p n w", w=width)
                        last = nc.tensor.matmul(seen_by[:, :, tt * P:(tt + 1) * P], identb[:, :],
                                                maskb[:, :].unsqueeze(1).broadcast_to([P, len(quads), P]),
                                                start=False, stop=True)
                return last

            def produce(s, par, work, prev, pos, free=None):
                users = items(prev, work)
                kind, c = users[pos]
                if pos >= 2:
                    free = (s, users[pos - 2])
                if free is not None:
                    at, (used, n) = free
                    if used == "floor":
                        pe.wait_ge(w_ok, at * NC_ + n + 1)
                    else:
                        pe.wait_ge(sc_ok, (at - 1) * NC_ + n + 1)
                if kind == "floor":
                    if c == 0:
                        pe.wait_ge(opd_ok, s * 4 + 2)
                    products(score[pos % 2], par, HYP, c, False).then_inc(m_ps, 1)
                else:
                    if c == 0:
                        pe.wait_ge(opd_ok, s * 4)
                    products(score[pos % 2], 1 - par, EUC, c, True).then_inc(e_ps, 1)

            def turn(b, par, c):
                pe.wait_ge(sub_ok, b * NC_ + c + 1)
                for j in range(2):
                    k = 2 * c + j
                    reuse(pe, exp_ok, b * HALVES + k - 1)
                    for n in range(4):
                        last = nc.tensor.transpose(tra[j][:, n * P:(n + 1) * P],
                                                   za[:, par, c, j * 512 + n * P:j * 512 + (n + 1) * P], ident[:, :])
                    last.then_inc(t_ps, 1)

            def attend(b, par, c):
                tt, rows, quads = CHUNKS[c]
                if c == 0:
                    reuse(pe, yev_ok, b)
                    pe.wait_ge(v_ok, 2 * b + 2)
                for j in range(2):
                    k = 2 * c + j
                    pe.wait_ge(exp_ok, b * HALVES + k + 1)
                    n = 0
                    for g in quads:
                        h = 4 * g + rows[j]
                        half, place = divmod(h, H // 2)
                        col = (half * TB + tt) * P
                        for t in range(tt + 1):
                            first = h * YW - place * (D + 1)
                            last = nc.tensor.matmul(
                                yps[0:YW, col:col + P], vflat[:, par, t, first:first + YW],
                                pt[:, k % 4, n * P:(n + 1) * P], start=(k == 0 and n == 0),
                                stop=(k == HALVES - 1 and g == quads[-1] and t == tt))
                            n += 1
                    last.then_inc(pv_ok, 1)

            def untangle(b, idx):
                pe.wait_ge(yev_ok, b + 1)
                pe.wait_ge(opd_ok, idx)
                for tt in range(TB):
                    for half in range(2):
                        last = nc.tensor.transpose(bldf[:, (tt * 2 + half) * YW:(tt * 2 + half + 1) * YW],
                                                   ysb[:, (half * TB + tt) * P:(half * TB + tt + 1) * P],
                                                   ident[0:YW, 0:YW])
                last.then_inc(ytr_ps, 1)

            def turn_y(n, bank):
                pe.wait_ge(y_ok, NB if n == NG - 1 else NB - 2 if n < NG - 2 and n == 0 else NB - 1)
                if bank is bldf:
                    pe.wait_ge(opd_ok, 4 * NB)
                    if n > 0:
                        pe.wait_ge(ao_ok, n)
                else:
                    pe.wait_ge(exp_ok, NB * HALVES)
                for k in range(G4):
                    last = nc.tensor.transpose(bank[:, k * P:(k + 1) * P], yatt[:, n * G4 + k, :], ident[:, :])
                last.then_inc(c_tr, 1)

            def project_y(n, bank):
                if n == 0:
                    pe.wait_ge(wc_in, 16 * 10)
                pe.wait_ge(c_ev, n + 1)
                for k in range(G4):
                    last = nc.tensor.matmul(bank[:, k * P:(k + 1) * P], ytr[:, n % 2, k * P:(k + 1) * P], wouts,
                                            start=True, stop=True)
                last.then_inc(c_pj, 1)

            def step(s, par, has_prev=True, has_two=True, work=True, build=True):
                b, bpar, a = s - 1, 1 - par, s - 2
                users = items(has_prev, work)

                def prod(pos):
                    produce(s, par, work, has_prev, pos)

                if has_prev and work:
                    prod(2)
                    prod(3)
                    if has_two:
                        reuse(pe, y_ok, a)
                    fill(s, EUC, 0, 4 * s + 2)
                    prod(4)
                    prod(5)
                    prod(6)
                    fill(s, EUC, 1, 4 * s + 3)
                    if has_two:
                        turn(a, par, 5)
                    prod(7)
                    if has_two:
                        attend(a, par, 3)
                    for pos in range(8, 10):
                        prod(pos)
                    if build:
                        fill(s + 1, HYP, 0, 4 * s + 4)
                    if has_two:
                        attend(a, par, 4)
                    prod(10)
                    turn(b, bpar, 0)
                    if has_two:
                        attend(a, par, 5)
                    prod(11)
                    if build:
                        fill(s + 1, HYP, 1, 4 * s + 5)
                    turn(b, bpar, 1)
                    if has_two:
                        untangle(a, 4 * s + (6 if build else 4))
                    attend(b, bpar, 0)
                elif work:
                    for pos in range(2, NC_):
                        prod(pos)
                else:
                    attend(a, par, 3)
                    prod(2)
                    attend(a, par, 4)
                    turn(a, par, 5)
                    prod(3)
                    attend(a, par, 5)
                    turn_y(0, bldf)
                    turn(b, bpar, 0)
                    project_y(0, bldf)
                    turn(b, bpar, 1)
                    pe.wait_ge(ao_ok, 1)
                    untangle(a, 4 * s)
                    attend(b, bpar, 0)
                    prod(4)
                    prod(5)
                    turn_y(1, bldf)
                    turn(b, bpar, 2)
                    project_y(1, bldf)
                    attend(b, bpar, 1)
                    turn_y(2, bldf)
                    turn(b, bpar, 3)
                    project_y(2, bldf)
                    attend(b, bpar, 2)
                    turn_y(3, bldf)
                    turn(b, bpar, 4)
                    project_y(3, bldf)
                    attend(b, bpar, 3)
                    turn_y(4, bldf)
                    attend(b, bpar, 4)
                    project_y(4, bldf)
                    turn(b, bpar, 5)
                    turn_y(5, bldf)
                    attend(b, bpar, 5)
                    project_y(5, bldf)
                    pe.wait_ge(ao_ok, 6)
                    untangle(b, 4 * s)
                    return
                if has_prev:
                    turn(b, bpar, 2)
                    attend(b, bpar, 1)
                if work:
                    produce(s + 1, 1 - par, build, True, 0, free=(s, users[-2]))
                if has_prev:
                    turn(b, bpar, 3)
                if work:
                    produce(s + 1, 1 - par, build, True, 1, free=(s, users[-1]))
                if has_prev:
                    attend(b, bpar, 2)
                    turn(b, bpar, 4)

            pe.wait_ge(proj_ok, NT)
            fill(0, HYP, 0, 0)
            fill(0, HYP, 1, 1)
            produce(0, 0, True, False, 0)
            produce(0, 0, True, False, 1)
            fill(0, EUC, 0, 2)
            fill(0, EUC, 1, 3)
            fill(1, HYP, 0, 4)
            fill(1, HYP, 1, 5)
            steps(pe, step)

            pe.wait_ge(sc_ok, NB * NC_)
            turn_y(NG - 2, tra[0])
            project_y(NG - 2, score[0])
            turn_y(NG - 1, tra[1])
            project_y(NG - 1, score[1])
            pre_bank = [score[0][:, 0:512], score[0][:, 512:1024], score[1][:, 0:512], score[1][:, 512:1024]]

            def route(n, u, part):
                if part == 0:
                    pe.wait_ge(hs_ok, n + 1)
                    reuse(pe, oht_ok, n)
                    for k in range(G4):
                        last = nc.tensor.transpose(bldf[:, k * P:(k + 1) * P], hs[:, u, k * P:(k + 1) * P],
                                                   ident[:, :])
                    last.then_inc(h_tr, 1)
                elif part == 1:
                    pe.wait_ge(h_ev, n + 1)
                    for k in range(G4):
                        last = nc.tensor.matmul(bldf[:, k * NE:(k + 1) * NE], hts[:, u, k * P:(k + 1) * P], wrs,
                                                start=True, stop=True)
                    last.then_inc(lg_ps, 1)
                else:
                    pe.wait_ge(oh_ok, n + 1)
                    pe.sem_inc(seen)
                    for k in range(G4):
                        last = nc.tensor.transpose(bldf[0:OW, k * P:(k + 1) * P], oh[:, u, k, :], ident[:, :])
                    last.then_inc(oh_tr, 1)

            def spread(n, u, e):
                if e < 2:
                    reuse(pe, xe_ok, n * NE)
                else:
                    pe.wait_ge(xe_ok, n * NE + e - 1)
                for k in range(G4):
                    last = nc.tensor.matmul(tra[e % 2][:, k * P:(k + 1) * P],
                                            ohb[:, u, k, e:e + 1].broadcast_to([P, P]), identb[:, :],
                                            start=True, stop=True)
                last.then_inc(mk_ps, 1)

            def biases(n, u):
                pe.wait_ge(oht_ok, n + 1)
                for f in range(FC):
                    reuse(pe, gel_ok, n * FC)
                    nc.tensor.matmul(pre_bank[f], b16[:, f * P:(f + 1) * P], oht[:, u, :], start=True, stop=False)

            def up(n, u, last_group):
                for e in range(NE):
                    pe.wait_ge(xe_ok, n * NE + e + 1)
                    for f in range(FC):
                        for w, half in ((w1h, 0), (w1h, 1), (w1l, 0)):
                            last = nc.tensor.matmul(pre_bank[f], w[:, e, f * P:(f + 1) * P], xte[:, e % 2, half, :],
                                                    start=False, stop=(e == NE - 1 and w is w1l))
                        if e == NE - 1:
                            last.then_inc(pre_ps, 1)
                    if e < NE - 1:
                        last.then_inc(xe_used, 1)
                    if e + 2 < NE:
                        spread(n, u, e + 2)
                    if not last_group and e in (1, 3, 6):
                        route(n + 1, 1 - u, (1, 3, 6).index(e))
                if not last_group:
                    spread(n + 1, 1 - u, 0)
                    spread(n + 1, 1 - u, 1)

            def down(n):
                pe.wait_ge(gel_ok, (n + 1) * FC)
                reuse(pe, yf_ok, n)
                for k in range(G4):
                    for f in range(FC):
                        last = nc.tensor.matmul(yps[:, k * P:(k + 1) * P], gel[:, f, k * P:(k + 1) * P], wos[:, f, :],
                                                start=(f == 0), stop=(f == FC - 1))
                last.then_inc(dn_ps, 1)

            def expert_group(n, u, last=False):
                up(n, u, last)
                down(n)
                if not last:
                    biases(n + 1, 1 - u)

            for part in range(3):
                route(0, 0, part)
            pe.wait_ge(w16_ok, 3)
            spread(0, 0, 0)
            spread(0, 0, 1)
            biases(0, 0)
            expert_groups(pe, expert_group)

        @block.scalar
        def _(act):
            act.wait_ge(dve_a, 1)
            nc.scalar.activation(curv[:, 1, :], curv[:, 0, :], ACT.Exp).then_inc(act_a, 1)
            nc.scalar.activation(sc1[:, 2:3], sc1[:, 1:2], ACT.Exp, scale=-1.0).then_inc(act_a, 1)
            act.wait_ge(act_a, 1)
            nc.scalar.activation(curv[:, 2, :], curv[:, 1, :], ACT.Ln, bias=1.0).then_inc(act_a, 1)

            def root_x(part):
                act.wait_ge(stat_ok, part + 1)
                t = X_PARTS[part]
                nc.scalar.activation(nmr[:, t], var[:, t], ACT.Sqrt).then_inc(root_ok, 1)

            def norm_x(n, u, part):
                act.wait_ge(rstd_ok, part + 1)
                reuse(act, xnt_ps, n - 1)
                for k in range(G4):
                    last = nc.scalar.activation(
                        xn[:, u, k, :], xin[:, ds(n * G4 + k, 1), :].rearrange("p a n -> p (a n)"), ACT.Identity,
                        scale=var[:, ds(n * G4 + k, 1)], bias=nmr[:, ds(n * G4 + k, 1)])
                last.then_inc(xn_ok, 1)

            def squares(n):
                act.wait_ge(proj_ok, (n + 1) * G4)
                nc.scalar.activation(
                    sq[:, ds(n * (G4 * 2 * H), G4 * 2 * H), :].rearrange("p (t v) d -> p t (v d)", t=G4),
                    proj[:, ds(n * G4, G4), 0:2 * C], ACT.Square).then_inc(act_p, 1)

            def evac(par, kind, side, idx):
                act.wait_ge(fill_ok, idx + 1)
                nc.scalar.activation(opd[:, par, 2 * side + kind, :, :].rearrange("p g n -> p (g n)"), bld[:, :],
                                     ACT.Copy).then_inc(opd_ok, 1)

            def lengths_root(part):
                v = PARTS[part][1]
                act.wait_ge(len_step, (3, NG * 3)[part])
                nc.scalar.activation(nrm[:, v], nrm[:, v], ACT.Sqrt).then_inc(root_ok, 1)

            def factors(part):
                t, v = PARTS[part]
                act.wait_ge(tm_ps, part + 1)
                nc.scalar.activation(acc[:, v], acc[:, v], ACT.Sqrt, bias=1.0).then_inc(root_ok, 1)
                nc.scalar.activation(sig[:, t, :], proj[:, t, II:II + H + 1], ACT.Exp, scale=-1.0).then_inc(root_ok, 1)

            def group_a(n, u, first=False, feeds=True):
                act.wait_ge(xnt_ps, n + 1)
                reuse(act, proj_ps, (n - 1) * G4)
                nc.scalar.activation(xnt[:, u, :], tra[u][:, :], ACT.Copy).then_inc(xnt_ok, 1)
                if first:
                    root_x(1)
                else:
                    squares(n - 1)
                if feeds:
                    norm_x(n + 2, u, 1)

            root_x(0)
            norm_x(0, 0, 0)
            norm_x(1, 1, 0)
            group_a(0, 0, first=True)
            group_a(1, 1)
            lengths_root(0)
            group_a(2, 0)
            factors(0)
            group_a(3, 1)
            with act.Fori(2, NG // 2 - 1) as i:
                group_a(i * 2, 0)
                group_a(i * 2 + 1, 1)
            group_a(NG - 2, 0, feeds=False)
            group_a(NG - 1, 1, feeds=False)
            squares(NG - 1)

            def log(s, par, c):
                if c < ZV:
                    act.wait_ge(z_ok, s * ZV + c + 1)
                else:
                    act.wait_ge(zp_ok, s * ZP + c - ZV + 1)
                nc.scalar.activation(za[:, par, c, :], za[:, par, c, :], ACT.Ln).then_inc(l_ok, 1)

            def exps(b, c):
                for j in range(2):
                    k = 2 * c + j
                    act.wait_ge(t_ps, b * HALVES + k + 1)
                    reuse(act, pv_ok, b * HALVES + k - 3)
                    nc.scalar.activation(pt[:, k % 4, :], tra[j][:, :], ACT.Exp, scale=-1.0).then_inc(exp_ok, 1)

            def feature_y(b):
                act.wait_ge(pv_ok, (b + 1) * HALVES)
                reuse(act, ytr_ps, b)
                nc.scalar.activation(ysb[:, :], yps[0:YW, :], ACT.Copy).then_inc(yev_ok, 1)

            def evac_y(n, bank):
                act.wait_ge(c_tr, n + 1)
                if n >= 2:
                    act.wait_ge(c_pj, n - 1)
                nc.scalar.activation(ytr[:, n % 2, :], bank[:, :], ACT.Copy).then_inc(c_ev, 1)

            def step(s, par, has_prev=True, has_two=True, work=True, build=True):
                if work:
                    for c in range(NC_):
                        if has_two and c in (0, 5):
                            act.wait_ge(t_ps, (s - 2) * HALVES + (10 if c == 0 else 12))
                        act.wait_ge(w_ok, s * NC_ + c + 1)
                        nc.scalar.activation(za[:, par, c, :], zb[:, c, :], ACT.Sqrt,
                                             scale=0.5 / (HS * HS)).then_inc(s1_ok, 1)
                        act.wait_ge(s1_ok, s * NC_ + c + 1)
                        nc.scalar.activation(zb[:, c, :], zb[:, c, :], ACT.Sqrt, bias=1.0,
                                             scale=0.5 / (HS * HS)).then_inc(s_ok, 1)
                        if has_prev and c in (1, 3):
                            evac(par, EUC, c // 2, 4 * s + 2 + c // 2)
                    if has_prev and build:
                        evac(1 - par, HYP, 0, 4 * s + 4)
                    nc.scalar.preload_act_table_set("natural_log_exp_and_others")
                if not work:
                    exps(s - 2, 5)
                    evac_y(0, bldf)
                    exps(s - 1, 0)
                    feature_y(s - 2)
                    exps(s - 1, 1)
                    for c in range(1, NC_ - 1):
                        evac_y(c, bldf)
                        exps(s - 1, c + 1)
                    evac_y(5, bldf)
                    feature_y(s - 1)
                    return
                if has_two:
                    exps(s - 2, 5)
                for c in range(NC_):
                    if work:
                        log(s, par, c)
                    if has_prev and build and c == 1:
                        evac(1 - par, HYP, 1, 4 * s + 5)
                    if has_prev and c < 5:
                        exps(s - 1, c)
                    if has_two and c == 0:
                        feature_y(s - 2)

            lengths_root(1)
            evac(0, HYP, 0, 0)
            evac(0, HYP, 1, 1)
            evac(0, EUC, 0, 2)
            evac(0, EUC, 1, 3)
            evac(1, HYP, 0, 4)
            evac(1, HYP, 1, 5)
            factors(1)
            steps(act, step)

            evac_y(NG - 2, tra[0])
            evac_y(NG - 1, tra[1])
            act.wait_ge(stat_c, 1)
            nc.scalar.activation(nmr[:, :], var[:, :], ACT.Sqrt).then_inc(root_c, 1)

            def norm_a(n):
                act.wait_ge(rstd_c, 1)
                for k in range(G4):
                    t = n * G4 + k
                    v = br[:, ds(t, 1), :].rearrange("p a n -> p (a n)")
                    last = nc.scalar.activation(v, v, ACT.Identity, scale=var[:, ds(t, 1)], bias=nmr[:, ds(t, 1)])
                last.then_inc(nrm_p, 1)

            def root_p_of(n):
                act.wait_ge(stat_p, n + 1)
                nc.scalar.activation(pnmr, pvar, ACT.Sqrt).then_inc(root_p, 1)

            def feed(n, u):
                act.wait_ge(rstd_p, n + 1)
                act.sem_inc(seen)
                for k in range(G4):
                    last = nc.scalar.activation(
                        hs[:, u, k * P:(k + 1) * P], x1[:, ds(n * G4 + k, 1), :].rearrange("p a n -> p (a n)"),
                        ACT.Identity, scale=pvar[:, k:k + 1], bias=pnmr[:, k:k + 1])
                last.then_inc(hs_ok, 1)

            def route(n, u):
                act.wait_ge(oh_tr, n + 1)
                nc.scalar.activation(oht[:, u, :], bldf[0:OW, :], ACT.Copy).then_inc(oht_ok, 1)

            def gelu(n):
                reuse(act, dn_ps, n)
                for f in range(FC):
                    act.wait_ge(pre_ps, n * FC + f + 1)
                    nc.scalar.activation(gel[:, f, :], [score[0][:, 0:512], score[0][:, 512:1024], score[1][:, 0:512],
                                                        score[1][:, 512:1024]][f], ACT.Gelu,
                                         scale=1.0 / WS).then_inc(gel_ok, 1)

            def polish(n):
                for half in range(2):
                    act.wait_ge(stat_g, n * 2 + half + 1)
                    nc.scalar.activation(gnmr, gvar, ACT.Sqrt).then_inc(root_g, 1)
                    act.wait_ge(rstd_g, n * 2 + half + 1)
                    act.sem_inc(seen)
                    for k in range(G4):
                        v = br[:, ds(n * G4 + k, 1), :].rearrange("p a n -> p (a n)")
                        last = nc.scalar.activation(v, v, ACT.Identity, scale=gvar[:, k:k + 1], bias=gnmr[:, k:k + 1])
                    last.then_inc(nrm_g, 1)

            def expert_group(n, u, last=False, feeds=True, first=False):
                if feeds:
                    norm_a(n + 2)
                if not first:
                    polish(n - 1)
                nc.scalar.preload_act_table_set("gelu_and_others")
                if not last:
                    route(n + 1, 1 - u)
                gelu(n)
                if feeds:
                    root_p_of(n + 2)
                    act.wait_ge(h_tr, n + 1)
                    act.wait_ge(hln_ok, n + 1)
                    feed(n + 2, u)

            norm_a(0)
            norm_a(1)
            root_p_of(0)
            feed(0, 0)
            route(0, 0)
            root_p_of(1)
            feed(1, 1)
            expert_group(0, 0, first=True)
            expert_group(1, 1)
            with act.Fori(1, NG // 2 - 1) as i:
                expert_group(i * 2, 0)
                expert_group(i * 2 + 1, 1)
            expert_group(NG - 2, 0, feeds=False)
            expert_group(NG - 1, 1, last=True, feeds=False)
            polish(NG - 1)

        @block.vector
        def _(dve):
            V = nc.vector
            count_a = [0]

            def link(ins):
                count_a[0] += 1
                ins.then_inc(dve_a, 1)
                dve.wait_ge(dve_a, count_a[0])

            count_c = [0]

            def link_c(ins):
                count_c[0] += 1
                ins.then_inc(dve_c, 1)
                dve.wait_ge(dve_c, count_c[0])

            def moments(eps, chain, stats=(st6, mu, var, tmp[:, 0, :], tmp[:, 1, :])):
                st, m, v, t0, t1 = stats
                chain(V.tensor_tensor(m[:, :], st[:, :, 1], st[:, :, 4], ALU.add))
                chain(V.tensor_tensor(t0, st[:, :, 1], st[:, :, 4], ALU.subtract))
                chain(V.tensor_tensor(t1, st[:, :, 2], st[:, :, 5], ALU.add))
                chain(V.tensor_scalar(m[:, :], m[:, :], 0.5, None, ALU.mult))
                chain(V.scalar_tensor_tensor(t0, t0, 0.25, t0, ALU.mult, ALU.mult))
                chain(V.scalar_tensor_tensor(t0, t1, 1.0 / C, t0, ALU.mult, ALU.add))
                return V.tensor_scalar(v[:, :], t0, eps, None, ALU.add)

            def inverses(chain, stats=(mu, var, nmr)):
                m, v, r = stats
                chain(V.reciprocal(v[:, :], r[:, :]))
                return V.scalar_tensor_tensor(r[:, :], m[:, :], -1.0, v[:, :], ALU.mult, ALU.mult)

            dve.wait_ge(cn_in, 48)
            link(V.scalar_tensor_tensor(curv[:, 0, :], lk[:, :], -1.0, lk[:, :], ALU.mult, ALU.min))
            dve.wait_ge(act_a, 3)
            link(V.tensor_scalar(curv[:, 3, :], curv[:, 1, :], 1.0, -1.0, ALU.add, ALU.add))
            link(V.tensor_scalar(curv[:, 3, :], curv[:, 3, :], 1e-30, None, ALU.add))
            link(V.reciprocal(curv[:, 3, :], curv[:, 3, :]))
            link(V.scalar_tensor_tensor(curv[:, 2, :], curv[:, 2, :], 1e-30, curv[:, 3, :], ALU.add, ALU.mult))
            link(V.tensor_tensor(curv[:, 2, :], curv[:, 2, :], curv[:, 1, :], ALU.mult))
            link(V.scalar_tensor_tensor(curv[:, 2, :], lk[:, :], 0.0, curv[:, 2, :], ALU.max, ALU.add))
            def link_b(ins):
                count_b[0] += 1
                ins.then_inc(dve_b, 1)
                dve.wait_ge(dve_b, count_b[0])

            count_b = [0]
            link_b(V.tensor_scalar(curv[:, 2, :], curv[:, 2, :], 1e-6, None, ALU.add))
            link_b(V.reciprocal(curv[:, 2, :], curv[:, 2, :]))
            link_b(V.tensor_scalar(curv[:, 2, :], curv[:, 2, :], -4.0, None, ALU.mult))
            link_b(V.tensor_scalar(sc1[:, 2:3], sc1[:, 2:3], 1.0, None, ALU.add))
            link_b(V.reciprocal(sc1[:, 2:3], sc1[:, 2:3]))
            link_b(V.tensor_scalar(sc1[:, 2:3], sc1[:, 2:3], 1.5, None, ALU.mult))

            def stats_x(part):
                t = X_PARTS[part]
                dve.wait_ge(x_in[part], 16)
                with dve.Fori(t.start // (2 * G4), t.stop // (2 * G4)) as n:
                    for k in range(2 * G4):
                        last = V.bn_stats(st6[:, ds(n * (2 * G4) + k, 1), :], xin[:, ds(n * (2 * G4) + k, 1), :])
                    last.then_inc(bn_ok, 2)
                dve.wait_ge(bn_ok, t.stop // G4)
                moments(LN_EPS, link_b, (st6[:, t], mu[:, t], var[:, t], tmp[:, 0, t], tmp[:, 1, t])).then_inc(stat_ok, 1)

            def inverses_x(part):
                t = X_PARTS[part]
                dve.wait_ge(root_ok, part + 1)
                inverses(link_b, (mu[:, t], var[:, t], nmr[:, t])).then_inc(rstd_ok, 1)

            stats_x(0)
            inverses_x(0)
            stats_x(1)
            inverses_x(1)
            dve.wait_ge(wa_in, 32)

            def bias_x(n, u):
                for k in range(G4):
                    dve.wait_ge(proj_ps, n * G4 + k + 1)
                    V.tensor_tensor(proj[:, ds(n * G4 + k, 1), :].rearrange("p a n -> p (a n)"),
                                    score[k // 2][:, (k % 2) * 512:(k % 2) * 512 + NP_], ball[:, :],
                                    ALU.add).then_inc(proj_ok, 1)

            def lengths(n):
                dve.wait_ge(act_p, n + 1)
                v = ds(n * (G4 * 2 * H), G4 * 2 * H)
                V.tensor_reduce(s7[:, v], sq[:, v, 1:D], AX, ALU.add).then_inc(len_step, 1)
                dve.wait_ge(len_step, n * 3 + 1)
                V.tensor_tensor(mk[:, v], s7[:, v], sq[:, v, 0], ALU.subtract).then_inc(len_step, 1)
                V.tensor_tensor(nrm[:, v], s7[:, v], sq[:, v, 0], ALU.add).then_inc(len_step, 1)

            def factors(part):
                t, v = PARTS[part]
                roots = 2 + 3 * part
                s7p, nrmp, mkp, accp, sigp = s7[:, v], nrm[:, v], mk[:, v], acc[:, v], sig[:, t, :]
                dve.wait_ge(root_ok, roots + 1)
                link_b(V.tensor_scalar(nrmp, nrmp, 1e-12, None, ALU.max))
                link_b(V.reciprocal(nrmp, nrmp))
                link_b(V.tensor_scalar(nrmp, nrmp, sc1[:, 2:3], None, ALU.mult))
                link_b(V.tensor_tensor(mkp, mkp, nrmp, ALU.mult))
                link_b(V.tensor_tensor(mkp, mkp, nrmp, ALU.mult))
                link_b(V.tensor_scalar(mkp, mkp, 1e-8, None, ALU.max))
                link_b(V.tensor_scalar(accp, mkp, 1.0 / factorial(15), None, ALU.mult))
                for k in range(6, 0, -1):
                    link_b(V.scalar_tensor_tensor(accp, accp, 1.0 / factorial(2 * k + 1), mkp, ALU.add, ALU.mult))
                link_b(V.scalar_tensor_tensor(nrmp, accp, 1.0, nrmp, ALU.add, ALU.mult))
                link_b(V.tensor_tensor(accp, nrmp, nrmp, ALU.mult))
                V.tensor_tensor(accp, accp, s7p, ALU.mult).then_inc(tm_ps, 1)
                nv = nrmp.rearrange("p (t q h) -> p t q h", q=2, h=H)
                for qk, sign in ((0, -HS), (1, HS)):
                    link_b(V.tensor_scalar(gfac[:, t, qk, :], nv[:, :, qk, :], sign, None, ALU.mult))
                dve.wait_ge(root_ok, roots + 3)
                link_b(V.tensor_scalar(tmt[:, t, :, :].rearrange("p t q h -> p (t q h)"), accp, HS, None, ALU.mult))
                link_b(V.tensor_scalar(sigp, sigp, 1.0, None, ALU.add))
                link_b(V.reciprocal(sigp, sigp))
                link_b(V.tensor_scalar(spk[:, t], sigp[:, :, 0], sc1[:, 0:1], None, ALU.is_gt))
                link_b(V.tensor_scalar(oma[:, t, :], sigp[:, :, 1:], -float(D) ** -0.5, float(D) ** -0.5,
                                       ALU.mult, ALU.add))
                V.tensor_tensor(acf[:, t, :], sigp[:, :, 1:],
                                curv[:, 2:3, :].broadcast_to([P, t.stop - t.start, H]), ALU.mult).then_inc(fac_ok, 1)
                dve.wait_ge(fac_ok, part + 1)

            bias_x(0, 0)
            bias_x(1, 1)
            lengths(0)
            factors(0)
            with dve.Fori(1, NG // 2) as i:
                bias_x(i * 2, 0)
                lengths(i * 2 - 1)
                bias_x(i * 2 + 1, 1)
                lengths(i * 2)
            lengths(NG - 1)
            dve.wait_ge(proj_ok, NT)
            factors(1)

            def floor(s, c, bank2, has_prev):
                dve.wait_ge(m_ps, s * NC_ + c + 1)
                if has_prev:
                    if c < ZV:
                        dve.wait_ge(z_ok, (s - 1) * ZV + c + 1)
                    else:
                        dve.wait_ge(zp_ok, (s - 1) * ZP + c - ZV + 1)
                V.tensor_scalar(zb[:, c, :], bank2[:, :], M_MIN * HS * HS, -HS * HS, ALU.max,
                                ALU.add).then_inc(w_ok, 1)

            def normalise(b):
                dve.wait_ge(ytr_ps, b + 1)
                V.reciprocal(rin[:, :], yv[:, :, D]).then_inc(yn_step, 1)
                dve.wait_ge(yn_step, b * 2 + 1)
                rv = rin[:, :].rearrange("p (t h) -> p t h", h=H)
                V.tensor_tensor(rv, rv, spk[:, ds(b * TB, TB)].unsqueeze(2).broadcast_to([P, TB, H]),
                                ALU.mult).then_inc(yn_step, 1)
                dve.wait_ge(yn_step, b * 2 + 2)
                V.tensor_tensor(yatt[:, ds(b * TB, TB), :].rearrange("p t (h d) -> p (t h) d", d=D), yv[:, :, 0:D],
                                rin[:, :].unsqueeze(2).broadcast_to([P, TB * H, D]), ALU.mult).then_inc(y_ok, 1)

            def mix(b, par, c, bank2):
                tt = CHUNKS[c][0]
                dve.wait_ge(l_ok, b * NC_ + c + 1)
                dve.wait_ge(v_ok, 2 * b + 1)
                for h, col, width in heads_of(c):
                    v = za[:, par, c, col:col + width]
                    last = V.scalar_tensor_tensor(v, v, acb[:, par, tt * H + h:tt * H + h + 1], v, ALU.mult, ALU.mult)
                last.then_inc(x_ok, 1)
                dve.wait_ge(x_ok, b * NC_ + c + 1)
                dve.wait_ge(e_ps, b * NC_ + c + 1)
                dve.sem_inc(seen)
                for h, col, width in heads_of(c):
                    v = za[:, par, c, col:col + width]
                    last = V.tensor_tensor_reduce(out=v, in0=bank2[:, col:col + width], in1=v, scale=1.0,
                                                  scalar=-3.0e38, op0=ALU.add, op1=ALU.max,
                                                  accum_out=mxs[:, par, tt * H + h:tt * H + h + 1])
                last.then_inc(sc_ok, 1)

            def add_roots(s, par, c):
                dve.wait_ge(s_ok, s * NC_ + c + 1)
                V.tensor_tensor(za[:, par, c, :], za[:, par, c, :], zb[:, c, :], ALU.add).then_inc(z_ok, 1)

            def project_y(n, bank):
                if n == 0:
                    dve.wait_ge(wc_in, 16 * 10)
                dve.wait_ge(c_pj, n + 1)
                g = slice(n * G4, (n + 1) * G4)
                V.tensor_tensor(br[:, g, :], bank[:, 0:512].rearrange("p (t n) -> p t n", n=C),
                                bouts.unsqueeze(1).broadcast_to([P, G4, C]), ALU.add).then_inc(ao_ok, 1)
                dve.wait_ge(ao_ok, n + 1)
                for t in range(n * G4, (n + 1) * G4):
                    last = V.bn_stats(st6[:, t:t + 1, :], br[:, t:t + 1, :])
                last.then_inc(bn_ok, 1)

            def step(s, par, has_prev=True, has_two=True, work=True, build=True):
                sums = {8: (0,), 9: (1,), 10: (2,), 11: (3,)} if has_prev and work else {}
                for pos, (kind, c) in enumerate(items(has_prev, work)):
                    for n in sums.get(pos, ()):
                        add_roots(s, par, n)
                    if kind == "floor":
                        floor(s, c, score[pos % 2], has_prev)
                    else:
                        mix(s - 1, 1 - par, c, score[pos % 2])
                    if has_two and (pos == 11 or (not work and pos == 3)):
                        normalise(s - 2)
                    if not work and pos in (2, 4, 5):
                        project_y((2, 4, 5).index(pos), bldf)
                if not work:
                    for n in range(3, NC_):
                        project_y(n, bldf)
                    normalise(s - 1)
                if work and not sums:
                    for n in range(ZV):
                        add_roots(s, par, n)

            steps(dve, step)
            V.memset(oh, 0.0).then_inc(oh_zero, 1)
            dve.wait_ge(oh_zero, 1)

            project_y(NG - 2, score[0])
            project_y(NG - 1, score[1])
            dve.wait_ge(bn_ok, 2 * NG)
            moments(LN_EPS, link_c).then_inc(stat_c, 1)
            for e in range(NE):
                last = V.memset(rank[:, e:e + 1], float(NE - e))
            link_c(last)
            dve.wait_ge(root_c, 1)
            inverses(link_c).then_inc(rstd_c, 1)
            dve.wait_ge(xc_in, 16)

            PS = 8

            def counted(signal, base):
                count = [base]

                def chain(ins):
                    count[0] = count[0] + 1
                    ins.then_inc(signal, 1)
                    dve.wait_ge(signal, count[0])
                return chain

            def prepare(n, part):
                xg = x1[:, ds(n * G4, G4), :]
                if part == 0:
                    dve.wait_ge(nrm_p, n + 1)
                    V.tensor_tensor(xg, xg, br[:, ds(n * G4, G4), :], ALU.add).then_inc(x1_ok, 1)
                elif part == 1:
                    chain = counted(pre_step, n * PS)
                    reuse(dve, hs_ok, n)
                    dve.wait_ge(x1_ok, n + 1)
                    dve.sem_inc(seen)
                    for k in range(G4):
                        last = V.bn_stats(pst[:, k:k + 1, :], x1[:, ds(n * G4 + k, 1), :])
                    chain(last)
                    moments(LN_EPS, chain, (pst, pmu, pvar, pt0, pt1)).then_inc(stat_p, 1)
                else:
                    dve.wait_ge(root_p, n + 1)
                    inverses(counted(pre_step, n * PS + 7), (pmu, pvar, pnmr)).then_inc(rstd_p, 1)

            for part in range(3):
                prepare(0, part)
            prepare(1, 0)

            OS = 6

            def route(n, u, part):
                if part == 0:
                    dve.wait_ge(h_tr, n + 1)
                    V.tensor_copy(hts[:, u, :], bldf[:, :]).then_inc(h_ev, 1)
                    dve.wait_ge(h_ev, n + 1)
                    V.tensor_copy(ht16[:, u, 0, :], hts[:, u, :]).then_inc(h16_ok, 1)
                    dve.wait_ge(h16_ok, n * 2 + 1)
                    V.tensor_tensor(ht16[:, u, 1, :], hts[:, u, :], ht16[:, u, 0, :], ALU.subtract).then_inc(h16_ok, 1)
                    return
                dve.wait_ge(lg_ps, n + 1)
                V.tensor_copy(lg, bldf[:, 0:G4 * NE].rearrange("p (t e) -> p t e", e=NE)).then_inc(oh_step, 1)
                dve.wait_ge(oh_step, n * OS + 1)
                V.tensor_reduce(lgm, lg, AX, ALU.max).then_inc(oh_step, 1)
                dve.wait_ge(oh_step, n * OS + 2)
                V.tensor_tensor(lg, lg, lgm.unsqueeze(2).broadcast_to([P, G4, NE]), ALU.is_equal).then_inc(oh_step, 1)
                dve.wait_ge(oh_step, n * OS + 3)
                V.tensor_tensor(eqr, lg, rank.unsqueeze(1).broadcast_to([P, G4, NE]), ALU.mult).then_inc(oh_step, 1)
                dve.wait_ge(oh_step, n * OS + 4)
                V.tensor_reduce(eqm, eqr, AX, ALU.max).then_inc(oh_step, 1)
                dve.wait_ge(oh_step, n * OS + 5)
                V.tensor_tensor(ohb[:, u, :, :], eqr, eqm.unsqueeze(2).broadcast_to([P, G4, NE]),
                                ALU.is_equal).then_inc(oh_step, 1)
                for first in (0, LO):
                    last = V.tensor_tensor(oh[:, u, :, first:first + NE], eqr,
                                           eqm.unsqueeze(2).broadcast_to([P, G4, NE]), ALU.is_equal)
                last.then_inc(oh_ok, 1)

            def select(n, u, experts):
                dve.wait_ge(h16_ok, (n + 1) * 2)
                for e in experts:
                    dve.wait_ge(mk_ps, n * NE + e + 1)
                    if e < 2:
                        reuse(dve, pre_ps, n * FC)
                    else:
                        dve.wait_ge(xe_used, n * (NE - 1) + e - 1)
                    V.tensor_tensor(xte[:, e % 2, :, :], ht16[:, u, :, :],
                                    tra[e % 2][:, :].unsqueeze(1).broadcast_to([P, 2, GT]),
                                    ALU.mult).then_inc(xe_ok, 1)

            def finish(n):
                dve.wait_ge(dn_ps, n + 1)
                g = br[:, ds(n * G4, G4), :]
                V.tensor_tensor(g, yps[:, :].rearrange("p (t n) -> p t n", n=C),
                                bos.unsqueeze(1).broadcast_to([P, G4, C]), ALU.add).then_inc(yf_ok, 1)
                dve.wait_ge(yf_ok, n + 1)
                dve.wait_ge(hln_ok, n + 1)
                V.tensor_tensor(g, g, hln[:, ds(n * G4, G4), :], ALU.add).then_inc(yr_ok, 1)
                dve.wait_ge(yr_ok, n + 1)
                stats(n)

            def stats(n):
                dve.sem_inc(seen)
                for k in range(G4):
                    last = V.bn_stats(gst[:, k:k + 1, :], br[:, ds(n * G4 + k, 1), :])
                last.then_inc(bn_ok, 1)

            LS = 16

            gstats = (gst, gmu, gvar, gt0, gt1)
            ginv = (gmu, gvar, gnmr)

            def polish(n, part):
                g = br[:, ds(n * G4, G4), :]
                base = n * LS
                if part == 0:
                    dve.wait_ge(bn_ok, 2 * NG + n * 2 + 1)
                    moments(FFN_EPS, counted(ln_step, base), gstats).then_inc(stat_g, 1)
                elif part == 1:
                    dve.wait_ge(root_g, n * 2 + 1)
                    inverses(counted(ln_step, base + 6), ginv).then_inc(rstd_g, 1)
                elif part == 2:
                    chain = counted(ln_step, base + 7)
                    dve.wait_ge(nrm_g, n * 2 + 1)
                    chain(V.tensor_tensor(g, g, gams.unsqueeze(1).broadcast_to([P, G4, C]), ALU.mult))
                    chain(V.tensor_tensor(g, g, bets.unsqueeze(1).broadcast_to([P, G4, C]), ALU.add))
                    stats(n)
                elif part == 3:
                    dve.wait_ge(bn_ok, 2 * NG + n * 2 + 2)
                    moments(LN_EPS, counted(ln_step, base + 9), gstats).then_inc(stat_g, 1)
                elif part == 4:
                    dve.wait_ge(root_g, n * 2 + 2)
                    inverses(counted(ln_step, base + 15), ginv).then_inc(rstd_g, 1)
                else:
                    dve.wait_ge(nrm_g, n * 2 + 2)
                    V.tensor_tensor(x1[:, ds(n * G4, G4), :], x1[:, ds(n * G4, G4), :], g, ALU.add).then_inc(fin_ok, 1)

            def expert_group(n, u, last=False, first=False, feeds=True):
                for e in range(2, NE):
                    select(n, u, (e,))
                    if not first and e < 7:
                        polish(n - 1, e - 2)
                    if feeds and e == 2:
                        prepare(n + 2, 0)
                    if not last and e in (3, 6):
                        route(n + 1, 1 - u, e // 6)
                    if feeds and e == 7:
                        prepare(n + 2, 1)
                if not last:
                    select(n + 1, 1 - u, (0, 1))
                if not first:
                    polish(n - 1, 5)
                if feeds:
                    prepare(n + 2, 2)
                finish(n)

            route(0, 0, 0)
            route(0, 0, 1)
            select(0, 0, (0, 1))
            prepare(1, 1)
            prepare(1, 2)
            expert_group(0, 0, first=True)
            expert_group(1, 1)
            with dve.Fori(1, NG // 2 - 1) as i:
                expert_group(i * 2, 0)
                expert_group(i * 2 + 1, 1)
            expert_group(NG - 2, 0, feeds=False)
            expert_group(NG - 1, 1, last=True, feeds=False)
            for part in range(6):
                polish(NG - 1, part)


def kernel(**inputs):
    import numpy as np
    import concourse.bacc as bacc
    from concourse import mybir as _mybir
    from concourse.bass_utils import run_bass_kernel_spmd

    a = {k.replace("L0_", ""): np.asarray(v) for k, v in inputs.items()}
    shape = a["attn_x"].shape
    c = shape[-1]
    data = {
        "x": a["attn_x"].reshape(-1, c),
        "w_all": np.concatenate([a["attn_Wqkv"], a["attn_Wimp"], a["attn_Walpha"]], 0).T,
        "b_all": np.concatenate([a["attn_bqkv"], a["attn_bimp"], a["attn_balpha"]], 0).reshape(1, -1),
        "wout": a["attn_Wout"].T,
        "bout": a["attn_bout"].reshape(1, -1),
        "thr": a["attn_spike_threshold"].reshape(1, 1),
        "log_k": a["attn_log_k"].reshape(1, -1),
        "qk_scale": a["attn_qk_scale"].reshape(1, 1),
        "wr": a["ffn_Wr"].T,
        "w1": a["ffn_W1"],
        "b1": a["ffn_b1"],
        "wo": a["ffn_Wo"],
        "bo": a["ffn_bo"].reshape(1, -1),
        "gamma": a["ffn_gamma"].reshape(1, -1),
        "beta": a["ffn_beta"].reshape(1, -1),
    }
    nc = bacc.Bacc("TRN2", target_bir_lowering=False, num_devices=1)
    arrays, args = {}, []
    for name, v in data.items():
        v = np.ascontiguousarray(v)
        arrays["in_" + name] = v
        args.append(nc.dram_tensor("in_" + name, v.shape, _mybir.dt.from_np(v.dtype), kind="ExternalInput").ap())
    out = nc.dram_tensor("out_x", data["x"].shape, _mybir.dt.float32, kind="ExternalOutput").ap()
    sandwich(nc, *args, out)
    r = run_bass_kernel_spmd(nc, [arrays], core_ids=[0])
    return r.results[0]["out_x"].reshape(shape)
```
